# Optimizing a Trainium2 kernel written in Bass

```python
import numpy as np
import jax
import jax.numpy as jnp

def _softmax(x, axis=-1):
    return jax.nn.softmax(x, axis=axis)

def _gelu(x):
    return jax.nn.gelu(x, approximate=True)

def _silu(x):
    return jax.nn.silu(x)

def _sigmoid(x):
    return jax.nn.sigmoid(x)

def _layernorm(x, axis=-1, eps=1e-05):
    m = jnp.mean(x, axis=axis, keepdims=True)
    v = jnp.var(x, axis=axis, keepdims=True)
    return (x - m) / jnp.sqrt(v + eps)

def _scatter_add(tgt, idx, src, axis=0):
    return tgt.at[idx].add(src)

def _segment_sum(src, seg, n):
    return jax.ops.segment_sum(src, seg, n)
kernel_name = 'mk_sandwich_d2_jaxref_r8_5d4d50'

def setup_inputs(seed: int=0):
    np.random.seed(seed)
    _w = jnp.asarray

    def _L0_attn_setup():
        import jax, jax.numpy as jnp
        import numpy as np
        D_MODEL = 128
        D_STATE = 64
        EXPAND = 2
        N_HEADS = 32
        NGROUPS = 1
        CHUNK = 128
        R = 2
        D_INNER = EXPAND * D_MODEL
        HEAD_DIM = D_INNER // N_HEADS
        BC = NGROUPS * D_STATE
        D_PROJ = D_INNER + D_INNER * R + BC * R + BC + 2 * N_HEADS + D_STATE // 2
        SCALE = (D_STATE * R) ** (-0.5)
        EPS = 1e-06
        NEG = -1e+30

        def _rms(x):
            return x * jax.lax.rsqrt(jnp.mean(x * x, axis=-1, keepdims=True) + EPS)

        def _rope(x, cos, sin):
            h = x.shape[-1] // 2
            x1, x2 = (x[..., :h], x[..., h:])
            return jnp.concatenate([x1 * cos - x2 * sin, x1 * sin + x2 * cos], axis=-1)
        key = jax.random.key(seed)
        ks = jax.random.split(key, 7)
        B, T = (2, 256)
        return {'x': jax.random.normal(ks[0], (B, T, D_MODEL), jnp.float32), 'W_in': jax.random.normal(ks[1], (D_MODEL, D_PROJ), jnp.float32) * 0.02, 'A_log': jax.random.normal(ks[2], (N_HEADS,), jnp.float32) * 0.5, 'dt_bias': jax.random.normal(ks[3], (N_HEADS,), jnp.float32) * 0.5, 'B_norm_bias': 1.0 + 0.1 * jax.random.normal(ks[4], (NGROUPS, D_STATE), jnp.float32), 'C_norm_bias': 1.0 + 0.1 * jax.random.normal(ks[5], (NGROUPS, D_STATE), jnp.float32), 'W_out': jax.random.normal(ks[6], (D_INNER, D_MODEL), jnp.float32) * 0.02}
    _L0_attn_in = _L0_attn_setup()

    def _L0_ffn_setup():
        import jax, jax.numpy as jnp
        import numpy as np
        D_IN, D_HID = (128, 512)

        def _ternary(key, shape):
            return jax.random.randint(key, shape, -1, 2).astype(jnp.float32)

        def _tlin(x, w, s):
            return jnp.einsum('bsi,oi->bso', x, w) * s
        key = jax.random.key(seed)
        ks = jax.random.split(key, 12)
        inv = lambda fan: 1.0 / np.sqrt(fan).astype(np.float32)
        return {'x': jax.random.normal(ks[0], (4, 256, D_IN), dtype=jnp.float32), 'w1_w': _ternary(ks[1], (D_HID, D_IN)), 'w1_s': jax.random.uniform(ks[2], (D_HID,), dtype=jnp.float32) * inv(D_IN), 'w2_w': _ternary(ks[3], (D_HID, D_IN)), 'w2_s': jax.random.uniform(ks[4], (D_HID,), dtype=jnp.float32) * inv(D_IN), 'h1_w': _ternary(ks[5], (D_HID, D_HID)), 'h1_s': jax.random.uniform(ks[6], (D_HID,), dtype=jnp.float32) * inv(D_HID), 'h2_w': _ternary(ks[7], (D_HID, D_HID)), 'h2_s': jax.random.uniform(ks[8], (D_HID,), dtype=jnp.float32) * inv(D_HID), 'w3_w': _ternary(ks[9], (D_IN, D_HID)), 'w3_s': jax.random.uniform(ks[10], (D_IN,), dtype=jnp.float32) * inv(D_HID)}
    _L0_ffn_in = _L0_ffn_setup()

    def _L1_attn_setup():
        import jax, jax.numpy as jnp
        import numpy as np
        import math
        D_MODEL = 128
        D_QUERY = 64
        key = jax.random.key(seed)
        k1, k2, k3, k4 = jax.random.split(key, 4)
        X = jax.random.normal(k1, (4, 512, D_MODEL), dtype=jnp.float32)
        Wq = jax.random.normal(k2, (D_MODEL, D_QUERY), dtype=jnp.float32) * (1.0 / math.sqrt(D_MODEL))
        Wk = jax.random.normal(k3, (D_MODEL, D_QUERY), dtype=jnp.float32) * (1.0 / math.sqrt(D_MODEL))
        Wv = jax.random.normal(k4, (D_MODEL, D_MODEL), dtype=jnp.float32) * (1.0 / math.sqrt(D_MODEL))
        return {'X': X, 'Wq': Wq, 'Wk': Wk, 'Wv': Wv}
    _L1_attn_in = _L1_attn_setup()

    def _L1_ffn_setup():
        import jax, jax.numpy as jnp
        import numpy as np
        E, D, F = (8, 128, 512)
        LN_EPS = 1e-05
        key = jax.random.key(seed)
        k = jax.random.split(key, 8)
        x = jax.random.normal(k[0], (4, 256, D), jnp.float32)
        centroids = jax.random.normal(k[1], (E, D), jnp.float32) * 0.1
        ln_g = jnp.ones((E, D), jnp.float32)
        ln_b = jnp.zeros((E, D), jnp.float32)
        w1 = jax.random.normal(k[2], (E, F, D), jnp.float32) * (1.0 / np.sqrt(D))
        b1 = jnp.zeros((E, F), jnp.float32)
        w2 = jax.random.normal(k[3], (E, D, F), jnp.float32) * (1.0 / np.sqrt(F))
        b2 = jnp.zeros((E, D), jnp.float32)
        return {'input_features': x, 'centroids': centroids, 'ln_g': ln_g, 'ln_b': ln_b, 'w1': w1, 'b1': b1, 'w2': w2, 'b2': b2}
    _L1_ffn_in = _L1_ffn_setup()
    _d = {'L0_attn_x': _L0_attn_in['x'], 'L0_attn_W_in': _L0_attn_in['W_in'], 'L0_attn_A_log': _L0_attn_in['A_log'], 'L0_attn_dt_bias': _L0_attn_in['dt_bias'], 'L0_attn_B_norm_bias': _L0_attn_in['B_norm_bias'], 'L0_attn_C_norm_bias': _L0_attn_in['C_norm_bias'], 'L0_attn_W_out': _L0_attn_in['W_out'], 'L0_ffn_w1_w': _L0_ffn_in['w1_w'], 'L0_ffn_w1_s': _L0_ffn_in['w1_s'], 'L0_ffn_w2_w': _L0_ffn_in['w2_w'], 'L0_ffn_w2_s': _L0_ffn_in['w2_s'], 'L0_ffn_h1_w': _L0_ffn_in['h1_w'], 'L0_ffn_h1_s': _L0_ffn_in['h1_s'], 'L0_ffn_h2_w': _L0_ffn_in['h2_w'], 'L0_ffn_h2_s': _L0_ffn_in['h2_s'], 'L0_ffn_w3_w': _L0_ffn_in['w3_w'], 'L0_ffn_w3_s': _L0_ffn_in['w3_s'], 'L1_attn_Wq': _L1_attn_in['Wq'], 'L1_attn_Wk': _L1_attn_in['Wk'], 'L1_attn_Wv': _L1_attn_in['Wv'], 'L1_ffn_centroids': _L1_ffn_in['centroids'], 'L1_ffn_ln_g': _L1_ffn_in['ln_g'], 'L1_ffn_ln_b': _L1_ffn_in['ln_b'], 'L1_ffn_w1': _L1_ffn_in['w1'], 'L1_ffn_b1': _L1_ffn_in['b1'], 'L1_ffn_w2': _L1_ffn_in['w2'], 'L1_ffn_b2': _L1_ffn_in['b2']}
    _x0 = _d['L0_attn_x']
    _d['L0_attn_x'] = jax.random.normal(jax.random.fold_in(jax.random.key(seed), 1), (1, 2048, 128), dtype=_x0.dtype)
    del _x0
    return _d

def reference(L0_attn_x, L0_attn_W_in, L0_attn_A_log, L0_attn_dt_bias, L0_attn_B_norm_bias, L0_attn_C_norm_bias, L0_attn_W_out, L0_ffn_w1_w, L0_ffn_w1_s, L0_ffn_w2_w, L0_ffn_w2_s, L0_ffn_h1_w, L0_ffn_h1_s, L0_ffn_h2_w, L0_ffn_h2_s, L0_ffn_w3_w, L0_ffn_w3_s, L1_attn_Wq, L1_attn_Wk, L1_attn_Wv, L1_ffn_centroids, L1_ffn_ln_g, L1_ffn_ln_b, L1_ffn_w1, L1_ffn_b1, L1_ffn_w2, L1_ffn_b2):

    def _L0_attn_ref(x, W_in, A_log, dt_bias, B_norm_bias, C_norm_bias, W_out):
        import jax, jax.numpy as jnp
        import numpy as np
        D_MODEL = 128
        D_STATE = 64
        EXPAND = 2
        N_HEADS = 32
        NGROUPS = 1
        CHUNK = 128
        R = 2
        D_INNER = EXPAND * D_MODEL
        HEAD_DIM = D_INNER // N_HEADS
        BC = NGROUPS * D_STATE
        D_PROJ = D_INNER + D_INNER * R + BC * R + BC + 2 * N_HEADS + D_STATE // 2
        SCALE = (D_STATE * R) ** (-0.5)
        EPS = 1e-06
        NEG = -1e+30

        def _rms(x):
            return x * jax.lax.rsqrt(jnp.mean(x * x, axis=-1, keepdims=True) + EPS)

        def _rope(x, cos, sin):
            h = x.shape[-1] // 2
            x1, x2 = (x[..., :h], x[..., h:])
            return jnp.concatenate([x1 * cos - x2 * sin, x1 * sin + x2 * cos], axis=-1)
        B, T, _ = x.shape
        L = CHUNK
        NC = T // L
        G, H, N, P = (NGROUPS, N_HEADS, D_STATE, HEAD_DIM)
        E = H // G
        proj = x @ W_in
        o = 0
        z = proj[..., :D_INNER]
        o = D_INNER
        x_raw = proj[..., o:o + D_INNER * R]
        o += D_INNER * R
        Bm = proj[..., o:o + BC * R]
        o += BC * R
        Cm = proj[..., o:o + BC]
        o += BC
        dt_raw = proj[..., o:o + H]
        o += H
        lam_raw = proj[..., o:o + H]
        o += H
        theta = proj[..., o:]
        x_raw = jax.nn.silu(x_raw)
        Bm = _rms(Bm.reshape(B, T, G, R, N)) * B_norm_bias[:, None, :]
        Cm = _rms(Cm.reshape(B, T, G, N)) * C_norm_bias
        A = -jnp.exp(A_log)
        dt = jnp.clip(jax.nn.softplus(dt_raw + dt_bias), 0.0001, 0.5)
        ang = -jnp.cumsum(jnp.mean(dt, axis=-1, keepdims=True) * theta, axis=1)
        cos, sin = (jnp.cos(ang), jnp.sin(ang))
        Cr = _rope(Cm, cos[:, :, None, :], sin[:, :, None, :])
        Br = _rope(Bm, cos[:, :, None, None, :], sin[:, :, None, None, :])
        xh = x_raw.reshape(B, T, H, R, P)
        log_dA = dt * A
        alpha = jnp.exp(log_dA)
        lam = jax.nn.sigmoid(lam_raw)
        xg = (lam * dt)[..., None, None] * xh
        x_prev = jnp.pad(xh, ((0, 0), (1, 0), (0, 0), (0, 0), (0, 0)))[:, :T]
        xb = ((1.0 - lam) * dt * alpha)[..., None, None] * x_prev
        Bb = jnp.pad(Br, ((0, 0), (1, 0), (0, 0), (0, 0), (0, 0)))[:, :T]

        def ch(a):
            return a.reshape(B, NC, L, *a.shape[2:])
        cum = jnp.cumsum(ch(log_dA), axis=2)
        mask = jnp.tril(jnp.ones((L, L), bool))
        diff = cum[:, :, :, None, :] - cum[:, :, None, :, :]
        dmat = jnp.exp(jnp.where(mask[None, None, :, :, None], diff, NEG))
        Cc = ch(Cr)
        Bgc, Bbc = (ch(Br), ch(Bb))
        xgc = ch(xg).reshape(B, NC, L, G, E, R, P)
        xbc = ch(xb).reshape(B, NC, L, G, E, R, P)
        sg = jnp.einsum('bclgn,bcmgrn->bclmgr', Cc, Bgc) * SCALE
        sb = jnp.einsum('bclgn,bcmgrn->bclmgr', Cc, Bbc) * SCALE
        dg = dmat.reshape(B, NC, L, L, G, E)
        y_intra = jnp.einsum('bclmgr,bclmge,bcmgerp->bclgep', sg, dg, xgc) + jnp.einsum('bclmgr,bclmge,bcmgerp->bclgep', sb, dg, xbc)
        dec_end = jnp.exp(cum[:, :, -1:, :] - cum).reshape(B, NC, L, G, E)
        st = (jnp.einsum('bclge,bclgrn,bclgerp->bcgenp', dec_end, Bgc, xgc) + jnp.einsum('bclge,bclgrn,bclgerp->bcgenp', dec_end, Bbc, xbc)).reshape(B, NC, H, N, P)
        cdec = jnp.exp(cum[:, :, -1, :])

        def step(S, inp):
            cd, s = inp
            return (cd[..., None, None] * S + s, S)
        _, Sprev = jax.lax.scan(step, jnp.zeros((B, H, N, P), x.dtype), (jnp.moveaxis(cdec, 1, 0), jnp.moveaxis(st, 1, 0)))
        Sprev = jnp.moveaxis(Sprev, 0, 1).reshape(B, NC, G, E, N, P)
        dec_in = jnp.exp(cum).reshape(B, NC, L, G, E)
        y_inter = SCALE * jnp.einsum('bclgn,bclge,bcgenp->bclgep', Cc, dec_in, Sprev)
        y = (y_intra + y_inter).reshape(B, T, D_INNER)
        y = _rms(y * jax.nn.silu(z))
        return y @ W_out

    def _L0_ffn_ref(x, w1_w, w1_s, w2_w, w2_s, h1_w, h1_s, h2_w, h2_s, w3_w, w3_s):
        import jax, jax.numpy as jnp
        import numpy as np
        D_IN, D_HID = (128, 512)

        def _ternary(key, shape):
            return jax.random.randint(key, shape, -1, 2).astype(jnp.float32)

        def _tlin(x, w, s):
            return jnp.einsum('bsi,oi->bso', x, w) * s
        h = jax.nn.silu(_tlin(x, w1_w, w1_s)) * _tlin(x, w2_w, w2_s)
        h = jax.nn.gelu(_tlin(h, h1_w, h1_s), approximate=False)
        h = jax.nn.gelu(_tlin(h, h2_w, h2_s), approximate=False)
        return _tlin(h, w3_w, w3_s)

    def _L1_attn_ref(X, Wq, Wk, Wv):
        import jax, jax.numpy as jnp
        import numpy as np
        import math
        D_MODEL = 128
        D_QUERY = 64
        B, T, _ = X.shape
        Q = X @ Wq
        K = X @ Wk
        V = X @ Wv
        scores = jnp.einsum('btd,bsd->bts', Q, K)
        causal = jnp.tril(jnp.ones((T, T), dtype=bool))
        scores = jnp.where(causal[None, :, :], scores, -jnp.inf)
        attn = jax.nn.softmax(scores / math.sqrt(D_QUERY), axis=2)
        return attn @ V

    def _L1_ffn_ref(input_features, centroids, ln_g, ln_b, w1, b1, w2, b2):
        import jax, jax.numpy as jnp
        import numpy as np
        E, D, F = (8, 128, 512)
        LN_EPS = 1e-05
        x = input_features.reshape(-1, D)
        aff = jax.lax.stop_gradient(x) @ centroids.T
        assign = jnp.argmax(aff, axis=1)
        onehot = jax.nn.one_hot(assign, E, dtype=x.dtype)
        mu = jnp.mean(x, axis=-1, keepdims=True)
        var = jnp.mean((x - mu) ** 2, axis=-1, keepdims=True)
        xhat = (x - mu) * jax.lax.rsqrt(var + LN_EPS)
        xn = xhat[None, :, :] * ln_g[:, None, :] + ln_b[:, None, :]
        h = jax.nn.relu(jnp.einsum('etd,efd->etf', xn, w1) + b1[:, None, :])
        y = x[None, :, :] + jnp.einsum('etf,edf->etd', h, w2) + b2[:, None, :]
        alpha = jax.nn.sigmoid(x @ centroids.T)
        a = alpha.T[:, :, None]
        gated = a * y + (1.0 - a) * x[None, :, :]
        out = jnp.einsum('te,etd->td', onehot, gated)
        return out.reshape(input_features.shape)
    x = L0_attn_x
    x = x + _layernorm(_L0_attn_ref(_layernorm(x, axis=-1), L0_attn_W_in, L0_attn_A_log, L0_attn_dt_bias, L0_attn_B_norm_bias, L0_attn_C_norm_bias, L0_attn_W_out), axis=-1)
    x = x + _layernorm(_L0_ffn_ref(_layernorm(x, axis=-1), L0_ffn_w1_w, L0_ffn_w1_s, L0_ffn_w2_w, L0_ffn_w2_s, L0_ffn_h1_w, L0_ffn_h1_s, L0_ffn_h2_w, L0_ffn_h2_s, L0_ffn_w3_w, L0_ffn_w3_s), axis=-1)
    x = x + _layernorm(_L1_attn_ref(_layernorm(x, axis=-1), L1_attn_Wq, L1_attn_Wk, L1_attn_Wv), axis=-1)
    x = x + _layernorm(_L1_ffn_ref(_layernorm(x, axis=-1), L1_ffn_centroids, L1_ffn_ln_g, L1_ffn_ln_b, L1_ffn_w1, L1_ffn_b1, L1_ffn_w2, L1_ffn_b2), axis=-1)
    return x

_drawn_inputs = setup_inputs


def setup_inputs(seed=0):
    import zlib

    import numpy as np

    out = dict(_drawn_inputs(seed))
    spreads = {'L1_ffn_ln_g': (1.0, 0.2),
     'L1_ffn_ln_b': (0.0, 0.424),
     'L1_ffn_b1': (0.0, 0.44),
     'L1_ffn_b2': (0.0, 0.308)}
    factors = {}
    for name, (base, spread) in spreads.items():
        noise = np.random.default_rng([zlib.crc32(name.encode()), seed]).standard_normal(out[name].shape)
        drawn = base * np.exp(spread * noise) if base else spread * noise
        out[name] = jnp.asarray(drawn.astype(out[name].dtype))
    for name, factor in factors.items():
        out[name] = (out[name] * factor).astype(out[name].dtype)
    return out
```

```python
from contextlib import ExitStack

import concourse.bass as bass
from concourse import mybir

F32 = mybir.dt.float32
ALU = mybir.AluOpType
ACT = mybir.ActivationFunctionType
X = mybir.AxisListType.X

P = 128
T = 2048
D = 128
NT = T // P
LEAD = 2

H, R, HD, N = 32, 2, 8, 64
DI = H * HD
ROT = N // 2
NBC = (R + 1) * N
REST = NBC + 2 * H + ROT
LEV = 7
SCALE = float(N * R) ** -0.5
F = 512
FB = F // P
G = T // F
TG = F // P
DQ = 64
E = 8

LN_EPS = 1e-5
RMS_EPS = 1e-6
PI = 3.141592653589793
TWO_PI_HI = 6.28125
TWO_PI_LO = 2 * PI - TWO_PI_HI
ROUND = 12582912.0
PI_INSIDE = 3.1415925
DT_MIN, DT_MAX = 1e-4, 0.5
LOWEST = -3e38


def tile(t, c):
    return t[:, bass.ds(c, 1), :].rearrange("p a d -> p (a d)")


def cell(t, c):
    return t[:, bass.ds(c, 1)]


def per_row(t, width):
    return t.unsqueeze(2).to_broadcast([t.shape[0], t.shape[1], width])


def last(c, n=NT):
    return isinstance(c, int) and c == n - 1


def tile_pairs(eng, body, n=NT, first=0):
    for c in range(first):
        body(c, c % 2)
    with eng.Fori(first // 2, n // 2 - 1) as i:
        for k in range(2):
            body(2 * i + k, k)
    for k in range(2):
        body(n - 2 + k, k)


class Program:

    def __init__(self, nc, inputs, ctx):
        self.nc, self.i, self.ctx, self.sems, self.counts = nc, inputs, ctx, {}, {}

    def sb(self, stack, name, shape):
        return stack.enter_context(self.nc.sbuf_tensor(name, shape, F32))

    def ps(self, stack, name, shape):
        return stack.enter_context(self.nc.psum_tensor(name, shape, F32))

    def sem(self, name):
        if name not in self.sems:
            self.sems[name] = self.ctx.enter_context(self.nc.semaphore(name))
        return self.sems[name]

    def lead(self, eng, *names, n=LEAD):
        for name in names:
            eng.sem_inc(self.sem(name), n)

    def after(self, eng, name, c):
        eng.wait_ge(self.sem(name), c + 1 + LEAD)

    def settled(self, eng, name, c):
        eng.wait_ge(self.sem(name), c + 1 + LEAD)

    def link(self, eng, ins, name, n=1):
        self.counts[name] = self.counts.get(name, 0) + n
        ins.then_inc(self.sem(name), 1)
        eng.wait_ge(self.sem(name), self.counts[name])

    def load(self, eng, name, dst, src):
        eng.dma_start(dst, src).then_inc(self.sem(name), 16)


    def row_stats(self, v, rows):
        with v.Fori(0, NT // 4) as q:
            for j in range(4):
                ins = self.nc.vector.bn_stats(tile(self.st, 4 * q + j), tile(rows, 4 * q + j))
            ins.then_inc(self.sem("rows_read"), 1)
        self.counts["rows_read"] = self.counts.get("rows_read", 0) + NT // 4
        v.wait_ge(self.sem("rows_read"), self.counts["rows_read"])

    def stats_dve(self, v, n, eps=None):
        nc, st, tmp = self.nc, self.st, self.tmp
        step = lambda ins: self.link(v, ins, "dve_step")
        step(nc.vector.tensor_tensor(tmp[:, 0, :], st[:, :, 1], st[:, :, 4], ALU.add))
        step(nc.vector.tensor_scalar(self.mean[:], tmp[:, 0, :], 0.5, None, ALU.mult))
        step(nc.vector.tensor_tensor(tmp[:, 1, :], st[:, :, 1], st[:, :, 4], ALU.subtract))
        step(nc.vector.scalar_tensor_tensor(tmp[:, 2, :], tmp[:, 1, :], 0.25, tmp[:, 1, :], ALU.mult, ALU.mult))
        step(nc.vector.tensor_tensor(tmp[:, 0, :], st[:, :, 2], st[:, :, 5], ALU.add))
        step(nc.vector.scalar_tensor_tensor(tmp[:, 1, :], tmp[:, 0, :], 1.0 / D, tmp[:, 2, :], ALU.mult, ALU.add))
        if eps is None:
            nc.vector.tensor_scalar(tmp[:, 3, :], tmp[:, 1, :], LN_EPS, None, ALU.add).then_inc(self.sem("var_ready"), 1)
        else:
            nc.vector.tensor_tensor(tmp[:, 3, :], tmp[:, 1, :], eps, ALU.add).then_inc(self.sem("var_ready"), 1)
        v.wait_ge(self.sem("root_ready"), n)
        nc.vector.reciprocal(self.rstd[:], self.root[:]).then_inc(self.sem("rstd_ready"), 1)
        v.wait_ge(self.sem("rstd_ready"), n)

    def stats_act(self, a, n):
        a.wait_ge(self.sem("var_ready"), n)
        self.nc.scalar.activation(self.root[:], self.tmp[:, 3, :], ACT.Sqrt).then_inc(self.sem("root_ready"), 1)

    def residual(self, v):
        nc, ao, x = self.nc, self.ao, self.x
        step = lambda ins: self.link(v, ins, "dve_step")
        step(nc.vector.tensor_tensor(ao[:], ao[:], per_row(self.mean[:], D), ALU.subtract))
        step(nc.vector.tensor_tensor(ao[:], ao[:], per_row(self.rstd[:], D), ALU.mult))
        step(nc.vector.tensor_tensor(x[:], x[:], ao[:], ALU.add))

    def normalise(self, src, dst, c):
        return self.nc.vector.tensor_scalar(dst, tile(src, c), cell(self.mean, c), cell(self.rstd, c),
                                            ALU.subtract, ALU.mult)


def program(nc, inputs, out):
    with ExitStack() as ctx:
        p = Program(nc, inputs, ctx)
        p.x = p.sb(ctx, "x_res", [P, NT, D])
        p.ao = p.sb(ctx, "layer_out", [P, NT, D])
        p.const = p.sb(ctx, "consts", [P, 6, P])
        p.ident, p.ones, p.shift, p.corner, p.mask_ts, p.mask_st = (p.const[:, j, :] for j in range(6))
        p.st = p.sb(ctx, "row_stats", [P, NT, 6])
        p.mean = p.sb(ctx, "mean", [P, NT])
        p.root = p.sb(ctx, "root", [P, NT])
        p.rstd = p.sb(ctx, "rstd", [P, NT])
        p.tmp = p.sb(ctx, "stats_tmp", [P, 4, NT])
        p.xn = p.sb(ctx, "xn", [P, 2, D])
        p.xt = p.sb(ctx, "xt", [P, 2, P])
        p.bias = p.sb(ctx, "act_bias", [P, 2])
        with ExitStack() as m:
            p.xb = p.sb(m, "x_heads", [P, NT, R * DI])
            p.sz = p.sb(m, "silu_z", [P, NT, DI])
            p.bcr = p.sb(m, "bc_rotated", [P, NT, NBC])
            p.es = p.sb(m, "source_scale", [P, LEV + 2, NT, H])
            p.et = p.sb(m, "target_scale", [P, LEV, NT, H])
            p.cd = p.sb(m, "chunk_decay", [N, NT, H])
            p.gmask = p.sb(m, "level_mask", [P, LEV + 1, R, P])
            with ExitStack() as m1:
                p.rest = p.sb(m1, "proj_rest", [P, NT, REST])
                project(p)
                decays(p)
            with ExitStack() as m1:
                p.y = p.xb[:, :, 0:DI]
                scan(p)
                mixer_out(p)
        mlp(p)
        attention(p)
        experts(p, out)


def project(p):
    nc, i = p.nc, p.i
    with ExitStack() as s:
        w_in = p.sb(s, "w_in", [P, DI + R * DI + REST])
        pt = p.ps(s, "xt_psum", [P, 2, 512])
        px = p.ps(s, "x_psum", [P, 2, 512])
        pz = p.ps(s, "z_psum", [P, 2, 512])
        pr = p.ps(s, "rest_psum", [P, 2, 512])
        block = s.enter_context(nc.Block())

        @block.sync
        def _(sp):
            p.load(sp, "x_in", p.x[:], i["L0_attn_x"].rearrange("a (c p) d -> p (a c) d", p=P))
            p.load(sp, "const_in", p.const[:], i["consts"])
            p.load(sp, "w_in_in", w_in[:], i["L0_attn_W_in"])

        @block.vector
        def _(v):
            p.lead(v, "rest_out", "a_normed")
            v.wait_ge(p.sem("x_in"), 16)
            p.row_stats(v, p.x)
            p.stats_dve(v, 1)

            def normed(c, k):
                p.after(v, "a_turned", c - 2)
                p.normalise(p.x, p.xn[:, k, :], c).then_inc(p.sem("a_normed"), 1)

            normed(0, 0)
            normed(1, 1)

            def body(c, k):
                p.after(v, "projected", c)
                p.settled(v, "projected", k)
                nc.vector.tensor_copy(tile(p.rest, c), pr[:, k, 0:REST]).then_inc(p.sem("rest_out"), 1)
                if not (isinstance(c, int) and c >= NT - 2):
                    normed(c + 2, k)

            tile_pairs(v, body)

        @block.tensor
        def _(t):
            p.lead(t, "a_turned", "projected")

            def turn(c, k):
                p.after(t, "a_normed", c)
                p.after(t, "a_xt_out", c - 2)
                nc.tensor.transpose(pt[:, k, 0:P], p.xn[:, k, :], p.ident).then_inc(p.sem("a_turned"), 1)

            t.wait_ge(p.sem("const_in"), 16)
            turn(0, 0)
            t.wait_ge(p.sem("w_in_in"), 16)

            def body(c, k):
                if not last(c):
                    turn(c + 1, 1 - k)
                p.after(t, "a_xt_out", c)
                p.after(t, "silu_out", c - 2)
                p.after(t, "rest_out", c - 2)
                for bank, lo, hi in ((px, DI, DI + R * DI), (pz, 0, DI), (pr, DI + R * DI, DI + R * DI + REST)):
                    ins = nc.tensor.matmul(bank[:, k, 0:hi - lo], p.xt[:, k, :], w_in[:, lo:hi], start=True, stop=True)
                ins.then_inc(p.sem("projected"), 1)

            tile_pairs(t, body)

        @block.scalar
        def _(a):
            p.lead(a, "a_xt_out", "silu_out")
            p.stats_act(a, 1)

            def xt_out(c, k):
                p.after(a, "a_turned", c)
                p.after(a, "projected", c - 2)
                nc.scalar.activation(p.xt[:, k, :], pt[:, k, 0:P], ACT.Copy).then_inc(p.sem("a_xt_out"), 1)

            xt_out(0, 0)

            def body(c, k):
                if not last(c):
                    xt_out(c + 1, 1 - k)
                p.after(a, "projected", c)
                p.settled(a, "projected", k)
                nc.scalar.activation(tile(p.xb, c).rearrange("p (r h q) -> p h r q", r=R, q=HD),
                                     px[:, k, :].rearrange("p (h r q) -> p h r q", r=R, q=HD), ACT.Silu)
                nc.scalar.activation(tile(p.sz, c), pz[:, k, 0:DI], ACT.Silu).then_inc(p.sem("silu_out"), 1)

            tile_pairs(a, body)


def decays(p):
    nc, i = p.nc, p.i
    rest = p.rest
    bc = rest[:, :, 0:NBC]
    dt_raw, lam_raw = rest[:, :, NBC:NBC + H], rest[:, :, NBC + H:NBC + 2 * H]
    theta = rest[:, :, NBC + 2 * H:REST]
    S = p.sem
    with ExitStack() as s:
        tri = p.sb(s, "triangles", [P, 2 * LEV, P])
        vecs = p.sb(s, "head_vecs", [P, 2, H])
        nbias = p.sb(s, "norm_bias", [P, R + 1, N])
        rms = p.sb(s, "rms", [P, NT * (R + 1)])
        m = p.sb(s, "dt_sum", [P, NT])
        names = ["u", "dt", "la", "lam", "v", "w", "mt", "cos", "sin", "turns", "angle"]
        small = {n: p.sb(s, "d_" + n, [P, NT, H]) for n in names}
        u, dt, la, lam, vv, w, mt, cos, sin, turns, angle = (small[n][:] for n in names)
        sq = p.sb(s, "squares", [P, NT, NBC])
        rot = p.sb(s, "rotation", [P, NT, R + 1, ROT])
        banks = [p.ps(s, f"exp_psum{j}", [P, 512]) for j in range(6)]
        p_ang = p.ps(s, "angle_psum", [P, 512])
        p_next = p.ps(s, "next_psum", [P, 512])
        flat = lambda ap: ap.rearrange("p c h -> p (c h)")
        block = s.enter_context(nc.Block())

        @block.sync
        def _(sp):
            p.load(sp, "tri_in", tri[:], i["triangles"])
            p.load(sp, "tri_in", p.gmask[:], i["level_masks"])
            p.load(sp, "vecs_in", vecs[:, 0, :], i["L0_attn_dt_bias"].unsqueeze(0).to_broadcast([P, H]))
            p.load(sp, "vecs_in", vecs[:, 1, :], i["L0_attn_A_log"].unsqueeze(0).to_broadcast([P, H]))
            for r, name in enumerate(["B", "B", "C"]):
                p.load(sp, "nbias_in", nbias[:, r, :], i[f"L0_attn_{name}_norm_bias"].to_broadcast([P, N]))

        sums = [(p.et[:, l, :, :], tri[:, l, :]) for l in range(LEV)]
        sums += [(p.es[:, l + 1, :, :], p.shift if l == 0 else tri[:, LEV + l - 1, :]) for l in range(LEV + 1)]
        sums += [(p.cd[:], p.ones[:, 0:N])]

        @block.vector
        def _(v):
            step = lambda ins: p.link(v, ins, "dve_step")
            step(nc.vector.memset(p.bias[:, 0:1], 1.0))
            nc.vector.memset(p.bias[:, 1:2], RMS_EPS).then_inc(S("bias_set"), 1)
            v.wait_ge(S("vecs_in"), 32)
            step(nc.vector.tensor_tensor(u, dt_raw, vecs[:, 0:1, :].to_broadcast([P, NT, H]), ALU.add))
            nc.vector.tensor_scalar(u, u, 20.0, None, ALU.min).then_inc(S("dt_arg"), 1)
            nc.vector.tensor_scalar(lam, lam_raw, -87.0, None, ALU.max).then_inc(S("lam_arg"), 1)
            v.wait_ge(S("softplus_out"), 1)
            step(nc.vector.tensor_scalar(dt, dt, DT_MIN, DT_MAX, ALU.max, ALU.min))
            nc.vector.scalar_tensor_tensor(la, dt, -1.0, vecs[:, 1:2, :].to_broadcast([P, NT, H]), ALU.mult, ALU.mult).then_inc(S("la_ready"), 1)
            step(nc.vector.tensor_reduce(m[:], dt, X, ALU.add))
            nc.vector.scalar_tensor_tensor(mt, theta, -1.0 / H, per_row(m[:], ROT), ALU.mult, ALU.mult).then_inc(S("turns_ready"), 1)
            v.wait_ge(S("lam_exp"), 1)
            step(nc.vector.tensor_scalar(lam, lam, 1.0, None, ALU.add))
            step(nc.vector.reciprocal(lam, lam))
            step(nc.vector.tensor_tensor(p.es[:, 0, :, :], lam, dt, ALU.mult))
            nc.vector.tensor_tensor(vv, dt, p.es[:, 0, :, :], ALU.subtract).then_inc(S("v_ready"), 1)
            v.wait_ge(S("squared"), 1)
            nc.vector.tensor_reduce(rms[:], sq[:].rearrange("p c (r n) -> p (c r) n", n=N), X, ALU.add).then_inc(S("ms_ready"), 1)
            v.wait_ge(S("angle_summed"), 1)
            step(nc.vector.tensor_scalar(flat(turns), p_ang[:], 1.0 / (2 * PI), ROUND, ALU.mult, ALU.add))
            step(nc.vector.tensor_scalar(turns, turns, ROUND, None, ALU.subtract))
            step(nc.vector.scalar_tensor_tensor(flat(angle), flat(turns), -TWO_PI_HI, p_ang[:], ALU.mult, ALU.add))
            step(nc.vector.scalar_tensor_tensor(angle, turns, -TWO_PI_LO, angle, ALU.mult, ALU.add))
            step(nc.vector.tensor_scalar(angle, angle, PI_INSIDE, -PI_INSIDE, ALU.min, ALU.max))
            step(nc.vector.scalar_tensor_tensor(turns, angle, -1.0, angle, ALU.mult, ALU.min))
            nc.vector.tensor_scalar(turns, turns, PI / 2, None, ALU.add).then_inc(S("angle_ready"), 1)
            v.wait_ge(S("rms_root"), 1)
            step(nc.vector.reciprocal(rms[:], rms[:]))
            c_rms = rms[:].rearrange("p (c r) -> p c r", r=R + 1)[:, :, R]
            nc.vector.tensor_scalar(c_rms, c_rms, SCALE, None, ALU.mult).then_inc(S("rms_ready"), 1)
            v.wait_ge(S("next_summed"), 1)
            step(nc.vector.tensor_tensor(flat(w), p_next[:], flat(p.es[:, 0, :, :]), ALU.add))
            for n, (dst, _) in enumerate(sums):
                if LEV <= n < 2 * LEV + 1:
                    v.wait_ge(S("exp_out"), n + 1)
                    step(nc.vector.tensor_tensor(dst, dst, w, ALU.mult))
            v.wait_ge(S("trig_out"), 1)
            v.wait_ge(S("bc_normed"), 1)
            halves = bc.rearrange("p c (r f n) -> p c r f n", r=R + 1, f=2)
            out = p.bcr[:].rearrange("p c (r f n) -> p c r f n", r=R + 1, f=2)
            for r in range(R + 1):
                nc.vector.tensor_tensor(out[:, :, r, 0, :], halves[:, :, r, 0, :], cos, ALU.mult)
                step(nc.vector.tensor_tensor(rot[:, :, r, :], halves[:, :, r, 1, :], sin, ALU.mult))
            nc.vector.tensor_tensor(out[:, :, :, 0, :], out[:, :, :, 0, :], rot[:], ALU.subtract).then_inc(S("rotated"), 1)

        @block.gpsimd
        def _(g):
            step = lambda ins: p.link(g, ins, "pool_step")
            g.wait_ge(S("rms_ready"), 1)
            g.wait_ge(S("nbias_in"), 48)
            groups = bc.rearrange("p c (r n) -> p c r n", n=N)
            for r in range(R + 1):
                step(nc.gpsimd.tensor_tensor(groups[:, :, r, :], groups[:, :, r, :],
                                             per_row(rms[:].rearrange("p (c r) -> p c r", r=R + 1)[:, :, r], N), ALU.mult))
            for r in range(R + 1):
                ins = nc.gpsimd.tensor_tensor(groups[:, :, r, :], groups[:, :, r, :],
                                              nbias[:, r:r + 1, :].to_broadcast([P, NT, N]), ALU.mult)
                ins.then_inc(S("bc_normed" if r == R else "bc_biased"), 1)
            g.wait_ge(S("bc_biased"), R)
            g.wait_ge(S("bc_normed"), 1)
            g.wait_ge(S("trig_out"), 1)
            halves = bc.rearrange("p c (r f n) -> p c r f n", r=R + 1, f=2)
            out = p.bcr[:].rearrange("p c (r f n) -> p c r f n", r=R + 1, f=2)
            prod = sq[:].rearrange("p c (f r n) -> p c f r n", f=2, r=R + 1)
            for r in range(R + 1):
                step(nc.gpsimd.tensor_tensor(prod[:, :, 0, r, :], halves[:, :, r, 0, :], sin, ALU.mult))
                step(nc.gpsimd.tensor_tensor(prod[:, :, 1, r, :], halves[:, :, r, 1, :], cos, ALU.mult))
                step(nc.gpsimd.tensor_tensor(out[:, :, r, 1, :], prod[:, :, 0, r, :], prod[:, :, 1, r, :], ALU.add))

        @block.scalar
        def _(a):
            step = lambda ins: p.link(a, ins, "act_step")
            a.wait_ge(S("vecs_in"), 32)
            step(nc.scalar.activation(vecs[:, 1, :], vecs[:, 1, :], ACT.Exp))
            a.wait_ge(S("dt_arg"), 1)
            a.wait_ge(S("bias_set"), 1)
            step(nc.scalar.activation(u, u, ACT.Exp))
            nc.scalar.activation(dt, u, ACT.Ln, bias=p.bias[:, 0:1]).then_inc(S("softplus_out"), 1)
            a.wait_ge(S("lam_arg"), 1)
            nc.scalar.activation(lam, lam, ACT.Exp, scale=-1.0).then_inc(S("lam_exp"), 1)
            nc.scalar.activation(sq[:], bc, ACT.Square).then_inc(S("squared"), 1)
            for n, (dst, _) in enumerate(sums):
                rows = N if n == 2 * LEV + 1 else P
                a.wait_ge(S("exp_summed"), n + 1)
                nc.scalar.activation(flat(dst), banks[n % 6][0:rows, :], ACT.Exp).then_inc(S("exp_out"), 1)
            a.wait_ge(S("ms_ready"), 1)
            nc.scalar.activation(rms[:], rms[:], ACT.Sqrt, scale=1.0 / N, bias=p.bias[:, 1:2]).then_inc(S("rms_root"), 1)
            a.wait_ge(S("angle_ready"), 1)
            step(nc.scalar.activation(sin, angle, ACT.Sin))
            nc.scalar.activation(cos, turns, ACT.Sin).then_inc(S("trig_out"), 1)

        @block.tensor
        def _(t):
            t.wait_ge(S("tri_in"), 32)
            t.wait_ge(S("turns_ready"), 1)
            nc.tensor.matmul(p_ang[:], tri[:, LEV - 1, :], flat(mt), start=True, stop=False)
            for c in range(NT - 1):
                n = NT - 1 - c
                ins = nc.tensor.matmul(p_ang[:, (c + 1) * ROT:].rearrange("p (c h) -> p c h", c=n), p.ones,
                                       mt[:, c:c + 1, :].to_broadcast([P, n, ROT]), start=False, stop=(c == NT - 2))
            ins.then_inc(S("angle_summed"), 1)
            t.wait_ge(S("v_ready"), 1)
            nc.tensor.matmul(p_next[:], p.shift, flat(vv), start=True, stop=False)
            nc.tensor.matmul(p_next[:, 0:(NT - 1) * H], p.corner, flat(vv)[:, H:], start=False, stop=True).then_inc(S("next_summed"), 1)
            t.wait_ge(S("la_ready"), 1)
            for n, (dst, lhs) in enumerate(sums):
                if n >= 6:
                    t.wait_ge(S("exp_out"), n - 5)
                rows = N if n == 2 * LEV + 1 else P
                nc.tensor.matmul(banks[n % 6][0:rows, :], lhs, flat(la), start=True, stop=True).then_inc(S("exp_summed"), 1)


BY_DVE = 5


def scan(p):
    nc = p.nc
    S = p.sem
    with ExitStack() as s:
        bcs = p.sb(s, "bc_tile", [P, 2, NBC])
        bct = p.sb(s, "bc_turned", [N, 2, R + 1, P])
        gm = p.sb(s, "scores", [P, 2, LEV + 1, R, P])
        xs = p.sb(s, "x_scaled", [P, 2, LEV + 2, R * DI])
        state = p.sb(s, "state", [N, 2, DI])
        decayed = p.sb(s, "state_decayed", [N, 2, DI])
        tm = p.sb(s, "terms", [P, 2, LEV, DI])
        pt = p.ps(s, "bct_psum", [P, 512])
        pg = p.ps(s, "score_psum", [P, 512])
        p_st = p.ps(s, "state_psum", [P, 512])
        p_terms = p.ps(s, "terms_psum", [P, LEV + 1, DI])
        block = s.enter_context(nc.Block())

        def scale(engine, c, k, level):
            heads = lambda ap: ap.rearrange("p (r h q) -> p r h q", r=R, q=HD)
            e = tile(p.es[:, level, :, :], c).unsqueeze(1).unsqueeze(3).to_broadcast([P, R, H, HD])
            return engine.tensor_tensor(heads(xs[:, k, level, :]), heads(tile(p.xb, c)), e, ALU.mult)

        @block.scalar
        def _(a):
            p.lead(a, "b_tile_in", "b_turned_out")

            def turned(c, k):
                p.after(a, "b_state_summed", c - 2)
                p.settled(a, "b_state_summed", k - 2)
                nc.scalar.activation(bcs[:, k, :], tile(p.bcr, c), ACT.Copy).then_inc(S("b_tile_in"), 1)
                p.after(a, "b_turned", c)
                p.after(a, "b_terms", c - 2)
                nc.scalar.activation(bct[:, k, :, :], pt[0:N, 0:(R + 1) * P].rearrange("p (r n) -> p r n", n=P),
                                     ACT.Copy).then_inc(S("b_turned_out"), 1)

            turned(0, 0)

            def body(c, k):
                if not last(c):
                    turned(c + 1, 1 - k)

            tile_pairs(a, body)

        @block.tensor
        def _(t):
            p.lead(t, "b_turned", "b_scores", "b_terms", "b_state_summed")

            def turn_waits(c):
                p.after(t, "b_tile_in", c)
                p.after(t, "b_turned_out", c - 1)

            def turn(k):
                for r in range(R + 1):
                    ins = nc.tensor.transpose(pt[0:N, r * P:(r + 1) * P], bcs[:, k, r * N:(r + 1) * N], p.ident)
                ins.then_inc(S("b_turned"), 1)

            def scores(c, k):
                p.after(t, "b_turned_out", c)
                p.after(t, "b_masked", c - 1)
                for r in range(R):
                    ins = nc.tensor.matmul(pg[:, r * P:(r + 1) * P], bct[:, k, r, :], bct[:, k, R, :], start=True, stop=True)
                ins.then_inc(S("b_scores"), 1)

            turn_waits(0)
            turn(0)
            scores(0, 0)

            def body(c, k):
                if not last(c):
                    turn_waits(c + 1)
                p.after(t, "b_scaled_dve", c)
                p.after(t, "b_scaled_pool", c)
                p.after(t, "b_state", c)
                for r in range(R):
                    ins = nc.tensor.matmul(p_st[0:N, 0:DI], bcs[:, k, r * N:(r + 1) * N],
                                           xs[:, k, LEV + 1, r * DI:(r + 1) * DI], start=(r == 0), stop=(r == R - 1))
                    if r == 0 and not last(c):
                        turn(1 - k)
                ins.then_inc(S("b_state_summed"), 1)
                if not last(c):
                    scores(c + 1, 1 - k)
                p.after(t, "b_masked", c)
                p.after(t, "b_terms_out", c - 1)
                for l in range(LEV):
                    parts = [(j, r) for j in ((0, 1) if l == 0 else (l + 1,)) for r in range(R)]
                    for n, (j, r) in enumerate(parts):
                        nc.tensor.matmul(p_terms[:, l, :], gm[:, k, j, r, :], xs[:, k, j, r * DI:(r + 1) * DI],
                                         start=(n == 0), stop=(n == len(parts) - 1))
                nc.tensor.matmul(p_terms[:, LEV, :], bct[:, k, R, :], state[:, k, :], start=True, stop=True).then_inc(S("b_terms"), 1)

            tile_pairs(t, body)

        @block.vector
        def _(v):
            p.lead(v, "b_masked", "b_scaled_dve", "b_decayed", "b_state", "b_terms_scaled", "b_terms_out", "b_gated")
            nc.vector.memset(state[:, 0, :], 0.0).then_inc(S("b_state"), 1)

            def sources(c, k):
                p.after(v, "b_scores", c)
                p.after(v, "b_terms", c - 2)
                nc.vector.tensor_tensor(gm[:, k, :, :, :].rearrange("p l r m -> p l (r m)"),
                                        pg[:, 0:R * P].unsqueeze(1).to_broadcast([P, LEV + 1, R * P]),
                                        p.gmask[:].rearrange("p l r m -> p l (r m)"), ALU.mult).then_inc(S("b_masked"), 1)
                for level in range(BY_DVE):
                    ins = scale(nc.vector, c, k, LEV + 1 - level)
                ins.then_inc(S("b_scaled_dve"), 1)

            def gate(c, k):
                p.after(v, "b_y", c)
                nc.vector.tensor_tensor(tile(p.y, c), tm[:, k, 0, :], tile(p.sz, c), ALU.mult).then_inc(S("b_gated"), 1)

            sources(0, 0)

            def body(c, k):
                if not last(c):
                    sources(c + 1, 1 - k)
                    p.after(v, "b_state", c)
                    nc.vector.tensor_tensor(decayed[:, k, :].rearrange("p (h q) -> p h q", q=HD),
                                            state[:, k, :].rearrange("p (h q) -> p h q", q=HD),
                                            per_row(tile(p.cd, c), HD), ALU.mult).then_inc(S("b_decayed"), 1)
                    p.after(v, "b_decayed", c)
                    p.after(v, "b_state_summed", c)
                    p.after(v, "b_terms", c - 1)
                    nc.vector.tensor_tensor(state[:, 1 - k, :], decayed[:, k, :], p_st[0:N, 0:DI], ALU.add).then_inc(S("b_state"), 1)
                if not (isinstance(c, int) and c == 0):
                    gate(c - 1, 1 - k)
                p.after(v, "b_terms", c)
                p.after(v, "b_gated", c - 2)
                e = p.et[:, :, bass.ds(c, 1), :].rearrange("p l c h -> p l (c h)").unsqueeze(3).to_broadcast([P, LEV, H, HD])
                nc.vector.tensor_tensor(tm[:, k, :, :].rearrange("p l (h q) -> p l h q", q=HD),
                                        p_terms[:, 1:LEV + 1, :].rearrange("p l (h q) -> p l h q", q=HD),
                                        e, ALU.mult).then_inc(S("b_terms_scaled"), 1)
                p.after(v, "b_terms_scaled", c)
                nc.vector.tensor_tensor(tm[:, k, 0, :], p_terms[:, 0, :], tm[:, k, 0, :], ALU.add).then_inc(S("b_terms_out"), 1)

            tile_pairs(v, body, first=2)
            gate(NT - 1, 1)

        @block.gpsimd
        def _(g):
            p.lead(g, "b_scaled_pool", "b_half", "b_quarter", "b_y")

            def sources(c, k):
                p.after(g, "b_terms", c - 2)
                p.settled(g, "b_terms", k - 2)
                for level in range(LEV + 2 - BY_DVE):
                    ins = scale(nc.gpsimd, c, k, level)
                ins.then_inc(S("b_scaled_pool"), 1)

            sources(0, 0)

            def body(c, k):
                if not last(c):
                    sources(c + 1, 1 - k)
                p.after(g, "b_terms_out", c)
                nc.gpsimd.tensor_tensor(tm[:, k, 0:3, :], tm[:, k, 0:3, :], tm[:, k, 4:7, :], ALU.add).then_inc(S("b_half"), 1)
                p.after(g, "b_half", c)
                nc.gpsimd.tensor_tensor(tm[:, k, 0:2, :], tm[:, k, 0:2, :], tm[:, k, 2:4, :], ALU.add).then_inc(S("b_quarter"), 1)
                p.after(g, "b_quarter", c)
                nc.gpsimd.tensor_tensor(tm[:, k, 0, :], tm[:, k, 0, :], tm[:, k, 1, :], ALU.add).then_inc(S("b_y"), 1)

            tile_pairs(g, body)


def mixer_out(p):
    nc, S = p.nc, p.sem
    with ExitStack() as s:
        wo = p.sb(s, "w_out", [P, 2, D])
        ys = p.sb(s, "y_gated", [P, 2, DI])
        sq = p.sb(s, "y_squares", [P, DI])
        yt = p.sb(s, "y_turned", [P, 2, DI])
        ss = p.sb(s, "y_square_sum", [P, NT])
        pt = p.ps(s, "yt_psum", [P, 2, 512])
        po = p.ps(s, "out_psum", [P, 2, 512])
        block = s.enter_context(nc.Block())

        @block.sync
        def _(sp):
            p.load(sp, "w_out_in", wo[:], p.i["L0_attn_W_out"].rearrange("(j p) d -> p j d", p=P))

        @block.tensor
        def _(t):
            p.lead(t, "c_turned", "c_multiplied")

            def turn(c, k):
                p.after(t, "c_gated", c)
                p.after(t, "c_turned_out", c - 2)
                for j in range(2):
                    ins = nc.tensor.transpose(pt[:, k, j * P:(j + 1) * P], ys[:, k, j * P:(j + 1) * P], p.ident)
                ins.then_inc(S("c_turned"), 1)

            turn(0, 0)
            t.wait_ge(S("w_out_in"), 16)

            def body(c, k):
                if not last(c):
                    turn(c + 1, 1 - k)
                p.after(t, "c_turned_out", c)
                p.after(t, "c_out", c - 2)
                for j in range(2):
                    ins = nc.tensor.matmul(po[:, k, 0:D], yt[:, k, j * P:(j + 1) * P], wo[:, j, :], start=(j == 0), stop=(j == 1))
                ins.then_inc(S("c_multiplied"), 1)

            tile_pairs(t, body)

        @block.scalar
        def _(a):
            p.lead(a, "c_gated", "c_squared", "c_turned_out")

            def body(c, k):
                p.after(a, "c_turned", c - 2)
                nc.scalar.activation(ys[:, k, :], tile(p.y, c), ACT.Copy).then_inc(S("c_gated"), 1)
                p.after(a, "c_squared", c - 1)
                nc.scalar.activation(sq[:], tile(p.y, c), ACT.Square, accum_out=cell(ss, c)).then_inc(S("c_squared"), 1)
                p.after(a, "c_turned", c)
                p.after(a, "c_multiplied", c - 2)
                nc.scalar.activation(yt[:, k, :], pt[:, k, 0:DI], ACT.Copy).then_inc(S("c_turned_out"), 1)

            tile_pairs(a, body)
            p.stats_act(a, 2)

        @block.vector
        def _(v):
            p.lead(v, "c_out")

            def body(c, k):
                p.after(v, "c_multiplied", c)
                p.settled(v, "c_multiplied", k)
                nc.vector.tensor_copy(tile(p.ao, c), po[:, k, 0:D])
                nc.vector.bn_stats(tile(p.st, c), po[:, k, 0:D]).then_inc(S("c_out"), 1)

            tile_pairs(v, body)
            p.after(v, "c_squared", NT - 1)
            p.after(v, "c_out", NT - 1)
            p.link(v, nc.vector.tensor_scalar(ss[:], ss[:], LN_EPS / DI, LN_EPS * RMS_EPS, ALU.mult, ALU.add), "dve_step")
            p.stats_dve(v, 2, eps=ss[:])
            p.residual(v)
            p.row_stats(v, p.x)


def mlp(p):
    nc, S, i = p.nc, p.sem, p.i
    with ExitStack() as s:
        w12 = p.sb(s, "w12", [P, 2, F])
        h12 = p.sb(s, "h12", [P, 2, FB, F])
        w3 = p.sb(s, "w3", [P, FB, D])
        scales = p.sb(s, "hidden_scales", [P, 4, FB])
        s3 = p.sb(s, "w3_scale", [P, D])
        xn4 = p.sb(s, "mlp_xn", [P, TG, D])
        xt4 = p.sb(s, "mlp_xt", [P, F])
        ts = p.sb(s, "silu_part", [P, 2, F])
        h = [p.sb(s, f"hidden{j}", [P, FB, F]) for j in range(3)]
        pt = p.ps(s, "mlp_xt_psum", [P, F])
        pa = p.ps(s, "w1_psum", [P, 2, F])
        pb = p.ps(s, "w2_psum", [P, 2, F])
        ph = p.ps(s, "hidden_psum", [P, 2, F])
        po = p.ps(s, "mlp_out_psum", [P, TG, D])
        block = s.enter_context(nc.Block())

        @block.sync
        def _(sp):
            p.load(sp, "w12_in", w12[:, 0, :], i["w1T"])
            p.load(sp, "w12_in", w12[:, 1, :], i["w2T"])
            for j, name in enumerate(["w1_s", "w2_s", "h1_s", "h2_s"]):
                p.load(sp, "scales_in", scales[:, j, :], i[name])
            p.load(sp, "scales_in", s3[:], i["L0_ffn_w3_s"].unsqueeze(0).to_broadcast([P, D]))
            for j in range(2):
                p.load(sp, "h12_in", h12[:, j, :, :], i[f"h{j + 1}T"].rearrange("(k p) o -> p k o", p=P))
            p.load(sp, "h12_in", w3[:], i["w3T"].rearrange("(k p) o -> p k o", p=P))

        def hidden(n, g, m):
            return FB * g + m + 1 + LEAD

        @block.tensor
        def _(t):
            p.lead(t, "d_turned", "d_up", "d_hidden", "d_down")
            t.wait_ge(S("w12_in"), 32)
            t.wait_ge(S("h12_in"), 48)
            with t.Fori(0, G) as g:
                t.wait_ge(S("d_normed"), g + 1)
                t.wait_ge(S("d_xt_out"), g + LEAD)
                for j in range(TG):
                    ins = nc.tensor.transpose(pt[:, j * P:(j + 1) * P], xn4[:, j, :], p.ident)
                ins.then_inc(S("d_turned"), 1)
                t.wait_ge(S("d_xt_out"), g + 1 + LEAD)
                for m in range(FB):
                    t.wait_ge(S("d_gated"), hidden(0, g, m - 2))
                    nc.tensor.matmul(pa[:, m % 2, :], w12[:, 0, m * P:(m + 1) * P], xt4[:], start=True, stop=True)
                    nc.tensor.matmul(pb[:, m % 2, :], w12[:, 1, m * P:(m + 1) * P], xt4[:], start=True, stop=True).then_inc(S("d_up"), 1)
                t.wait_ge(S("d_gated"), hidden(0, g, FB - 1))
                for l in range(2):
                    for m in range(FB):
                        n = FB * l + m
                        t.wait_ge(S("d_gelu"), 2 * FB * g + n - 1 + LEAD)
                        for kk in range(FB):
                            ins = nc.tensor.matmul(ph[:, m % 2, :], h12[:, l, kk, m * P:(m + 1) * P], h[l][:, kk, :],
                                                   start=(kk == 0), stop=(kk == FB - 1))
                        ins.then_inc(S("d_hidden"), 1)
                    t.wait_ge(S("d_gelu"), 2 * FB * g + FB * (l + 1) + LEAD)
                t.wait_ge(S("d_out"), g + LEAD)
                for j in range(TG):
                    for kk in range(FB):
                        ins = nc.tensor.matmul(po[:, j, :], h[2][:, kk, j * P:(j + 1) * P], w3[:, kk, :],
                                               start=(kk == 0), stop=(kk == FB - 1))
                ins.then_inc(S("d_down"), 1)

        @block.scalar
        def _(a):
            p.stats_act(a, 3)
            p.lead(a, "d_xt_out", "d_silu", "d_gelu")
            a.wait_ge(S("scales_in"), 80)
            with a.Fori(0, G) as g:
                a.wait_ge(S("d_turned"), g + 1 + LEAD)
                a.wait_ge(S("d_up"), hidden(0, g, -1))
                nc.scalar.activation(xt4[:], pt[:], ACT.Copy).then_inc(S("d_xt_out"), 1)
                for m in range(FB):
                    a.wait_ge(S("d_up"), hidden(0, g, m))
                    a.wait_ge(S("d_gated"), hidden(0, g, m - 2))
                    nc.scalar.activation(ts[:, m % 2, :], pa[:, m % 2, :], ACT.Silu, scale=scales[:, 0, m:m + 1]).then_inc(S("d_silu"), 1)
                for l in range(2):
                    for m in range(FB):
                        a.wait_ge(S("d_hidden"), 2 * FB * g + FB * l + m + 1 + LEAD)
                        if l == 1 and m == 0:
                            a.wait_ge(S("d_down"), g + LEAD)
                        nc.scalar.activation(h[l + 1][:, m, :], ph[:, m % 2, :], ACT.Gelu, scale=scales[:, 2 + l, m:m + 1]).then_inc(S("d_gelu"), 1)
            p.stats_act(a, 4)

        @block.vector
        def _(v):
            p.lead(v, "d_gated", "d_out")
            p.stats_dve(v, 3)
            v.wait_ge(S("scales_in"), 80)
            with v.Fori(0, G) as g:
                v.wait_ge(S("d_turned"), g + LEAD)
                for j in range(TG):
                    ins = p.normalise(p.x, xn4[:, j, :], TG * g + j)
                ins.then_inc(S("d_normed"), 1)
                for m in range(FB):
                    v.wait_ge(S("d_silu"), hidden(0, g, m))
                    nc.vector.scalar_tensor_tensor(h[0][:, m, :], pb[:, m % 2, :], scales[:, 1, m:m + 1], ts[:, m % 2, :],
                                                   ALU.mult, ALU.mult).then_inc(S("d_gated"), 1)
                v.wait_ge(S("d_down"), g + 1 + LEAD)
                nc.vector.tensor_tensor(p.ao[:, bass.ds(TG * g, TG), :], po[:], s3[:].unsqueeze(1).to_broadcast([P, TG, D]),
                                        ALU.mult).then_inc(S("d_out"), 1)
            v.wait_ge(S("d_out"), G + LEAD)
            p.row_stats(v, p.ao)
            p.stats_dve(v, 4)
            p.residual(v)
            p.row_stats(v, p.x)


def attention(p):
    nc, S, i = p.nc, p.sem, p.i
    QV = D + DQ
    with ExitStack() as s:
        wk = p.sb(s, "w_q_k", [P, 2, DQ])
        wvq = p.sb(s, "w_v_q", [P, QV])
        qt = p.sb(s, "q_turned", [DQ, T])
        kt = p.sb(s, "k_turned", [DQ + 1, T])
        q = p.sb(s, "q_rows", [P, NT, DQ + 1])
        val = p.sb(s, "v_rows", [P, NT, D + 1])
        qta = p.sb(s, "q_max_turned", [DQ + 1, T])
        part = p.sb(s, "part_max", [P, NT, G])
        mx = p.sb(s, "row_max", [P, NT])
        probs = p.sb(s, "probs", [P, 4, F])
        den = p.sb(s, "denominator", [P, NT])

        with ExitStack() as b:
            pt = p.ps(b, "att_xt_psum", [P, 2, 512])
            pqk = p.ps(b, "qk_psum", [P, 2, 512])
            pvq = p.ps(b, "vq_psum", [P, 2, 512])
            block = b.enter_context(nc.Block())

            @block.sync
            def _(sp):
                p.load(sp, "att_in", wk[:, 0, :], i["L1_attn_Wq"])
                p.load(sp, "att_in", wk[:, 1, :], i["L1_attn_Wk"])
                p.load(sp, "att_in", wvq[:, 0:D], i["L1_attn_Wv"])
                p.load(sp, "att_in", wvq[:, D:QV], i["L1_attn_Wq"])

            @block.gpsimd
            def _(g):
                p.link(g, nc.gpsimd.memset(kt[DQ:DQ + 1, :], 1.0), "pool_step")
                nc.gpsimd.memset(val[:, :, D:D + 1], 1.0).then_inc(S("ones_set"), 1)

            @block.tensor
            def _(t):
                p.lead(t, "e_turned", "e_projected")

                def turn(c, k):
                    p.after(t, "e_normed", c)
                    p.after(t, "e_xt_out", c - 2)
                    nc.tensor.transpose(pt[:, k, 0:P], p.xn[:, k, :], p.ident).then_inc(S("e_turned"), 1)

                turn(0, 0)
                t.wait_ge(S("att_in"), 64)

                def body(c, k):
                    if not last(c):
                        turn(c + 1, 1 - k)
                    p.after(t, "e_xt_out", c)
                    p.after(t, "e_qk_out", c - 2)
                    p.after(t, "e_vq_out", c - 2)
                    for j in range(2):
                        nc.tensor.matmul(pqk[0:DQ, k, j * P:(j + 1) * P], wk[:, j, :], p.xt[:, k, :], start=True, stop=True)
                    nc.tensor.matmul(pvq[:, k, 0:QV], p.xt[:, k, :], wvq[:], start=True, stop=True).then_inc(S("e_projected"), 1)

                tile_pairs(t, body)

            @block.scalar
            def _(a):
                p.stats_act(a, 5)
                p.lead(a, "e_xt_out", "e_qk_out")

                def xt_out(c, k):
                    p.after(a, "e_turned", c)
                    p.after(a, "e_projected", c - 2)
                    nc.scalar.activation(p.xt[:, k, :], pt[:, k, 0:P], ACT.Copy).then_inc(S("e_xt_out"), 1)

                xt_out(0, 0)

                def body(c, k):
                    if not last(c):
                        xt_out(c + 1, 1 - k)
                    p.after(a, "e_projected", c)
                    p.settled(a, "e_projected", k)
                    nc.scalar.activation(qt[:, bass.ts(c, P)], pqk[0:DQ, k, 0:P], ACT.Copy)
                    nc.scalar.activation(kt[0:DQ, bass.ts(c, P)], pqk[0:DQ, k, P:2 * P], ACT.Copy).then_inc(S("e_qk_out"), 1)

                tile_pairs(a, body)

            @block.vector
            def _(v):
                p.lead(v, "e_vq_out", "e_normed")
                p.stats_dve(v, 5)
                nc.vector.memset(part[:], LOWEST).then_inc(S("part_set"), 1)

                def normed(c, k):
                    p.after(v, "e_turned", c - 2)
                    p.normalise(p.x, p.xn[:, k, :], c).then_inc(S("e_normed"), 1)

                normed(0, 0)
                normed(1, 1)

                def body(c, k):
                    if not (isinstance(c, int) and c >= NT - 2):
                        normed(c + 2, k)
                    p.after(v, "e_projected", c)
                    p.settled(v, "e_projected", k)
                    nc.vector.tensor_copy(val[:, bass.ds(c, 1), 0:D].rearrange("p a d -> p (a d)"), pvq[:, k, 0:D])
                    nc.vector.tensor_copy(q[:, bass.ds(c, 1), 0:DQ].rearrange("p a d -> p (a d)"), pvq[:, k, D:QV]).then_inc(S("e_vq_out"), 1)

                tile_pairs(v, body)

        with ExitStack() as b:
            banks = [p.ps(b, f"score_bank{j}", [P, 512]) for j in range(8)]
            block = b.enter_context(nc.Block())
            chunks = [(c, j) for c in range(NT) for j in range(c // TG + 1)]

            def width(c, j):
                return F if j < c // TG else (c % TG + 1) * P

            @block.tensor
            def _(t):
                for n, (c, j) in enumerate(chunks):
                    if n >= 8:
                        t.wait_ge(S("chunk_read"), n - 7)
                    nc.tensor.matmul(banks[n % 8][:, 0:width(c, j)], qt[:, c * P:(c + 1) * P], kt[0:DQ, j * F:j * F + width(c, j)],
                                     start=True, stop=True).then_inc(S("chunk_scored"), 1)
                t.wait_ge(S("max_set"), 1)
                for g in range(G):
                    for j in range(TG):
                        c = TG * g + j
                        ins = nc.tensor.transpose(banks[g][0:DQ + 1, j * P:(j + 1) * P], q[:, c, :], p.ident)
                    ins.then_inc(S("q_turned"), 1)

            @block.vector
            def _(v):
                for n, (c, j) in enumerate(chunks):
                    v.wait_ge(S("chunk_scored"), n + 1)
                    w = width(c, j)
                    if j == c // TG:
                        p.link(v, nc.vector.tensor_tensor(banks[n % 8][:, w - P:w], banks[n % 8][:, w - P:w], p.mask_ts, ALU.add), "dve_step")
                    nc.vector.tensor_reduce(part[:, c, j:j + 1], banks[n % 8][:, 0:w], X, ALU.max).then_inc(S("chunk_read"), 1)
                v.wait_ge(S("chunk_read"), len(chunks))
                p.link(v, nc.vector.tensor_reduce(mx[:], part[:], X, ALU.max), "dve_step")
                nc.vector.tensor_scalar(q[:, :, DQ], mx[:], -1.0, None, ALU.mult).then_inc(S("max_set"), 1)

            @block.scalar
            def _(a):
                for g in range(G):
                    a.wait_ge(S("q_turned"), g + 1)
                    nc.scalar.activation(qta[:, g * F:(g + 1) * F], banks[g][0:DQ + 1, :], ACT.Copy).then_inc(S("q_turned_out"), 1)

        with ExitStack() as b:
            banks = [p.ps(b, f"turned_bank{j}", [P, 512]) for j in range(4)]
            sums = [p.ps(b, f"v_sum{j}", [P, 512]) for j in range(TG)]
            block = b.enter_context(nc.Block())
            steps = [(g, kb, max(0, kb - TG * g)) for g in range(G) for kb in range(TG * (g + 1))]

            @block.tensor
            def _(t):
                def scores(n):
                    g, kb, t0 = steps[n]
                    if n >= 4:
                        t.wait_ge(S("exp_done"), n - 3)
                    nc.tensor.matmul(banks[n % 4][:, t0 * P:F], kt[:, kb * P:(kb + 1) * P], qta[:, g * F + t0 * P:(g + 1) * F],
                                     start=True, stop=True).then_inc(S("turned_scored"), 1)

                scores(0)
                scores(1)
                for n, (g, kb, t0) in enumerate(steps):
                    if n + 2 < len(steps):
                        scores(n + 2)
                    t.wait_ge(S("exp_done"), n + 1)
                    if kb == 0 and g:
                        t.wait_ge(S("v_sums_out"), g)
                    for j in range(t0, TG):
                        ins = nc.tensor.matmul(sums[j][:, 0:D + 1], probs[:, n % 4, j * P:(j + 1) * P], val[:, kb, :],
                                               start=(kb == 0), stop=(kb == TG * g + j))
                    ins.then_inc(S("v_summed"), 1)

            @block.vector
            def _(v):
                for n, (g, kb, t0) in enumerate(steps):
                    if kb >= TG * g:
                        v.wait_ge(S("turned_scored"), n + 1)
                        d = slice(t0 * P, (t0 + 1) * P)
                        nc.vector.tensor_tensor(banks[n % 4][:, d], banks[n % 4][:, d], p.mask_st, ALU.add).then_inc(S("diagonal_masked"), 1)
                    if kb == TG * (g + 1) - 1:
                        v.wait_ge(S("v_summed"), n + 1)
                        for j in range(TG):
                            c = TG * g + j
                            nc.vector.tensor_copy(p.ao[:, c, :], sums[j][:, 0:D])
                            nc.vector.bn_stats(p.st[:, c, :], sums[j][:, 0:D])
                            ins = nc.vector.tensor_copy(den[:, c:c + 1], sums[j][:, D:D + 1])
                        ins.then_inc(S("v_sums_out"), 1)
                v.wait_ge(S("v_sums_out"), G)
                p.link(v, nc.vector.scalar_tensor_tensor(den[:], den[:], LN_EPS, den[:], ALU.mult, ALU.mult), "dve_step")
                p.stats_dve(v, 6, eps=den[:])
                p.residual(v)
                p.row_stats(v, p.x)

            @block.scalar
            def _(a):
                masked = 0
                for n, (g, kb, t0) in enumerate(steps):
                    if kb >= TG * g:
                        masked += 1
                        a.wait_ge(S("diagonal_masked"), masked)
                    else:
                        a.wait_ge(S("turned_scored"), n + 1)
                    if n >= 4:
                        a.wait_ge(S("v_summed"), n - 3)
                    nc.scalar.activation(probs[:, n % 4, t0 * P:F], banks[n % 4][:, t0 * P:F], ACT.Exp, scale=DQ ** -0.5).then_inc(S("exp_done"), 1)
                p.stats_act(a, 6)


def experts(p, out):
    nc, S, i = p.nc, p.sem, p.i
    with ExitStack() as s:
        x4 = p.sb(s, "x4", [P, NT, D])
        xht = p.sb(s, "xhat_turned", [P, T])
        acc = p.sb(s, "expert_sum", [P, NT, D])
        cent = p.sb(s, "centroids", [P, E])
        aff = p.sb(s, "affinity", [P, NT, E])
        gate = p.sb(s, "gate", [P, NT, E])
        hot = p.sb(s, "one_hot", [P, NT, E])
        top = p.sb(s, "top", [P, NT])
        rank = p.sb(s, "rank", [P, E])
        lng = p.sb(s, "ln_g", [P, 2, E])
        b2 = p.sb(s, "b2", [1, E, D])

        with ExitStack() as b:
            pt = p.ps(b, "e_xt_psum", [P, 2, 512])
            pa = p.ps(b, "aff_psum", [P, 2, 512])
            block = b.enter_context(nc.Block())

            @block.sync
            def _(sp):
                p.load(sp, "cent_in", cent[:], i["centT"])
                p.load(sp, "cent_in", rank[:], i["rank"])
                p.load(sp, "expert_vecs_in", lng[:, 0, :], i["ln_gT"])
                p.load(sp, "expert_vecs_in", lng[:, 1, :], i["ln_bT"])
                p.load(sp, "expert_vecs_in", b2[:], i["L1_ffn_b2"].unsqueeze(0))

            @block.gpsimd
            def _(g):
                nc.gpsimd.memset(acc[:], 0.0).then_inc(S("sum_cleared"), 1)

            @block.tensor
            def _(t):
                p.lead(t, "f_turned", "f_multiplied")
                t.wait_ge(S("cent_in"), 32)

                def body(c, k):
                    p.after(t, "f_normed", c)
                    p.after(t, "f_xt_out", c - 2)
                    nc.tensor.transpose(pt[:, k, 0:P], p.xn[:, k, :], p.ident).then_inc(S("f_turned"), 1)
                    p.after(t, "f_xt_out", c)
                    p.after(t, "f_aff_out", c - 2)
                    nc.tensor.matmul(pa[:, k, 0:E], p.xt[:, k, :], cent[:], start=True, stop=True).then_inc(S("f_multiplied"), 1)

                tile_pairs(t, body)

            @block.scalar
            def _(a):
                p.stats_act(a, 7)
                p.lead(a, "f_xt_out")

                def body(c, k):
                    p.after(a, "f_turned", c)
                    p.after(a, "f_multiplied", c - 2)
                    nc.scalar.activation(p.xt[:, k, :], pt[:, k, 0:P], ACT.Copy).then_inc(S("f_xt_out"), 1)

                tile_pairs(a, body)
                p.stats_act(a, 8)
                a.wait_ge(S("aff_negated"), 1)
                nc.scalar.activation(gate[:], gate[:], ACT.Exp, scale=-1.0).then_inc(S("gate_exp"), 1)

            @block.vector
            def _(v):
                step = lambda ins: p.link(v, ins, "dve_step")
                p.lead(v, "f_normed", "f_kept", "f_aff_out")
                p.stats_dve(v, 7)

                def normed(c, k):
                    p.after(v, "f_turned", c - 2)
                    p.normalise(p.x, p.xn[:, k, :], c).then_inc(S("f_normed"), 1)
                    p.after(v, "f_normed", c)
                    p.settled(v, "f_normed", k)
                    nc.vector.tensor_copy(tile(x4, c), p.xn[:, k, :]).then_inc(S("f_kept"), 1)

                normed(0, 0)
                normed(1, 1)

                def body(c, k):
                    if not (isinstance(c, int) and c >= NT - 2):
                        p.after(v, "f_kept", c)
                        normed(c + 2, k)
                    p.after(v, "f_multiplied", c)
                    p.settled(v, "f_multiplied", k)
                    nc.vector.tensor_copy(tile(aff, c), pa[:, k, 0:E]).then_inc(S("f_aff_out"), 1)

                tile_pairs(v, body)
                p.after(v, "f_kept", NT - 1)
                p.after(v, "f_aff_out", NT - 1)
                p.row_stats(v, x4)
                p.stats_dve(v, 8)
                nc.vector.tensor_scalar(gate[:], aff[:], -87.0, None, ALU.max).then_inc(S("aff_negated"), 1)
                step(nc.vector.tensor_reduce(top[:], aff[:], X, ALU.max))
                step(nc.vector.tensor_tensor(hot[:], aff[:], per_row(top[:], E), ALU.is_equal))
                v.wait_ge(S("cent_in"), 32)
                step(nc.vector.tensor_tensor(hot[:], hot[:], rank[:].unsqueeze(1).to_broadcast([P, NT, E]), ALU.mult))
                step(nc.vector.tensor_reduce(top[:], hot[:], X, ALU.max))
                step(nc.vector.tensor_tensor(hot[:], hot[:], per_row(top[:], E), ALU.is_equal))
                v.wait_ge(S("gate_exp"), 1)
                step(nc.vector.tensor_scalar(gate[:], gate[:], 1.0, None, ALU.add))
                step(nc.vector.reciprocal(gate[:], gate[:]))
                step(nc.vector.tensor_tensor(gate[:], gate[:], hot[:], ALU.mult))

        with ExitStack() as b:
            w1 = p.sb(b, "expert_w1", [P, 2, F])
            w2 = p.sb(b, "expert_w2", [P, 2, FB, D])
            b1 = p.sb(b, "expert_b1", [P, 2, FB])
            xe = p.sb(b, "expert_x", [P, 2, T])
            hid = p.sb(b, "expert_hidden", [P, 2, FB, F])
            pt = p.ps(b, "xhat_psum", [P, 512])
            pu = p.ps(b, "up_psum", [P, 4, F])
            pd = p.ps(b, "down_psum", [P, 2, TG, D])
            block = b.enter_context(nc.Block())


            @block.sync
            def _(sp):
                def body(e, k):
                    sp.wait_ge(S("g_down"), G * (e - 1) + 2 * G)
                    sp.dma_start(w1[:, k, :], i["ew1T"][bass.ds(e, 1), :, :].rearrange("a d f -> d (a f)")).then_inc(S(f"expert_w_in{k}"), 16)
                    sp.dma_start(w2[:, k, :, :], i["ew2T"][bass.ds(e, 1), :, :].rearrange("a (k p) d -> p (a k) d", p=P)).then_inc(S(f"expert_w_in{k}"), 16)
                    sp.dma_start(b1[:, k, :], i["b1T"][bass.ds(e, 1), :, :].rearrange("a p b -> p (a b)")).then_inc(S(f"expert_w_in{k}"), 16)

                tile_pairs(sp, body, E)

            @block.tensor
            def _(t):
                p.lead(t, "g_turned", "g_up")
                p.lead(t, "g_down", n=2 * G)

                def turn(c, k):
                    p.after(t, "g_xhat", c)
                    p.after(t, "g_xhat_out", c - 1)
                    nc.tensor.transpose(pt[:, 0:P], p.xn[:, k, :], p.ident).then_inc(S("g_turned"), 1)

                tile_pairs(t, turn)

                def up(e, k, g):
                    if g == 0:
                        t.wait_ge(S(f"expert_w_in{k}"), 24 * e + 48 - 24 * k)
                        p.after(t, "g_scaled", e)
                    for m in range(FB):
                        t.wait_ge(S("g_relu"), FB * (G * e + g) + m + 1)
                        nc.tensor.matmul(pu[:, m, :], w1[:, k, m * P:(m + 1) * P], xe[:, k, g * F:(g + 1) * F],
                                         start=True, stop=True).then_inc(S("g_up"), 1)

                def down(e, k, g):
                    n = G * e + g
                    t.wait_ge(S("g_relu"), FB * (n + 1) + FB)
                    t.wait_ge(S("g_added"), n - 1 + G)
                    for tb in range(TG):
                        for m in range(FB):
                            nc.tensor.matmul(pd[:, g % 2, tb, :], hid[:, g % 2, m, tb * P:(tb + 1) * P], w2[:, k, m, :],
                                             start=(m == 0), stop=False)
                        ins = nc.tensor.matmul(pd[:, g % 2, tb, :], p.ones[0:1, :],
                                               b2[0:1, bass.ds(e, 1), :].rearrange("a b d -> a (b d)"), start=False, stop=True)
                    ins.then_inc(S("g_down"), 1)

                up(0, 0, 0)

                def body(e, k):
                    for g in range(1, G):
                        up(e, k, g)
                        down(e, k, g - 1)
                    if not last(e, E):
                        up(e + 1, 1 - k, 0)
                    down(e, k, G - 1)

                tile_pairs(t, body, E)

            @block.scalar
            def _(a):
                p.lead(a, "g_xhat_out")
                p.lead(a, "g_relu", n=FB)

                def xt_out(c, k):
                    p.after(a, "g_turned", c)
                    p.settled(a, "g_turned", k)
                    nc.scalar.activation(xht[:, bass.ts(c, P)], pt[:, 0:P], ACT.Copy).then_inc(S("g_xhat_out"), 1)

                tile_pairs(a, xt_out)

                def body(e, k):
                    for g in range(G):
                        n = G * e + g
                        a.wait_ge(S("g_down"), n - 1 + 2 * G)
                        for m in range(FB):
                            a.wait_ge(S("g_up"), FB * n + m + 1 + LEAD)
                            nc.scalar.activation(hid[:, g % 2, m, :], pu[:, m, :], ACT.Relu,
                                                 bias=b1[:, k, m:m + 1]).then_inc(S("g_relu"), 1)

                tile_pairs(a, body, E)
                p.stats_act(a, 9)

            @block.vector
            def _(v):
                p.lead(v, "g_scaled", "g_xhat")
                p.lead(v, "g_added", n=G)

                def xhat(c, k):
                    p.after(v, "g_turned", c - 2)
                    p.normalise(x4, p.xn[:, k, :], c).then_inc(S("g_xhat"), 1)

                tile_pairs(v, xhat)
                v.wait_ge(S("expert_vecs_in"), 48)
                p.after(v, "g_xhat_out", NT - 1)

                def scaled(e, k):
                    v.wait_ge(S("g_down"), G * (e - 1) + 2 * G)
                    nc.vector.tensor_scalar(xe[:, k, :], xht[:], cell(lng[:, 0, :], e), cell(lng[:, 1, :], e),
                                            ALU.mult, ALU.add).then_inc(S("g_scaled"), 1)

                scaled(0, 0)

                def body(e, k):
                    if not last(e, E):
                        scaled(e + 1, 1 - k)
                    for g in range(G):
                        n = G * e + g
                        v.wait_ge(S("g_down"), n + 1 + 2 * G)
                        v.wait_ge(S("g_added"), n - 3 + G)
                        for tb in range(TG):
                            c = TG * g + tb
                            ins = nc.vector.scalar_tensor_tensor(acc[:, c, :], pd[:, g % 2, tb, :],
                                                                 gate[:, c, bass.ds(e, 1)], acc[:, c, :], ALU.mult, ALU.add)
                        ins.then_inc(S("g_added"), 1)

                v.wait_ge(S("sum_cleared"), 1)
                tile_pairs(v, body, E)
                v.wait_ge(S("g_added"), G * E + G)
                p.link(v, nc.vector.tensor_tensor(p.ao[:], x4[:], acc[:], ALU.add), "dve_step")
                p.row_stats(v, p.ao)
                p.stats_dve(v, 9)
                p.residual(v)

        block = s.enter_context(nc.Block())

        @block.sync
        def _(sp):
            p.load(sp, "out_written", out.rearrange("a (c p) d -> p (a c) d", p=P), p.x[:])
            sp.wait_ge(S("out_written"), 16)



_DIRECT = ["L0_attn_x", "L0_attn_W_in", "L0_attn_A_log", "L0_attn_dt_bias", "L0_attn_B_norm_bias",
           "L0_attn_C_norm_bias", "L0_attn_W_out", "L0_ffn_w3_s", "L1_attn_Wq", "L1_attn_Wk", "L1_attn_Wv", "L1_ffn_b2"]


def constants():
    import numpy as np

    j, m = np.arange(P)[:, None], np.arange(P)[None, :]
    consts = [j == m, j >= 0 * m, j == m + 1, (j == 0) & (m == P - 1)]
    consts = [np.broadcast_to(a, (P, P)).astype(np.float32) for a in consts]
    consts += [np.where(m > j, -1e30, 0.0).astype(np.float32), np.where(j > m, -1e30, 0.0).astype(np.float32)]
    blocks = range(1, LEV + 1)
    triangles = [((j >> k) == (m >> k)) & (j <= m) for k in blocks] + [((j >> k) == (m >> k)) & (j > m) for k in blocks]
    levels = [j == m] + [((j >> (k + 1)) == (m >> (k + 1))) & ((j >> k) % 2 == 0) & ((m >> k) % 2 == 1) for k in range(LEV)]
    stack = lambda masks: np.ascontiguousarray(np.stack(masks, axis=1).astype(np.float32))
    return {
        "consts": stack(consts),
        "triangles": stack(triangles),
        "level_masks": np.ascontiguousarray(np.repeat(stack(levels)[:, :, None, :], R, axis=2)),
        "rank": np.ascontiguousarray(np.broadcast_to(np.arange(E, 0, -1, dtype=np.float32), (P, E))),
    }


def kernel(**inputs):
    import numpy as np
    import concourse.bacc as _bacc
    from concourse import mybir as _mybir
    from concourse.bass_utils import run_bass_kernel_spmd as _run

    a = {n: np.asarray(v) for n, v in inputs.items()}
    arrays = {n: a[n] for n in _DIRECT}
    arrays["w1T"], arrays["w2T"] = a["L0_ffn_w1_w"].T, a["L0_ffn_w2_w"].T
    arrays["h1T"], arrays["h2T"], arrays["w3T"] = a["L0_ffn_h1_w"].T, a["L0_ffn_h2_w"].T, a["L0_ffn_w3_w"].T
    for n in ("w1_s", "w2_s", "h1_s", "h2_s"):
        arrays[n] = a["L0_ffn_" + n].reshape(FB, P).T
    arrays["centT"] = a["L1_ffn_centroids"].T
    arrays["ln_gT"], arrays["ln_bT"] = a["L1_ffn_ln_g"].T, a["L1_ffn_ln_b"].T
    arrays["b1T"] = a["L1_ffn_b1"].reshape(E, FB, P).transpose(0, 2, 1)
    arrays["ew1T"], arrays["ew2T"] = a["L1_ffn_w1"].transpose(0, 2, 1), a["L1_ffn_w2"].transpose(0, 2, 1)
    arrays.update(constants())
    arrays = {n: np.ascontiguousarray(v) for n, v in arrays.items()}

    nc = _bacc.Bacc("TRN2", target_bir_lowering=False, num_devices=1)
    drams = {n: nc.dram_tensor("in_" + n, v.shape, _mybir.dt.from_np(v.dtype), kind="ExternalInput").ap() for n, v in arrays.items()}
    out = nc.dram_tensor("out", a["L0_attn_x"].shape, _mybir.dt.float32, kind="ExternalOutput").ap()
    program(nc, drams, out)
    r = _run(nc, [{"in_" + n: v for n, v in arrays.items()}], core_ids=[0])
    return r.results[0]["out"]
```

```python
from contextlib import ExitStack

import concourse.bass as bass
from concourse import mybir

F32 = mybir.dt.float32
U32 = mybir.dt.uint32
I32 = mybir.dt.int32
ALU = mybir.AluOpType
ACT = mybir.ActivationFunctionType
X = mybir.AxisListType.X

P = 128
T = 2048
D = 128
NT = T // P
LEAD = 2

H, R, HD, N = 32, 2, 8, 64
DI = H * HD
ROT = N // 2
NBC = (R + 1) * N
REST = NBC + 2 * H + ROT
LEV = 7
SCALE = float(N * R) ** -0.5
F = 512
FB = F // P
G = T // F
TG = F // P
DQ = 64
E = 8
SL = NT + E
ROUTE = ((0, P), (P, P + E), (P + E, P + E + SL), (P + E + SL, P + E + SL + NT),
         (P + E + SL + NT, P + E + 2 * SL + NT))

LN_EPS = 1e-5
RMS_EPS = 1e-6
PI = 3.141592653589793
TWO_PI_HI = 6.28125
TWO_PI_LO = 2 * PI - TWO_PI_HI
ROUND = 12582912.0
PI_INSIDE = 3.1415925
DT_MIN, DT_MAX = 1e-4, 0.5
LOWEST = -3e38


def tile(t, c):
    return t[:, bass.ds(c, 1), :].rearrange("p a d -> p (a d)")


def cell(t, c):
    return t[:, bass.ds(c, 1)]


def per_row(t, width):
    return t.unsqueeze(2).to_broadcast([t.shape[0], t.shape[1], width])


def last(c, n=NT):
    return isinstance(c, int) and c == n - 1


def tile_pairs(eng, body, n=NT, first=0):
    for c in range(first):
        body(c, c % 2)
    with eng.Fori(first // 2, n // 2 - 1) as i:
        for k in range(2):
            body(2 * i + k, k)
    for k in range(2):
        body(n - 2 + k, k)


class Program:

    def __init__(self, nc, inputs, ctx):
        self.nc, self.i, self.ctx, self.sems, self.counts = nc, inputs, ctx, {}, {}

    def sb(self, stack, name, shape):
        return stack.enter_context(self.nc.sbuf_tensor(name, shape, F32))

    def ps(self, stack, name, shape):
        return stack.enter_context(self.nc.psum_tensor(name, shape, F32))

    def sem(self, name):
        if name not in self.sems:
            self.sems[name] = self.ctx.enter_context(self.nc.semaphore(name))
        return self.sems[name]

    def lead(self, eng, *names, n=LEAD):
        for name in names:
            eng.sem_inc(self.sem(name), n)

    def after(self, eng, name, c):
        eng.wait_ge(self.sem(name), c + 1 + LEAD)

    def settled(self, eng, name, c):
        eng.wait_ge(self.sem(name), c + 1 + LEAD)

    def link(self, eng, ins, name, n=1):
        self.counts[name] = self.counts.get(name, 0) + n
        ins.then_inc(self.sem(name), 1)
        eng.wait_ge(self.sem(name), self.counts[name])

    def load(self, eng, name, dst, src):
        eng.dma_start(dst, src).then_inc(self.sem(name), 16)


    def row_stats(self, v, rows):
        with v.Fori(0, NT // 4) as q:
            for j in range(4):
                ins = self.nc.vector.bn_stats(tile(self.st, 4 * q + j), tile(rows, 4 * q + j))
            ins.then_inc(self.sem("rows_read"), 1)
        self.counts["rows_read"] = self.counts.get("rows_read", 0) + NT // 4
        v.wait_ge(self.sem("rows_read"), self.counts["rows_read"])

    def stats_dve(self, v, n, eps=None):
        nc, st, tmp = self.nc, self.st, self.tmp
        step = lambda ins: self.link(v, ins, "dve_step")
        step(nc.vector.tensor_tensor(tmp[:, 0, :], st[:, :, 1], st[:, :, 4], ALU.add))
        step(nc.vector.tensor_scalar(self.mean[:], tmp[:, 0, :], 0.5, None, ALU.mult))
        step(nc.vector.tensor_tensor(tmp[:, 1, :], st[:, :, 1], st[:, :, 4], ALU.subtract))
        step(nc.vector.scalar_tensor_tensor(tmp[:, 2, :], tmp[:, 1, :], 0.25, tmp[:, 1, :], ALU.mult, ALU.mult))
        step(nc.vector.tensor_tensor(tmp[:, 0, :], st[:, :, 2], st[:, :, 5], ALU.add))
        step(nc.vector.scalar_tensor_tensor(tmp[:, 1, :], tmp[:, 0, :], 1.0 / D, tmp[:, 2, :], ALU.mult, ALU.add))
        if eps is None:
            nc.vector.tensor_scalar(tmp[:, 3, :], tmp[:, 1, :], LN_EPS, None, ALU.add).then_inc(self.sem("var_ready"), 1)
        else:
            nc.vector.tensor_tensor(tmp[:, 3, :], tmp[:, 1, :], eps, ALU.add).then_inc(self.sem("var_ready"), 1)
        v.wait_ge(self.sem("root_ready"), n)
        nc.vector.reciprocal(self.rstd[:], self.root[:]).then_inc(self.sem("rstd_ready"), 1)
        v.wait_ge(self.sem("rstd_ready"), n)

    def stats_act(self, a, n):
        a.wait_ge(self.sem("var_ready"), n)
        self.nc.scalar.activation(self.root[:], self.tmp[:, 3, :], ACT.Sqrt).then_inc(self.sem("root_ready"), 1)

    def residual(self, v):
        nc, ao, x = self.nc, self.ao, self.x
        step = lambda ins: self.link(v, ins, "dve_step")
        step(nc.vector.tensor_tensor(ao[:], ao[:], per_row(self.mean[:], D), ALU.subtract))
        step(nc.vector.tensor_tensor(ao[:], ao[:], per_row(self.rstd[:], D), ALU.mult))
        step(nc.vector.tensor_tensor(x[:], x[:], ao[:], ALU.add))

    def normalise(self, src, dst, c):
        return self.nc.vector.tensor_scalar(dst, tile(src, c), cell(self.mean, c), cell(self.rstd, c),
                                            ALU.subtract, ALU.mult)


def program(nc, inputs, out):
    with ExitStack() as ctx:
        p = Program(nc, inputs, ctx)
        p.x = p.sb(ctx, "x_res", [P, NT, D])
        p.ao = p.sb(ctx, "layer_out", [P, NT, D])
        p.const = p.sb(ctx, "consts", [P, 6, P])
        p.ident, p.ones, p.shift, p.corner, p.mask_ts, p.mask_st = (p.const[:, j, :] for j in range(6))
        p.st = p.sb(ctx, "row_stats", [P, NT, 6])
        p.mean = p.sb(ctx, "mean", [P, NT])
        p.root = p.sb(ctx, "root", [P, NT])
        p.rstd = p.sb(ctx, "rstd", [P, NT])
        p.tmp = p.sb(ctx, "stats_tmp", [P, 4, NT])
        p.xn = p.sb(ctx, "xn", [P, 2, D])
        p.xt = p.sb(ctx, "xt", [P, 2, P])
        p.bias = p.sb(ctx, "act_bias", [P, 2])
        with ExitStack() as m:
            p.xb = p.sb(m, "x_heads", [P, NT, R * DI])
            p.sz = p.sb(m, "silu_z", [P, NT, DI])
            p.bcr = p.sb(m, "bc_rotated", [P, NT, NBC])
            p.es = p.sb(m, "source_scale", [P, LEV + 2, NT, H])
            p.et = p.sb(m, "target_scale", [P, LEV, NT, H])
            p.cd = p.sb(m, "chunk_decay", [N, NT, H])
            p.gmask = p.sb(m, "level_mask", [P, LEV + 1, R, P])
            with ExitStack() as m1:
                p.rest = p.sb(m1, "proj_rest", [P, NT, REST])
                project(p)
                decays(p)
            with ExitStack() as m1:
                p.y = p.xb[:, :, 0:DI]
                scan(p)
                mixer_out(p)
        mlp(p)
        p.ew1 = p.sb(ctx, "expert_w1", [P, E, F])
        p.ew2 = p.sb(ctx, "expert_w2", [P, E * FB, D])
        p.route = p.sb(ctx, "route_consts", [P, ROUTE[-1][1]])
        p.clear = p.sb(ctx, "clear_slots", [P, SL, D + 1])
        p.slots = nc.dram_tensor("slots", (SL * P, D + 1), F32, kind="Internal").ap()
        p.routed = nc.dram_tensor("routed", (T + SL * P, D), F32, kind="Internal").ap()
        attention(p)
        experts(p, out)


def project(p):
    nc, i = p.nc, p.i
    with ExitStack() as s:
        w_in = p.sb(s, "w_in", [P, DI + R * DI + REST])
        pt = p.ps(s, "xt_psum", [P, 2, 512])
        px = p.ps(s, "x_psum", [P, 2, 512])
        pz = p.ps(s, "z_psum", [P, 2, 512])
        pr = p.ps(s, "rest_psum", [P, 2, 512])
        block = s.enter_context(nc.Block())

        @block.sync
        def _(sp):
            p.load(sp, "x_in", p.x[:], i["L0_attn_x"].rearrange("a (c p) d -> p (a c) d", p=P))
            p.load(sp, "const_in", p.const[:], i["consts"])
            p.load(sp, "w_in_in", w_in[:], i["L0_attn_W_in"])

        @block.vector
        def _(v):
            p.lead(v, "rest_out", "a_normed")
            v.wait_ge(p.sem("x_in"), 16)
            p.row_stats(v, p.x)
            p.stats_dve(v, 1)

            def normed(c, k):
                p.after(v, "a_turned", c - 2)
                p.normalise(p.x, p.xn[:, k, :], c).then_inc(p.sem("a_normed"), 1)

            normed(0, 0)
            normed(1, 1)

            def body(c, k):
                p.after(v, "projected", c)
                p.settled(v, "projected", k)
                nc.vector.tensor_copy(tile(p.rest, c), pr[:, k, 0:REST]).then_inc(p.sem("rest_out"), 1)
                if not (isinstance(c, int) and c >= NT - 2):
                    normed(c + 2, k)

            tile_pairs(v, body)

        @block.tensor
        def _(t):
            p.lead(t, "a_turned", "projected")

            def turn(c, k):
                p.after(t, "a_normed", c)
                p.after(t, "a_xt_out", c - 2)
                nc.tensor.transpose(pt[:, k, 0:P], p.xn[:, k, :], p.ident).then_inc(p.sem("a_turned"), 1)

            t.wait_ge(p.sem("const_in"), 16)
            turn(0, 0)
            t.wait_ge(p.sem("w_in_in"), 16)

            def body(c, k):
                if not last(c):
                    turn(c + 1, 1 - k)
                p.after(t, "a_xt_out", c)
                p.after(t, "silu_out", c - 2)
                p.after(t, "rest_out", c - 2)
                for bank, lo, hi in ((px, DI, DI + R * DI), (pz, 0, DI), (pr, DI + R * DI, DI + R * DI + REST)):
                    ins = nc.tensor.matmul(bank[:, k, 0:hi - lo], p.xt[:, k, :], w_in[:, lo:hi], start=True, stop=True)
                ins.then_inc(p.sem("projected"), 1)

            tile_pairs(t, body)

        @block.scalar
        def _(a):
            p.lead(a, "a_xt_out", "silu_out")
            p.stats_act(a, 1)

            def xt_out(c, k):
                p.after(a, "a_turned", c)
                p.after(a, "projected", c - 2)
                nc.scalar.activation(p.xt[:, k, :], pt[:, k, 0:P], ACT.Copy).then_inc(p.sem("a_xt_out"), 1)

            xt_out(0, 0)

            def body(c, k):
                if not last(c):
                    xt_out(c + 1, 1 - k)
                p.after(a, "projected", c)
                p.settled(a, "projected", k)
                nc.scalar.activation(tile(p.xb, c).rearrange("p (r h q) -> p h r q", r=R, q=HD),
                                     px[:, k, :].rearrange("p (h r q) -> p h r q", r=R, q=HD), ACT.Silu)
                nc.scalar.activation(tile(p.sz, c), pz[:, k, 0:DI], ACT.Silu).then_inc(p.sem("silu_out"), 1)

            tile_pairs(a, body)


def decays(p):
    nc, i = p.nc, p.i
    rest = p.rest
    bc = rest[:, :, 0:NBC]
    dt_raw, lam_raw = rest[:, :, NBC:NBC + H], rest[:, :, NBC + H:NBC + 2 * H]
    theta = rest[:, :, NBC + 2 * H:REST]
    S = p.sem
    with ExitStack() as s:
        tri = p.sb(s, "triangles", [P, 2 * LEV, P])
        vecs = p.sb(s, "head_vecs", [P, 2, H])
        nbias = p.sb(s, "norm_bias", [P, R + 1, N])
        rms = p.sb(s, "rms", [P, NT * (R + 1)])
        m = p.sb(s, "dt_sum", [P, NT])
        names = ["u", "dt", "la", "lam", "v", "w", "mt", "cos", "sin", "turns", "angle"]
        small = {n: p.sb(s, "d_" + n, [P, NT, H]) for n in names}
        u, dt, la, lam, vv, w, mt, cos, sin, turns, angle = (small[n][:] for n in names)
        sq = p.sb(s, "squares", [P, NT, NBC])
        rot = p.sb(s, "rotation", [P, NT, R + 1, ROT])
        banks = [p.ps(s, f"exp_psum{j}", [P, 512]) for j in range(6)]
        p_ang = p.ps(s, "angle_psum", [P, 512])
        p_next = p.ps(s, "next_psum", [P, 512])
        flat = lambda ap: ap.rearrange("p c h -> p (c h)")
        block = s.enter_context(nc.Block())

        @block.sync
        def _(sp):
            p.load(sp, "tri_in", tri[:], i["triangles"])
            p.load(sp, "tri_in", p.gmask[:], i["level_masks"])
            p.load(sp, "vecs_in", vecs[:, 0, :], i["L0_attn_dt_bias"].unsqueeze(0).to_broadcast([P, H]))
            p.load(sp, "vecs_in", vecs[:, 1, :], i["L0_attn_A_log"].unsqueeze(0).to_broadcast([P, H]))
            for r, name in enumerate(["B", "B", "C"]):
                p.load(sp, "nbias_in", nbias[:, r, :], i[f"L0_attn_{name}_norm_bias"].to_broadcast([P, N]))

        sums = [(p.et[:, l, :, :], tri[:, l, :]) for l in range(LEV)]
        sums += [(p.es[:, l + 1, :, :], p.shift if l == 0 else tri[:, LEV + l - 1, :]) for l in range(LEV + 1)]
        sums += [(p.cd[:], p.ones[:, 0:N])]

        @block.vector
        def _(v):
            step = lambda ins: p.link(v, ins, "dve_step")
            step(nc.vector.memset(p.bias[:, 0:1], 1.0))
            nc.vector.memset(p.bias[:, 1:2], RMS_EPS).then_inc(S("bias_set"), 1)
            v.wait_ge(S("vecs_in"), 32)
            step(nc.vector.tensor_tensor(u, dt_raw, vecs[:, 0:1, :].to_broadcast([P, NT, H]), ALU.add))
            nc.vector.tensor_scalar(u, u, 20.0, None, ALU.min).then_inc(S("dt_arg"), 1)
            nc.vector.tensor_scalar(lam, lam_raw, -87.0, None, ALU.max).then_inc(S("lam_arg"), 1)
            v.wait_ge(S("softplus_out"), 1)
            step(nc.vector.tensor_scalar(dt, dt, DT_MIN, DT_MAX, ALU.max, ALU.min))
            nc.vector.scalar_tensor_tensor(la, dt, -1.0, vecs[:, 1:2, :].to_broadcast([P, NT, H]), ALU.mult, ALU.mult).then_inc(S("la_ready"), 1)
            step(nc.vector.tensor_reduce(m[:], dt, X, ALU.add))
            nc.vector.scalar_tensor_tensor(mt, theta, -1.0 / H, per_row(m[:], ROT), ALU.mult, ALU.mult).then_inc(S("turns_ready"), 1)
            v.wait_ge(S("lam_exp"), 1)
            step(nc.vector.tensor_scalar(lam, lam, 1.0, None, ALU.add))
            step(nc.vector.reciprocal(lam, lam))
            step(nc.vector.tensor_tensor(p.es[:, 0, :, :], lam, dt, ALU.mult))
            nc.vector.tensor_tensor(vv, dt, p.es[:, 0, :, :], ALU.subtract).then_inc(S("v_ready"), 1)
            v.wait_ge(S("squared"), 1)
            nc.vector.tensor_reduce(rms[:], sq[:].rearrange("p c (r n) -> p (c r) n", n=N), X, ALU.add).then_inc(S("ms_ready"), 1)
            v.wait_ge(S("angle_summed"), 1)
            step(nc.vector.tensor_scalar(flat(turns), p_ang[:], 1.0 / (2 * PI), ROUND, ALU.mult, ALU.add))
            step(nc.vector.tensor_scalar(turns, turns, ROUND, None, ALU.subtract))
            step(nc.vector.scalar_tensor_tensor(flat(angle), flat(turns), -TWO_PI_HI, p_ang[:], ALU.mult, ALU.add))
            step(nc.vector.scalar_tensor_tensor(angle, turns, -TWO_PI_LO, angle, ALU.mult, ALU.add))
            step(nc.vector.tensor_scalar(angle, angle, PI_INSIDE, -PI_INSIDE, ALU.min, ALU.max))
            step(nc.vector.scalar_tensor_tensor(turns, angle, -1.0, angle, ALU.mult, ALU.min))
            nc.vector.tensor_scalar(turns, turns, PI / 2, None, ALU.add).then_inc(S("angle_ready"), 1)
            v.wait_ge(S("rms_root"), 1)
            step(nc.vector.reciprocal(rms[:], rms[:]))
            c_rms = rms[:].rearrange("p (c r) -> p c r", r=R + 1)[:, :, R]
            nc.vector.tensor_scalar(c_rms, c_rms, SCALE, None, ALU.mult).then_inc(S("rms_ready"), 1)
            v.wait_ge(S("next_summed"), 1)
            step(nc.vector.tensor_tensor(flat(w), p_next[:], flat(p.es[:, 0, :, :]), ALU.add))
            for n, (dst, _) in enumerate(sums):
                if LEV <= n < 2 * LEV + 1:
                    v.wait_ge(S("exp_out"), n + 1)
                    step(nc.vector.tensor_tensor(dst, dst, w, ALU.mult))
            v.wait_ge(S("trig_out"), 1)
            v.wait_ge(S("bc_normed"), 1)
            halves = bc.rearrange("p c (r f n) -> p c r f n", r=R + 1, f=2)
            out = p.bcr[:].rearrange("p c (r f n) -> p c r f n", r=R + 1, f=2)
            for r in range(R + 1):
                nc.vector.tensor_tensor(out[:, :, r, 0, :], halves[:, :, r, 0, :], cos, ALU.mult)
                step(nc.vector.tensor_tensor(rot[:, :, r, :], halves[:, :, r, 1, :], sin, ALU.mult))
            nc.vector.tensor_tensor(out[:, :, :, 0, :], out[:, :, :, 0, :], rot[:], ALU.subtract).then_inc(S("rotated"), 1)

        @block.gpsimd
        def _(g):
            step = lambda ins: p.link(g, ins, "pool_step")
            g.wait_ge(S("rms_ready"), 1)
            g.wait_ge(S("nbias_in"), 48)
            groups = bc.rearrange("p c (r n) -> p c r n", n=N)
            for r in range(R + 1):
                step(nc.gpsimd.tensor_tensor(groups[:, :, r, :], groups[:, :, r, :],
                                             per_row(rms[:].rearrange("p (c r) -> p c r", r=R + 1)[:, :, r], N), ALU.mult))
            for r in range(R + 1):
                ins = nc.gpsimd.tensor_tensor(groups[:, :, r, :], groups[:, :, r, :],
                                              nbias[:, r:r + 1, :].to_broadcast([P, NT, N]), ALU.mult)
                ins.then_inc(S("bc_normed" if r == R else "bc_biased"), 1)
            g.wait_ge(S("bc_biased"), R)
            g.wait_ge(S("bc_normed"), 1)
            g.wait_ge(S("trig_out"), 1)
            halves = bc.rearrange("p c (r f n) -> p c r f n", r=R + 1, f=2)
            out = p.bcr[:].rearrange("p c (r f n) -> p c r f n", r=R + 1, f=2)
            prod = sq[:].rearrange("p c (f r n) -> p c f r n", f=2, r=R + 1)
            for r in range(R + 1):
                step(nc.gpsimd.tensor_tensor(prod[:, :, 0, r, :], halves[:, :, r, 0, :], sin, ALU.mult))
                step(nc.gpsimd.tensor_tensor(prod[:, :, 1, r, :], halves[:, :, r, 1, :], cos, ALU.mult))
                step(nc.gpsimd.tensor_tensor(out[:, :, r, 1, :], prod[:, :, 0, r, :], prod[:, :, 1, r, :], ALU.add))

        @block.scalar
        def _(a):
            step = lambda ins: p.link(a, ins, "act_step")
            a.wait_ge(S("vecs_in"), 32)
            step(nc.scalar.activation(vecs[:, 1, :], vecs[:, 1, :], ACT.Exp))
            a.wait_ge(S("dt_arg"), 1)
            a.wait_ge(S("bias_set"), 1)
            step(nc.scalar.activation(u, u, ACT.Exp))
            nc.scalar.activation(dt, u, ACT.Ln, bias=p.bias[:, 0:1]).then_inc(S("softplus_out"), 1)
            a.wait_ge(S("lam_arg"), 1)
            nc.scalar.activation(lam, lam, ACT.Exp, scale=-1.0).then_inc(S("lam_exp"), 1)
            nc.scalar.activation(sq[:], bc, ACT.Square).then_inc(S("squared"), 1)
            for n, (dst, _) in enumerate(sums):
                rows = N if n == 2 * LEV + 1 else P
                a.wait_ge(S("exp_summed"), n + 1)
                nc.scalar.activation(flat(dst), banks[n % 6][0:rows, :], ACT.Exp).then_inc(S("exp_out"), 1)
            a.wait_ge(S("ms_ready"), 1)
            nc.scalar.activation(rms[:], rms[:], ACT.Sqrt, scale=1.0 / N, bias=p.bias[:, 1:2]).then_inc(S("rms_root"), 1)
            a.wait_ge(S("angle_ready"), 1)
            step(nc.scalar.activation(sin, angle, ACT.Sin))
            nc.scalar.activation(cos, turns, ACT.Sin).then_inc(S("trig_out"), 1)

        @block.tensor
        def _(t):
            t.wait_ge(S("tri_in"), 32)
            t.wait_ge(S("turns_ready"), 1)
            nc.tensor.matmul(p_ang[:], tri[:, LEV - 1, :], flat(mt), start=True, stop=False)
            for c in range(NT - 1):
                n = NT - 1 - c
                ins = nc.tensor.matmul(p_ang[:, (c + 1) * ROT:].rearrange("p (c h) -> p c h", c=n), p.ones,
                                       mt[:, c:c + 1, :].to_broadcast([P, n, ROT]), start=False, stop=(c == NT - 2))
            ins.then_inc(S("angle_summed"), 1)
            t.wait_ge(S("v_ready"), 1)
            nc.tensor.matmul(p_next[:], p.shift, flat(vv), start=True, stop=False)
            nc.tensor.matmul(p_next[:, 0:(NT - 1) * H], p.corner, flat(vv)[:, H:], start=False, stop=True).then_inc(S("next_summed"), 1)
            t.wait_ge(S("la_ready"), 1)
            for n, (dst, lhs) in enumerate(sums):
                if n >= 6:
                    t.wait_ge(S("exp_out"), n - 5)
                rows = N if n == 2 * LEV + 1 else P
                nc.tensor.matmul(banks[n % 6][0:rows, :], lhs, flat(la), start=True, stop=True).then_inc(S("exp_summed"), 1)


BY_DVE = 5


def scan(p):
    nc = p.nc
    S = p.sem
    with ExitStack() as s:
        bcs = p.sb(s, "bc_tile", [P, 2, NBC])
        bct = p.sb(s, "bc_turned", [N, 2, R + 1, P])
        gm = p.sb(s, "scores", [P, 2, LEV + 1, R, P])
        xs = p.sb(s, "x_scaled", [P, 2, LEV + 2, R * DI])
        state = p.sb(s, "state", [N, 2, DI])
        decayed = p.sb(s, "state_decayed", [N, 2, DI])
        tm = p.sb(s, "terms", [P, 2, LEV, DI])
        pt = p.ps(s, "bct_psum", [P, 512])
        pg = p.ps(s, "score_psum", [P, 512])
        p_st = p.ps(s, "state_psum", [P, 512])
        p_terms = p.ps(s, "terms_psum", [P, LEV + 1, DI])
        block = s.enter_context(nc.Block())

        def scale(engine, c, k, level):
            heads = lambda ap: ap.rearrange("p (r h q) -> p r h q", r=R, q=HD)
            e = tile(p.es[:, level, :, :], c).unsqueeze(1).unsqueeze(3).to_broadcast([P, R, H, HD])
            return engine.tensor_tensor(heads(xs[:, k, level, :]), heads(tile(p.xb, c)), e, ALU.mult)

        @block.scalar
        def _(a):
            p.lead(a, "b_tile_in", "b_turned_out")

            def turned(c, k):
                p.after(a, "b_state_summed", c - 2)
                p.settled(a, "b_state_summed", k - 2)
                nc.scalar.activation(bcs[:, k, :], tile(p.bcr, c), ACT.Copy).then_inc(S("b_tile_in"), 1)
                p.after(a, "b_turned", c)
                p.after(a, "b_terms", c - 2)
                nc.scalar.activation(bct[:, k, :, :], pt[0:N, 0:(R + 1) * P].rearrange("p (r n) -> p r n", n=P),
                                     ACT.Copy).then_inc(S("b_turned_out"), 1)

            turned(0, 0)

            def body(c, k):
                if not last(c):
                    turned(c + 1, 1 - k)

            tile_pairs(a, body)

        @block.tensor
        def _(t):
            p.lead(t, "b_turned", "b_scores", "b_terms", "b_state_summed")

            def turn_waits(c):
                p.after(t, "b_tile_in", c)
                p.after(t, "b_turned_out", c - 1)

            def turn(k):
                for r in range(R + 1):
                    ins = nc.tensor.transpose(pt[0:N, r * P:(r + 1) * P], bcs[:, k, r * N:(r + 1) * N], p.ident)
                ins.then_inc(S("b_turned"), 1)

            def scores(c, k):
                p.after(t, "b_turned_out", c)
                p.after(t, "b_masked", c - 1)
                for r in range(R):
                    ins = nc.tensor.matmul(pg[:, r * P:(r + 1) * P], bct[:, k, r, :], bct[:, k, R, :], start=True, stop=True)
                ins.then_inc(S("b_scores"), 1)

            turn_waits(0)
            turn(0)
            scores(0, 0)

            def body(c, k):
                if not last(c):
                    turn_waits(c + 1)
                p.after(t, "b_scaled_dve", c)
                p.after(t, "b_scaled_pool", c)
                p.after(t, "b_state", c)
                for r in range(R):
                    ins = nc.tensor.matmul(p_st[0:N, 0:DI], bcs[:, k, r * N:(r + 1) * N],
                                           xs[:, k, LEV + 1, r * DI:(r + 1) * DI], start=(r == 0), stop=(r == R - 1))
                    if r == 0 and not last(c):
                        turn(1 - k)
                ins.then_inc(S("b_state_summed"), 1)
                if not last(c):
                    scores(c + 1, 1 - k)
                p.after(t, "b_masked", c)
                p.after(t, "b_terms_out", c - 1)
                for l in range(LEV):
                    parts = [(j, r) for j in ((0, 1) if l == 0 else (l + 1,)) for r in range(R)]
                    for n, (j, r) in enumerate(parts):
                        nc.tensor.matmul(p_terms[:, l, :], gm[:, k, j, r, :], xs[:, k, j, r * DI:(r + 1) * DI],
                                         start=(n == 0), stop=(n == len(parts) - 1))
                nc.tensor.matmul(p_terms[:, LEV, :], bct[:, k, R, :], state[:, k, :], start=True, stop=True).then_inc(S("b_terms"), 1)

            tile_pairs(t, body)

        @block.vector
        def _(v):
            p.lead(v, "b_masked", "b_scaled_dve", "b_decayed", "b_state", "b_terms_scaled", "b_terms_out", "b_gated")
            nc.vector.memset(state[:, 0, :], 0.0).then_inc(S("b_state"), 1)

            def sources(c, k):
                p.after(v, "b_scores", c)
                p.after(v, "b_terms", c - 2)
                nc.vector.tensor_tensor(gm[:, k, :, :, :].rearrange("p l r m -> p l (r m)"),
                                        pg[:, 0:R * P].unsqueeze(1).to_broadcast([P, LEV + 1, R * P]),
                                        p.gmask[:].rearrange("p l r m -> p l (r m)"), ALU.mult).then_inc(S("b_masked"), 1)
                for level in range(BY_DVE):
                    ins = scale(nc.vector, c, k, LEV + 1 - level)
                ins.then_inc(S("b_scaled_dve"), 1)

            def gate(c, k):
                p.after(v, "b_y", c)
                nc.vector.tensor_tensor(tile(p.y, c), tm[:, k, 0, :], tile(p.sz, c), ALU.mult).then_inc(S("b_gated"), 1)

            sources(0, 0)

            def body(c, k):
                if not last(c):
                    sources(c + 1, 1 - k)
                    p.after(v, "b_state", c)
                    nc.vector.tensor_tensor(decayed[:, k, :].rearrange("p (h q) -> p h q", q=HD),
                                            state[:, k, :].rearrange("p (h q) -> p h q", q=HD),
                                            per_row(tile(p.cd, c), HD), ALU.mult).then_inc(S("b_decayed"), 1)
                    p.after(v, "b_decayed", c)
                    p.after(v, "b_state_summed", c)
                    p.after(v, "b_terms", c - 1)
                    nc.vector.tensor_tensor(state[:, 1 - k, :], decayed[:, k, :], p_st[0:N, 0:DI], ALU.add).then_inc(S("b_state"), 1)
                if not (isinstance(c, int) and c == 0):
                    gate(c - 1, 1 - k)
                p.after(v, "b_terms", c)
                p.after(v, "b_gated", c - 2)
                e = p.et[:, :, bass.ds(c, 1), :].rearrange("p l c h -> p l (c h)").unsqueeze(3).to_broadcast([P, LEV, H, HD])
                nc.vector.tensor_tensor(tm[:, k, :, :].rearrange("p l (h q) -> p l h q", q=HD),
                                        p_terms[:, 1:LEV + 1, :].rearrange("p l (h q) -> p l h q", q=HD),
                                        e, ALU.mult).then_inc(S("b_terms_scaled"), 1)
                p.after(v, "b_terms_scaled", c)
                nc.vector.tensor_tensor(tm[:, k, 0, :], p_terms[:, 0, :], tm[:, k, 0, :], ALU.add).then_inc(S("b_terms_out"), 1)

            tile_pairs(v, body, first=2)
            gate(NT - 1, 1)

        @block.gpsimd
        def _(g):
            p.lead(g, "b_scaled_pool", "b_half", "b_quarter", "b_y")

            def sources(c, k):
                p.after(g, "b_terms", c - 2)
                p.settled(g, "b_terms", k - 2)
                for level in range(LEV + 2 - BY_DVE):
                    ins = scale(nc.gpsimd, c, k, level)
                ins.then_inc(S("b_scaled_pool"), 1)

            sources(0, 0)

            def body(c, k):
                if not last(c):
                    sources(c + 1, 1 - k)
                p.after(g, "b_terms_out", c)
                nc.gpsimd.tensor_tensor(tm[:, k, 0:3, :], tm[:, k, 0:3, :], tm[:, k, 4:7, :], ALU.add).then_inc(S("b_half"), 1)
                p.after(g, "b_half", c)
                nc.gpsimd.tensor_tensor(tm[:, k, 0:2, :], tm[:, k, 0:2, :], tm[:, k, 2:4, :], ALU.add).then_inc(S("b_quarter"), 1)
                p.after(g, "b_quarter", c)
                nc.gpsimd.tensor_tensor(tm[:, k, 0, :], tm[:, k, 0, :], tm[:, k, 1, :], ALU.add).then_inc(S("b_y"), 1)

            tile_pairs(g, body)


def mixer_out(p):
    nc, S = p.nc, p.sem
    with ExitStack() as s:
        wo = p.sb(s, "w_out", [P, 2, D])
        ys = p.sb(s, "y_gated", [P, 2, DI])
        sq = p.sb(s, "y_squares", [P, DI])
        yt = p.sb(s, "y_turned", [P, 2, DI])
        ss = p.sb(s, "y_square_sum", [P, NT])
        pt = p.ps(s, "yt_psum", [P, 2, 512])
        po = p.ps(s, "out_psum", [P, 2, 512])
        block = s.enter_context(nc.Block())

        @block.sync
        def _(sp):
            p.load(sp, "w_out_in", wo[:], p.i["L0_attn_W_out"].rearrange("(j p) d -> p j d", p=P))

        @block.tensor
        def _(t):
            p.lead(t, "c_turned", "c_multiplied")

            def turn(c, k):
                p.after(t, "c_gated", c)
                p.after(t, "c_turned_out", c - 2)
                for j in range(2):
                    ins = nc.tensor.transpose(pt[:, k, j * P:(j + 1) * P], ys[:, k, j * P:(j + 1) * P], p.ident)
                ins.then_inc(S("c_turned"), 1)

            turn(0, 0)
            t.wait_ge(S("w_out_in"), 16)

            def body(c, k):
                if not last(c):
                    turn(c + 1, 1 - k)
                p.after(t, "c_turned_out", c)
                p.after(t, "c_out", c - 2)
                for j in range(2):
                    ins = nc.tensor.matmul(po[:, k, 0:D], yt[:, k, j * P:(j + 1) * P], wo[:, j, :], start=(j == 0), stop=(j == 1))
                ins.then_inc(S("c_multiplied"), 1)

            tile_pairs(t, body)

        @block.scalar
        def _(a):
            p.lead(a, "c_gated", "c_squared", "c_turned_out")

            def body(c, k):
                p.after(a, "c_turned", c - 2)
                nc.scalar.activation(ys[:, k, :], tile(p.y, c), ACT.Copy).then_inc(S("c_gated"), 1)
                p.after(a, "c_squared", c - 1)
                nc.scalar.activation(sq[:], tile(p.y, c), ACT.Square, accum_out=cell(ss, c)).then_inc(S("c_squared"), 1)
                p.after(a, "c_turned", c)
                p.after(a, "c_multiplied", c - 2)
                nc.scalar.activation(yt[:, k, :], pt[:, k, 0:DI], ACT.Copy).then_inc(S("c_turned_out"), 1)

            tile_pairs(a, body)
            p.stats_act(a, 2)

        @block.vector
        def _(v):
            p.lead(v, "c_out")

            def body(c, k):
                p.after(v, "c_multiplied", c)
                p.settled(v, "c_multiplied", k)
                nc.vector.tensor_copy(tile(p.ao, c), po[:, k, 0:D])
                nc.vector.bn_stats(tile(p.st, c), po[:, k, 0:D]).then_inc(S("c_out"), 1)

            tile_pairs(v, body)
            p.after(v, "c_squared", NT - 1)
            p.after(v, "c_out", NT - 1)
            p.link(v, nc.vector.tensor_scalar(ss[:], ss[:], LN_EPS / DI, LN_EPS * RMS_EPS, ALU.mult, ALU.add), "dve_step")
            p.stats_dve(v, 2, eps=ss[:])
            p.residual(v)
            p.row_stats(v, p.x)


def mlp(p):
    nc, S, i = p.nc, p.sem, p.i
    with ExitStack() as s:
        w12 = p.sb(s, "w12", [P, 2, F])
        h12 = p.sb(s, "h12", [P, 2, FB, F])
        w3 = p.sb(s, "w3", [P, FB, D])
        scales = p.sb(s, "hidden_scales", [P, 4, FB])
        s3 = p.sb(s, "w3_scale", [P, D])
        xn4 = p.sb(s, "mlp_xn", [P, TG, D])
        xt4 = p.sb(s, "mlp_xt", [P, F])
        ts = p.sb(s, "silu_part", [P, 2, F])
        h = [p.sb(s, f"hidden{j}", [P, FB, F]) for j in range(3)]
        pt = p.ps(s, "mlp_xt_psum", [P, F])
        pa = p.ps(s, "w1_psum", [P, 2, F])
        pb = p.ps(s, "w2_psum", [P, 2, F])
        ph = p.ps(s, "hidden_psum", [P, 2, F])
        po = p.ps(s, "mlp_out_psum", [P, TG, D])
        block = s.enter_context(nc.Block())

        @block.sync
        def _(sp):
            p.load(sp, "w12_in", w12[:, 0, :], i["w1T"])
            p.load(sp, "w12_in", w12[:, 1, :], i["w2T"])
            for j, name in enumerate(["w1_s", "w2_s", "h1_s", "h2_s"]):
                p.load(sp, "scales_in", scales[:, j, :], i[name])
            p.load(sp, "scales_in", s3[:], i["L0_ffn_w3_s"].unsqueeze(0).to_broadcast([P, D]))
            for j in range(2):
                p.load(sp, "h12_in", h12[:, j, :, :], i[f"h{j + 1}T"].rearrange("(k p) o -> p k o", p=P))
            p.load(sp, "h12_in", w3[:], i["w3T"].rearrange("(k p) o -> p k o", p=P))

        def hidden(n, g, m):
            return FB * g + m + 1 + LEAD

        @block.tensor
        def _(t):
            p.lead(t, "d_turned", "d_up", "d_hidden", "d_down")
            t.wait_ge(S("w12_in"), 32)
            t.wait_ge(S("h12_in"), 48)
            with t.Fori(0, G) as g:
                t.wait_ge(S("d_normed"), g + 1)
                t.wait_ge(S("d_xt_out"), g + LEAD)
                for j in range(TG):
                    ins = nc.tensor.transpose(pt[:, j * P:(j + 1) * P], xn4[:, j, :], p.ident)
                ins.then_inc(S("d_turned"), 1)
                t.wait_ge(S("d_xt_out"), g + 1 + LEAD)
                for m in range(FB):
                    t.wait_ge(S("d_gated"), hidden(0, g, m - 2))
                    nc.tensor.matmul(pa[:, m % 2, :], w12[:, 0, m * P:(m + 1) * P], xt4[:], start=True, stop=True)
                    nc.tensor.matmul(pb[:, m % 2, :], w12[:, 1, m * P:(m + 1) * P], xt4[:], start=True, stop=True).then_inc(S("d_up"), 1)
                t.wait_ge(S("d_gated"), hidden(0, g, FB - 1))
                for l in range(2):
                    for m in range(FB):
                        n = FB * l + m
                        t.wait_ge(S("d_gelu"), 2 * FB * g + n - 1 + LEAD)
                        for kk in range(FB):
                            ins = nc.tensor.matmul(ph[:, m % 2, :], h12[:, l, kk, m * P:(m + 1) * P], h[l][:, kk, :],
                                                   start=(kk == 0), stop=(kk == FB - 1))
                        ins.then_inc(S("d_hidden"), 1)
                    t.wait_ge(S("d_gelu"), 2 * FB * g + FB * (l + 1) + LEAD)
                t.wait_ge(S("d_out"), g + LEAD)
                for j in range(TG):
                    for kk in range(FB):
                        ins = nc.tensor.matmul(po[:, j, :], h[2][:, kk, j * P:(j + 1) * P], w3[:, kk, :],
                                               start=(kk == 0), stop=(kk == FB - 1))
                ins.then_inc(S("d_down"), 1)

        @block.scalar
        def _(a):
            p.stats_act(a, 3)
            p.lead(a, "d_xt_out", "d_silu", "d_gelu")
            a.wait_ge(S("scales_in"), 80)
            with a.Fori(0, G) as g:
                a.wait_ge(S("d_turned"), g + 1 + LEAD)
                a.wait_ge(S("d_up"), hidden(0, g, -1))
                nc.scalar.activation(xt4[:], pt[:], ACT.Copy).then_inc(S("d_xt_out"), 1)
                for m in range(FB):
                    a.wait_ge(S("d_up"), hidden(0, g, m))
                    a.wait_ge(S("d_gated"), hidden(0, g, m - 2))
                    nc.scalar.activation(ts[:, m % 2, :], pa[:, m % 2, :], ACT.Silu, scale=scales[:, 0, m:m + 1]).then_inc(S("d_silu"), 1)
                for l in range(2):
                    for m in range(FB):
                        a.wait_ge(S("d_hidden"), 2 * FB * g + FB * l + m + 1 + LEAD)
                        if l == 1 and m == 0:
                            a.wait_ge(S("d_down"), g + LEAD)
                        nc.scalar.activation(h[l + 1][:, m, :], ph[:, m % 2, :], ACT.Gelu, scale=scales[:, 2 + l, m:m + 1]).then_inc(S("d_gelu"), 1)
            p.stats_act(a, 4)

        @block.vector
        def _(v):
            p.lead(v, "d_gated", "d_out")
            p.stats_dve(v, 3)
            v.wait_ge(S("scales_in"), 80)
            with v.Fori(0, G) as g:
                v.wait_ge(S("d_turned"), g + LEAD)
                for j in range(TG):
                    ins = p.normalise(p.x, xn4[:, j, :], TG * g + j)
                ins.then_inc(S("d_normed"), 1)
                for m in range(FB):
                    v.wait_ge(S("d_silu"), hidden(0, g, m))
                    nc.vector.scalar_tensor_tensor(h[0][:, m, :], pb[:, m % 2, :], scales[:, 1, m:m + 1], ts[:, m % 2, :],
                                                   ALU.mult, ALU.mult).then_inc(S("d_gated"), 1)
                v.wait_ge(S("d_down"), g + 1 + LEAD)
                nc.vector.tensor_tensor(p.ao[:, bass.ds(TG * g, TG), :], po[:], s3[:].unsqueeze(1).to_broadcast([P, TG, D]),
                                        ALU.mult).then_inc(S("d_out"), 1)
            v.wait_ge(S("d_out"), G + LEAD)
            p.row_stats(v, p.ao)
            p.stats_dve(v, 4)
            p.residual(v)
            p.row_stats(v, p.x)


def attention(p):
    nc, S, i = p.nc, p.sem, p.i
    QV = D + DQ
    with ExitStack() as s:
        wk = p.sb(s, "w_q_k", [P, 2, DQ])
        wvq = p.sb(s, "w_v_q", [P, QV])
        qt = p.sb(s, "q_turned", [DQ, T])
        kt = p.sb(s, "k_turned", [DQ + 1, T])
        q = p.sb(s, "q_rows", [P, NT, DQ + 1])
        val = p.sb(s, "v_rows", [P, NT, D + 1])
        qta = p.sb(s, "q_max_turned", [DQ + 1, T])
        part = p.sb(s, "part_max", [P, NT, G])
        mx = p.sb(s, "row_max", [P, NT])
        probs = p.sb(s, "probs", [P, 4, F])
        den = p.sb(s, "denominator", [P, NT])

        with ExitStack() as b:
            pt = p.ps(b, "att_xt_psum", [P, 2, 512])
            pqk = p.ps(b, "qk_psum", [P, 2, 512])
            pvq = p.ps(b, "vq_psum", [P, 2, 512])
            block = b.enter_context(nc.Block())

            @block.sync
            def _(sp):
                p.load(sp, "att_in", wk[:, 0, :], i["L1_attn_Wq"])
                p.load(sp, "att_in", wk[:, 1, :], i["L1_attn_Wk"])
                p.load(sp, "att_in", wvq[:, 0:D], i["L1_attn_Wv"])
                p.load(sp, "att_in", wvq[:, D:QV], i["L1_attn_Wq"])
                p.load(sp, "route_in", p.route[:], i["route"])
                p.load(sp, "experts_in", p.ew1[:], i["ew1T"])
                p.load(sp, "experts_in", p.ew2[:], i["ew2T"])
                sp.wait_ge(S("clear_set"), 1)
                p.load(sp, "slots_cleared", p.slots.rearrange("(n p) d -> p n d", p=P), p.clear[:])

            @block.gpsimd
            def _(g):
                p.link(g, nc.gpsimd.memset(kt[DQ:DQ + 1, :], 1.0), "pool_step")
                nc.gpsimd.memset(val[:, :, D:D + 1], 1.0).then_inc(S("ones_set"), 1)
                p.link(g, nc.gpsimd.memset(p.clear[:, :, 0:D], 0.0), "pool_step")
                g.wait_ge(S("route_in"), 16)
                nc.gpsimd.tensor_copy(p.clear[:, :, D], p.route[:, slice(*ROUTE[4])]).then_inc(S("clear_set"), 1)

            @block.tensor
            def _(t):
                p.lead(t, "e_turned", "e_projected")

                def turn(c, k):
                    p.after(t, "e_normed", c)
                    p.after(t, "e_xt_out", c - 2)
                    nc.tensor.transpose(pt[:, k, 0:P], p.xn[:, k, :], p.ident).then_inc(S("e_turned"), 1)

                turn(0, 0)
                t.wait_ge(S("att_in"), 64)

                def body(c, k):
                    if not last(c):
                        turn(c + 1, 1 - k)
                    p.after(t, "e_xt_out", c)
                    p.after(t, "e_qk_out", c - 2)
                    p.after(t, "e_vq_out", c - 2)
                    for j in range(2):
                        nc.tensor.matmul(pqk[0:DQ, k, j * P:(j + 1) * P], wk[:, j, :], p.xt[:, k, :], start=True, stop=True)
                    nc.tensor.matmul(pvq[:, k, 0:QV], p.xt[:, k, :], wvq[:], start=True, stop=True).then_inc(S("e_projected"), 1)

                tile_pairs(t, body)

            @block.scalar
            def _(a):
                p.stats_act(a, 5)
                p.lead(a, "e_xt_out", "e_qk_out")

                def xt_out(c, k):
                    p.after(a, "e_turned", c)
                    p.after(a, "e_projected", c - 2)
                    nc.scalar.activation(p.xt[:, k, :], pt[:, k, 0:P], ACT.Copy).then_inc(S("e_xt_out"), 1)

                xt_out(0, 0)

                def body(c, k):
                    if not last(c):
                        xt_out(c + 1, 1 - k)
                    p.after(a, "e_projected", c)
                    p.settled(a, "e_projected", k)
                    nc.scalar.activation(qt[:, bass.ts(c, P)], pqk[0:DQ, k, 0:P], ACT.Copy)
                    nc.scalar.activation(kt[0:DQ, bass.ts(c, P)], pqk[0:DQ, k, P:2 * P], ACT.Copy).then_inc(S("e_qk_out"), 1)

                tile_pairs(a, body)

            @block.vector
            def _(v):
                p.lead(v, "e_vq_out", "e_normed")
                p.stats_dve(v, 5)
                nc.vector.memset(part[:], LOWEST).then_inc(S("part_set"), 1)

                def normed(c, k):
                    p.after(v, "e_turned", c - 2)
                    p.normalise(p.x, p.xn[:, k, :], c).then_inc(S("e_normed"), 1)

                normed(0, 0)
                normed(1, 1)

                def body(c, k):
                    if not (isinstance(c, int) and c >= NT - 2):
                        normed(c + 2, k)
                    p.after(v, "e_projected", c)
                    p.settled(v, "e_projected", k)
                    nc.vector.tensor_copy(val[:, bass.ds(c, 1), 0:D].rearrange("p a d -> p (a d)"), pvq[:, k, 0:D])
                    nc.vector.tensor_copy(q[:, bass.ds(c, 1), 0:DQ].rearrange("p a d -> p (a d)"), pvq[:, k, D:QV]).then_inc(S("e_vq_out"), 1)

                tile_pairs(v, body)

        with ExitStack() as b:
            banks = [p.ps(b, f"score_bank{j}", [P, 512]) for j in range(8)]
            block = b.enter_context(nc.Block())
            chunks = [(c, j) for c in range(NT) for j in range(c // TG + 1)]

            def width(c, j):
                return F if j < c // TG else (c % TG + 1) * P

            @block.tensor
            def _(t):
                for n, (c, j) in enumerate(chunks):
                    if n >= 8:
                        t.wait_ge(S("chunk_read"), n - 7)
                    nc.tensor.matmul(banks[n % 8][:, 0:width(c, j)], qt[:, c * P:(c + 1) * P], kt[0:DQ, j * F:j * F + width(c, j)],
                                     start=True, stop=True).then_inc(S("chunk_scored"), 1)
                t.wait_ge(S("max_set"), 1)
                for g in range(G):
                    for j in range(TG):
                        c = TG * g + j
                        ins = nc.tensor.transpose(banks[g][0:DQ + 1, j * P:(j + 1) * P], q[:, c, :], p.ident)
                    ins.then_inc(S("q_turned"), 1)

            @block.vector
            def _(v):
                for n, (c, j) in enumerate(chunks):
                    v.wait_ge(S("chunk_scored"), n + 1)
                    w = width(c, j)
                    if j == c // TG:
                        p.link(v, nc.vector.tensor_tensor(banks[n % 8][:, w - P:w], banks[n % 8][:, w - P:w], p.mask_ts, ALU.add), "dve_step")
                    nc.vector.tensor_reduce(part[:, c, j:j + 1], banks[n % 8][:, 0:w], X, ALU.max).then_inc(S("chunk_read"), 1)
                v.wait_ge(S("chunk_read"), len(chunks))
                p.link(v, nc.vector.tensor_reduce(mx[:], part[:], X, ALU.max), "dve_step")
                nc.vector.tensor_scalar(q[:, :, DQ], mx[:], -1.0, None, ALU.mult).then_inc(S("max_set"), 1)

            @block.scalar
            def _(a):
                for g in range(G):
                    a.wait_ge(S("q_turned"), g + 1)
                    nc.scalar.activation(qta[:, g * F:(g + 1) * F], banks[g][0:DQ + 1, :], ACT.Copy).then_inc(S("q_turned_out"), 1)

        with ExitStack() as b:
            banks = [p.ps(b, f"turned_bank{j}", [P, 512]) for j in range(4)]
            sums = [p.ps(b, f"v_sum{j}", [P, 512]) for j in range(TG)]
            block = b.enter_context(nc.Block())
            steps = [(g, kb, max(0, kb - TG * g)) for g in range(G) for kb in range(TG * (g + 1))]

            @block.tensor
            def _(t):
                def scores(n):
                    g, kb, t0 = steps[n]
                    if n >= 4:
                        t.wait_ge(S("exp_done"), n - 3)
                    nc.tensor.matmul(banks[n % 4][:, t0 * P:F], kt[:, kb * P:(kb + 1) * P], qta[:, g * F + t0 * P:(g + 1) * F],
                                     start=True, stop=True).then_inc(S("turned_scored"), 1)

                scores(0)
                scores(1)
                for n, (g, kb, t0) in enumerate(steps):
                    if n + 2 < len(steps):
                        scores(n + 2)
                    t.wait_ge(S("exp_done"), n + 1)
                    if kb == 0 and g:
                        t.wait_ge(S("v_sums_out"), g)
                    for j in range(t0, TG):
                        ins = nc.tensor.matmul(sums[j][:, 0:D + 1], probs[:, n % 4, j * P:(j + 1) * P], val[:, kb, :],
                                               start=(kb == 0), stop=(kb == TG * g + j))
                    ins.then_inc(S("v_summed"), 1)

            @block.vector
            def _(v):
                for n, (g, kb, t0) in enumerate(steps):
                    if kb >= TG * g:
                        v.wait_ge(S("turned_scored"), n + 1)
                        d = slice(t0 * P, (t0 + 1) * P)
                        nc.vector.tensor_tensor(banks[n % 4][:, d], banks[n % 4][:, d], p.mask_st, ALU.add).then_inc(S("diagonal_masked"), 1)
                    if kb == TG * (g + 1) - 1:
                        v.wait_ge(S("v_summed"), n + 1)
                        for j in range(TG):
                            c = TG * g + j
                            nc.vector.tensor_copy(p.ao[:, c, :], sums[j][:, 0:D])
                            nc.vector.bn_stats(p.st[:, c, :], sums[j][:, 0:D])
                            ins = nc.vector.tensor_copy(den[:, c:c + 1], sums[j][:, D:D + 1])
                        ins.then_inc(S("v_sums_out"), 1)
                v.wait_ge(S("v_sums_out"), G)
                p.link(v, nc.vector.scalar_tensor_tensor(den[:], den[:], LN_EPS, den[:], ALU.mult, ALU.mult), "dve_step")
                p.stats_dve(v, 6, eps=den[:])
                p.residual(v)
                p.row_stats(v, p.x)

            @block.scalar
            def _(a):
                masked = 0
                for n, (g, kb, t0) in enumerate(steps):
                    if kb >= TG * g:
                        masked += 1
                        a.wait_ge(S("diagonal_masked"), masked)
                    else:
                        a.wait_ge(S("turned_scored"), n + 1)
                    if n >= 4:
                        a.wait_ge(S("v_summed"), n - 3)
                    nc.scalar.activation(probs[:, n % 4, t0 * P:F], banks[n % 4][:, t0 * P:F], ACT.Exp, scale=DQ ** -0.5).then_inc(S("exp_done"), 1)
                p.stats_act(a, 6)


def experts(p, out):
    nc, S, i = p.nc, p.sem, p.i
    w1, w2 = p.ew1, p.ew2
    with ExitStack() as s:
        x4 = p.sb(s, "x4", [P, NT, D])
        pay = p.sb(s, "payload", [P, NT, D + 1])
        cent = p.sb(s, "centroids", [P, E])
        aff = p.sb(s, "affinity", [P, NT, E])
        gate = p.sb(s, "gate", [P, NT])
        hot = p.sb(s, "one_hot", [P, NT, E])
        pos = p.sb(s, "position", [P, NT, E])
        top = p.sb(s, "top", [P, NT])
        first = p.sb(s, "first_rank", [P, NT])
        ratio = p.sb(s, "xhat_scale", [P, NT])
        share = p.sb(s, "expert_share", [P, E])
        ends = p.sb(s, "expert_ends", [P, 6, E])
        before = p.sb(s, "ends_before", [1, SL, E])
        slot_f = p.sb(s, "slot_float", [P, NT])
        owner_f = p.sb(s, "owner_float", [1, SL])
        slot = s.enter_context(nc.sbuf_tensor("slot", [P, NT], U32))
        owner = s.enter_context(nc.sbuf_tensor("owner", [1, SL], I32))
        upto, rank, tiles, numbers, _ = (p.route[:, lo:hi] for lo, hi in ROUTE)

        with ExitStack() as b:
            pt = p.ps(b, "e_xt_psum", [P, 2, 512])
            pa = p.ps(b, "aff_psum", [P, 2, 512])
            pp = p.ps(b, "position_psum", [P, 512])
            pc = p.ps(b, "count_psum", [P, 512])
            block = b.enter_context(nc.Block())

            @block.sync
            def _(sp):
                p.load(sp, "cent_in", cent[:], i["centT"])

            @block.tensor
            def _(t):
                p.lead(t, "f_turned", "f_multiplied")
                t.wait_ge(S("cent_in"), 16)

                def body(c, k):
                    p.after(t, "f_normed", c)
                    p.after(t, "f_xt_out", c - 2)
                    nc.tensor.transpose(pt[:, k, 0:P], p.xn[:, k, :], p.ident).then_inc(S("f_turned"), 1)
                    p.after(t, "f_xt_out", c)
                    p.after(t, "f_aff_out", c - 2)
                    nc.tensor.matmul(pa[:, k, 0:E], p.xt[:, k, :], cent[:], start=True, stop=True).then_inc(S("f_multiplied"), 1)

                tile_pairs(t, body)
                t.wait_ge(S("one_hot"), 1)
                t.wait_ge(S("route_in"), 16)
                nc.tensor.matmul(pp[:, 0:NT * E], upto, hot[:].rearrange("p c e -> p (c e)"), start=True, stop=False)
                for c in range(NT - 1):
                    n = NT - 1 - c
                    ins = nc.tensor.matmul(pp[:, (c + 1) * E:NT * E].rearrange("p (c e) -> p c e", c=n), p.ones,
                                           hot[:, c:c + 1, :].to_broadcast([P, n, E]), start=False, stop=(c == NT - 2))
                ins.then_inc(S("positions_summed"), 1)
                t.wait_ge(S("shared"), 1)
                nc.tensor.matmul(pc[:, 0:E], p.ones, share[:], start=True, stop=True).then_inc(S("counted"), 1)

            @block.scalar
            def _(a):
                p.stats_act(a, 7)
                a.wait_ge(S("xhat_var"), 1)
                nc.scalar.activation(ratio[:], ratio[:], ACT.Sqrt).then_inc(S("xhat_root"), 1)
                p.lead(a, "f_xt_out")

                def body(c, k):
                    p.after(a, "f_turned", c)
                    p.after(a, "f_multiplied", c - 2)
                    nc.scalar.activation(p.xt[:, k, :], pt[:, k, 0:P], ACT.Copy).then_inc(S("f_xt_out"), 1)

                tile_pairs(a, body)
                a.wait_ge(S("aff_bounded"), 1)
                nc.scalar.activation(gate[:], gate[:], ACT.Exp, scale=-1.0).then_inc(S("gate_exp"), 1)

            @block.vector
            def _(v):
                step = lambda ins: p.link(v, ins, "dve_step")
                p.lead(v, "f_normed", "f_kept", "f_aff_out")
                p.stats_dve(v, 7)
                step(nc.vector.tensor_tensor(ratio[:], p.tmp[:, 1, :], p.rstd[:], ALU.mult))
                step(nc.vector.tensor_tensor(ratio[:], ratio[:], p.rstd[:], ALU.mult))
                nc.vector.tensor_scalar(ratio[:], ratio[:], LN_EPS, None, ALU.add).then_inc(S("xhat_var"), 1)

                def normed(c, k):
                    p.after(v, "f_turned", c - 2)
                    p.normalise(p.x, p.xn[:, k, :], c).then_inc(S("f_normed"), 1)
                    p.after(v, "f_normed", c)
                    nc.vector.tensor_copy(tile(x4, c), p.xn[:, k, :]).then_inc(S("f_kept"), 1)

                normed(0, 0)
                normed(1, 1)
                v.wait_ge(S("xhat_root"), 1)
                nc.vector.reciprocal(ratio[:], ratio[:]).then_inc(S("xhat_scale"), 1)

                def body(c, k):
                    if not (isinstance(c, int) and c >= NT - 2):
                        p.after(v, "f_kept", c)
                        normed(c + 2, k)
                    p.after(v, "f_multiplied", c)
                    nc.vector.tensor_copy(tile(aff, c), pa[:, k, 0:E]).then_inc(S("f_aff_out"), 1)

                tile_pairs(v, body)
                p.after(v, "f_kept", NT - 1)
                p.after(v, "f_aff_out", NT - 1)
                step(nc.vector.tensor_reduce(top[:], aff[:], X, ALU.max))
                nc.vector.tensor_scalar(gate[:], top[:], -87.0, None, ALU.max).then_inc(S("aff_bounded"), 1)
                step(nc.vector.tensor_tensor(hot[:], aff[:], per_row(top[:], E), ALU.is_equal))
                v.wait_ge(S("route_in"), 16)
                step(nc.vector.tensor_tensor(pos[:], hot[:], rank.unsqueeze(1).to_broadcast([P, NT, E]), ALU.mult))
                step(nc.vector.tensor_reduce(first[:], pos[:], X, ALU.max))
                nc.vector.tensor_tensor(hot[:], pos[:], per_row(first[:], E), ALU.is_equal).then_inc(S("one_hot"), 1)
                v.wait_ge(S("one_hot"), 1)
                nc.vector.tensor_reduce(share[:], hot[:].rearrange("p c e -> p e c"), X, ALU.add).then_inc(S("shared"), 1)
                v.wait_ge(S("gate_exp"), 1)
                step(nc.vector.tensor_scalar(gate[:], gate[:], 1.0, None, ALU.add))
                step(nc.vector.reciprocal(gate[:], gate[:]))
                v.wait_ge(S("counted"), 1)
                step(nc.vector.tensor_scalar(ends[:, 0, :], pc[:, 0:E], 1.0 / P, 0.5 - 0.5 / P, ALU.mult, ALU.add))
                step(nc.vector.tensor_scalar(ends[:, 0, :], ends[:, 0, :], ROUND, None, ALU.add))
                step(nc.vector.tensor_scalar(ends[:, 0, :], ends[:, 0, :], ROUND, None, ALU.subtract))
                for j in range(3):
                    d = 1 << j
                    nc.vector.tensor_copy(ends[:, j + 1, 0:d], ends[:, j, 0:d])
                    step(nc.vector.tensor_tensor(ends[:, j + 1, d:], ends[:, j, d:], ends[:, j, 0:E - d], ALU.add))
                step(nc.vector.tensor_tensor(ends[:, 4, :], ends[:, 3, :], ends[:, 0, :], ALU.subtract))
                step(nc.vector.tensor_scalar(ends[:, 5, :], ends[:, 4, :], float(P), -1.0, ALU.mult, ALU.add))
                v.wait_ge(S("positions_summed"), 1)
                step(nc.vector.tensor_tensor(pos[:], pp[:, 0:NT * E].rearrange("p (c e) -> p c e", e=E),
                                             ends[:, 5:6, :].to_broadcast([P, NT, E]), ALU.add))
                step(nc.vector.tensor_tensor(pos[:], pos[:], hot[:], ALU.mult))
                step(nc.vector.tensor_reduce(slot_f[:], pos[:], X, ALU.add))
                nc.vector.tensor_copy(slot[:], slot_f[:]).then_inc(S("slots_ready"), 1)
                step(nc.vector.tensor_tensor(before[:], ends[0:1, 3:4, :].to_broadcast([1, SL, E]),
                                             per_row(tiles[0:1, :], E), ALU.is_le))
                step(nc.vector.tensor_reduce(owner_f[:], before[:], X, ALU.add))
                step(nc.vector.tensor_scalar(owner_f[:], owner_f[:], float(E - 1), None, ALU.min))
                step(nc.vector.tensor_copy(owner[:], owner_f[:]))

            @block.gpsimd
            def _(g):
                g.wait_ge(S("xhat_scale"), 1)
                p.after(g, "f_kept", NT - 1)
                g.wait_ge(S("route_in"), 16)
                p.link(g, nc.gpsimd.tensor_tensor(pay[:, :, 0:D], x4[:], per_row(ratio[:], D), ALU.mult), "pool_step")
                p.link(g, nc.gpsimd.tensor_copy(pay[:, :, D], numbers), "pool_step")
                g.wait_ge(S("slots_ready"), 1)
                g.wait_ge(S("slots_cleared"), 16)
                for c in range(NT):
                    g.indirect_dma_start(p.slots, bass.IndirectOffsetOnAxis(ap=slot[:, c:c + 1], axis=0),
                                         pay[:, c, :], None).then_inc(S("scattered"), 16)
                g.wait_ge(S("scattered"), 16 * NT)

        with ExitStack() as b:
            xs = p.sb(b, "slot_rows", [P, 4, D + 1])
            xst = p.sb(b, "slot_turned", [P, 2, P])
            hid = p.sb(b, "expert_hidden", [P, 2, F])
            hit = p.sb(b, "expert_hidden_turned", [P, 2, F])
            ys = p.sb(b, "slot_out", [P, 2, D])
            vecs = p.sb(b, "slot_vecs", [P, 4, 2 + FB])
            b2 = p.sb(b, "slot_b2", [P, 4, D])
            tok = [b.enter_context(nc.sbuf_tensor(f"slot_token{k}", [P, 1], U32)) for k in range(2)]
            pt = p.ps(b, "slot_psum", [P, 2, 512])
            pu = p.ps(b, "slot_up_psum", [P, 2, F])
            ph = p.ps(b, "turned_hidden_psum", [P, 2, F])
            pd = p.ps(b, "slot_down_psum", [P, 2, 512])
            block = b.enter_context(nc.Block())


            def tile_quads(eng, body, ahead=0):
                for n in range(4):
                    body(n, n)
                with eng.Fori(1, SL // 4 - 1) as j:
                    for q in range(4):
                        body(4 * j + q, q)
                for q in range(4 - ahead):
                    body(SL - 4 + q, q)

            def owner_of(eng, n):
                return eng.value_load(owner[0:1, bass.ds(n, 1)], min_val=0, max_val=E - 1)

            @block.sync
            def _(sp):
                def body(n, q):
                    e = owner_of(sp, n)
                    if not (isinstance(n, int) and n < 4):
                        for name in ("s_turned", "s_tokens", "s_out", "s_relu"):
                            p.after(sp, name, n - 4)
                    sp.dma_start(xs[:, q, :], p.slots.rearrange("(n p) d -> n p d", p=P)[bass.ds(n, 1), :, :].rearrange("n p d -> p (n d)")).then_inc(S(f"slot_in{q}"), 16)
                    sp.dma_start(vecs[:, q, :], i["expert_vecs"][bass.ds(e, 1), :, :].rearrange("a p v -> p (a v)")).then_inc(S(f"vecs_in{q}"), 16)
                    sp.dma_start(b2[:, q, :], i["L1_ffn_b2"][bass.ds(e, 1), :].to_broadcast([P, D])).then_inc(S(f"vecs_in{q}"), 16)

                tile_quads(sp, body)
                for k in range(2):
                    sp.wait_ge(S(f"returned{k}"), 8 * SL)
                p.load(sp, "routed_in", p.ao[:], p.routed[0:T, :].rearrange("(c p) d -> p c d", p=P))

            @block.tensor
            def _(t):
                p.lead(t, "s_turned", "s_up", "s_hidden_turned", "s_down")
                t.wait_ge(S("experts_in"), 32)

                def turn(n, q):
                    t.wait_ge(S(f"slot_in{q}"), 4 * n + 16 - 4 * q)
                    p.after(t, "s_xst", n - 2)
                    nc.tensor.transpose(pt[:, q % 2, 0:P], xs[:, q, 0:D], p.ident).then_inc(S("s_turned"), 1)

                def up(n, k, e):
                    p.after(t, "s_xst", n)
                    p.after(t, "s_hidden", n - 2)
                    nc.tensor.matmul(pu[:, k, :], xst[:, k, :], w1[:, bass.ds(e, 1), :].rearrange("p a f -> p (a f)"),
                                     start=True, stop=True).then_inc(S("s_up"), 1)

                def turn_hidden(n, k):
                    p.after(t, "s_hidden", n)
                    p.after(t, "s_relu", n - 2)
                    for m in range(FB):
                        ins = nc.tensor.transpose(ph[:, k, m * P:(m + 1) * P], hid[:, k, m * P:(m + 1) * P], p.ident)
                    ins.then_inc(S("s_hidden_turned"), 1)

                def down(n, k, e):
                    p.after(t, "s_relu", n)
                    p.after(t, "s_out", n - 2)
                    for m in range(FB):
                        ins = nc.tensor.matmul(pd[:, k, 0:D], hit[:, k, m * P:(m + 1) * P],
                                               w2[:, bass.ds(FB * e + m, 1), :].rearrange("p a d -> p (a d)"),
                                               start=(m == 0), stop=(m == FB - 1))
                    ins.then_inc(S("s_down"), 1)

                turn(0, 0)
                turn(1, 1)
                up(0, 0, owner_of(t, 0))

                def quad(n):
                    e = [owner_of(t, n + q) for q in range(4 if last(n + 3, SL) else 5)]
                    for q in range(4):
                        k = q % 2
                        turn_hidden(n + q, k)
                        if not last(n + q, SL):
                            up(n + q + 1, 1 - k, e[q + 1])
                        if not (isinstance(n, int) and n + q >= SL - 2):
                            turn(n + q + 2, (q + 2) % 4)
                        down(n + q, k, e[q])

                with t.Fori(0, SL // 4 - 1) as j:
                    quad(4 * j)
                quad(SL - 4)

            @block.scalar
            def _(a):
                p.lead(a, "s_relu")

                def body(n, q):
                    k = q % 2
                    p.after(a, "s_hidden_turned", n)
                    p.after(a, "s_down", n - 2)
                    a.wait_ge(S(f"vecs_in{q}"), 8 * n + 32 - 8 * q)
                    for m in range(FB):
                        ins = nc.scalar.activation(hit[:, k, m * P:(m + 1) * P], ph[:, k, m * P:(m + 1) * P], ACT.Relu,
                                                   bias=vecs[:, q, 2 + m:3 + m])
                    ins.then_inc(S("s_relu"), 1)

                tile_quads(a, body)
                p.stats_act(a, 8)

            @block.gpsimd
            def _(g):
                for n in range(SL):
                    p.after(g, "s_out", n)
                    g.indirect_dma_start(p.routed, bass.IndirectOffsetOnAxis(ap=tok[n % 2][:], axis=0),
                                         ys[:, n % 2, :], None).then_inc(S(f"returned{n % 2}"), 16)

            @block.vector
            def _(v):
                step = lambda ins: p.link(v, ins, "dve_step")
                p.lead(v, "s_xst", "s_hidden", "s_out", "s_tokens")

                def scaled(n, q):
                    k = q % 2
                    v.wait_ge(S(f"vecs_in{q}"), 8 * n + 32 - 8 * q)
                    p.after(v, "s_turned", n)
                    p.after(v, "s_up", n - 2)
                    nc.vector.tensor_scalar(xst[:, k, :], pt[:, k, 0:P], vecs[:, q, 0:1], vecs[:, q, 1:2],
                                            ALU.mult, ALU.add).then_inc(S("s_xst"), 1)

                def hidden(n, k):
                    p.after(v, "s_up", n)
                    p.after(v, "s_hidden_turned", n - 2)
                    nc.vector.tensor_copy(hid[:, k, :], pu[:, k, :]).then_inc(S("s_hidden"), 1)

                def returned(n, q):
                    k = q % 2
                    if not (isinstance(n, int) and n < 2):
                        v.wait_ge(S(f"returned{k}"), 8 * n - 8 * k)
                    v.wait_ge(S(f"slot_in{q}"), 4 * n + 16 - 4 * q)
                    nc.vector.tensor_copy(tok[k][:], xs[:, q, D:D + 1]).then_inc(S("s_tokens"), 1)
                    p.after(v, "s_down", n)
                    nc.vector.tensor_tensor(ys[:, k, :], pd[:, k, 0:D], b2[:, q, :], ALU.add).then_inc(S("s_out"), 1)

                scaled(0, 0)
                hidden(0, 0)
                scaled(1, 1)

                def body(n, q):
                    hidden(n + 1, (q + 1) % 2)
                    if not (isinstance(n, int) and n >= SL - 2):
                        scaled(n + 2, (q + 2) % 4)
                    returned(n, q)

                tile_quads(v, body, ahead=1)
                returned(SL - 1, 3)
                v.wait_ge(S("routed_in"), 16)
                step(nc.vector.tensor_tensor(p.ao[:], p.ao[:], per_row(gate[:], D), ALU.mult))
                step(nc.vector.tensor_tensor(p.ao[:], p.ao[:], x4[:], ALU.add))
                p.row_stats(v, p.ao)
                p.stats_dve(v, 8)
                p.residual(v)

        block = s.enter_context(nc.Block())

        @block.sync
        def _(sp):
            p.load(sp, "out_written", out.rearrange("a (c p) d -> p (a c) d", p=P), p.x[:])
            sp.wait_ge(S("out_written"), 16)



_DIRECT = ["L0_attn_x", "L0_attn_W_in", "L0_attn_A_log", "L0_attn_dt_bias", "L0_attn_B_norm_bias",
           "L0_attn_C_norm_bias", "L0_attn_W_out", "L0_ffn_w3_s", "L1_attn_Wq", "L1_attn_Wk", "L1_attn_Wv", "L1_ffn_b2"]


def constants():
    import numpy as np

    j, m = np.arange(P)[:, None], np.arange(P)[None, :]
    consts = [j == m, j >= 0 * m, j == m + 1, (j == 0) & (m == P - 1)]
    consts = [np.broadcast_to(a, (P, P)).astype(np.float32) for a in consts]
    consts += [np.where(m > j, -1e30, 0.0).astype(np.float32), np.where(j > m, -1e30, 0.0).astype(np.float32)]
    blocks = range(1, LEV + 1)
    triangles = [((j >> k) == (m >> k)) & (j <= m) for k in blocks] + [((j >> k) == (m >> k)) & (j > m) for k in blocks]
    levels = [j == m] + [((j >> (k + 1)) == (m >> (k + 1))) & ((j >> k) % 2 == 0) & ((m >> k) % 2 == 1) for k in range(LEV)]
    stack = lambda masks: np.ascontiguousarray(np.stack(masks, axis=1).astype(np.float32))
    return {
        "consts": stack(consts),
        "triangles": stack(triangles),
        "level_masks": np.ascontiguousarray(np.repeat(stack(levels)[:, :, None, :], R, axis=2)),
        "route": np.concatenate([j <= m] + [np.broadcast_to(np.array(row), (P, len(row))) for row in (range(E, 0, -1), range(SL))]
                                + [np.arange(T).reshape(NT, P).T, T + np.arange(SL * P).reshape(SL, P).T], axis=1).astype(np.float32),
    }


def kernel(**inputs):
    import numpy as np
    import concourse.bacc as _bacc
    from concourse import mybir as _mybir
    from concourse.bass_utils import run_bass_kernel_spmd as _run

    a = {n: np.asarray(v) for n, v in inputs.items()}
    arrays = {n: a[n] for n in _DIRECT}
    arrays["w1T"], arrays["w2T"] = a["L0_ffn_w1_w"].T, a["L0_ffn_w2_w"].T
    arrays["h1T"], arrays["h2T"], arrays["w3T"] = a["L0_ffn_h1_w"].T, a["L0_ffn_h2_w"].T, a["L0_ffn_w3_w"].T
    for n in ("w1_s", "w2_s", "h1_s", "h2_s"):
        arrays[n] = a["L0_ffn_" + n].reshape(FB, P).T
    arrays["centT"] = a["L1_ffn_centroids"].T
    arrays["expert_vecs"] = np.concatenate([a["L1_ffn_ln_g"][:, :, None], a["L1_ffn_ln_b"][:, :, None],
                                            a["L1_ffn_b1"].reshape(E, FB, P).transpose(0, 2, 1)], axis=2)
    arrays["ew1T"] = a["L1_ffn_w1"].transpose(2, 0, 1)
    arrays["ew2T"] = a["L1_ffn_w2"].reshape(E, D, FB, P).transpose(3, 0, 2, 1).reshape(P, E * FB, D)
    arrays.update(constants())
    arrays = {n: np.ascontiguousarray(v) for n, v in arrays.items()}

    nc = _bacc.Bacc("TRN2", target_bir_lowering=False, num_devices=1)
    drams = {n: nc.dram_tensor("in_" + n, v.shape, _mybir.dt.from_np(v.dtype), kind="ExternalInput").ap() for n, v in arrays.items()}
    out = nc.dram_tensor("out", a["L0_attn_x"].shape, _mybir.dt.float32, kind="ExternalOutput").ap()
    program(nc, drams, out)
    r = _run(nc, [{"in_" + n: v for n, v in arrays.items()}], core_ids=[0])
    return r.results[0]["out"]
```

```python
from contextlib import ExitStack

import concourse.bass as bass
from concourse import mybir

F32 = mybir.dt.float32
F32R = mybir.dt.float32r
U32 = mybir.dt.uint32
I32 = mybir.dt.int32
ALU = mybir.AluOpType
ACT = mybir.ActivationFunctionType
X = mybir.AxisListType.X

P = 128
T = 2048
D = 128
NT = T // P
LEAD = 2

H, R, HD, N = 32, 2, 8, 64
DI = H * HD
ROT = N // 2
NBC = (R + 1) * N
REST = NBC + 2 * H + ROT
LEV = 7
SCALE = float(N * R) ** -0.5
F = 512
FB = F // P
G = T // F
TG = F // P
MLP_COLUMNS = {"w1": 0, "w2": F, "h1": 2 * F, "h2": (2 + FB) * F, "w3": (2 + 2 * FB) * F}
MLP_WIDTH = (2 + 2 * FB) * F + FB * D
DQ = 64
E = 8
SL = NT + E
ROUTE = ((0, P), (P, P + E), (P + E, P + E + SL), (P + E + SL, P + E + SL + NT),
         (P + E + SL + NT, P + E + 2 * SL + NT))

LN_EPS = 1e-5
RMS_EPS = 1e-6
PI = 3.141592653589793
TWO_PI_HI = 6.28125
TWO_PI_LO = 2 * PI - TWO_PI_HI
ROUND = 12582912.0
PI_INSIDE = 3.1415925
DT_MIN, DT_MAX = 1e-4, 0.5
LOWEST = -3e38


def tile(t, c):
    return t[:, bass.ds(c, 1), :].rearrange("p a d -> p (a d)")


def cell(t, c):
    return t[:, bass.ds(c, 1)]


def per_row(t, width):
    return t.unsqueeze(2).to_broadcast([t.shape[0], t.shape[1], width])


def last(c, n=NT):
    return isinstance(c, int) and c == n - 1


def tile_pairs(eng, body, n=NT, first=0):
    for c in range(first):
        body(c, c % 2)
    with eng.Fori(first // 2, n // 2 - 1) as i:
        for k in range(2):
            body(2 * i + k, k)
    for k in range(2):
        body(n - 2 + k, k)


def straight(body, n=NT):
    for c in range(n):
        body(c, c % 2)


class Program:

    def __init__(self, nc, inputs, ctx):
        self.nc, self.i, self.ctx, self.sems, self.counts = nc, inputs, ctx, {}, {}

    def sb(self, stack, name, shape):
        return stack.enter_context(self.nc.sbuf_tensor(name, shape, F32))

    def ps(self, stack, name, shape):
        return stack.enter_context(self.nc.psum_tensor(name, shape, F32))

    def sem(self, name):
        if name not in self.sems:
            self.sems[name] = self.ctx.enter_context(self.nc.semaphore(name))
        return self.sems[name]

    def lead(self, eng, *names, n=LEAD):
        for name in names:
            eng.sem_inc(self.sem(name), n)

    def after(self, eng, name, c):
        eng.wait_ge(self.sem(name), c + 1 + LEAD)

    def settled(self, eng, name, c):
        eng.wait_ge(self.sem(name), c + 1 + LEAD)

    def link(self, eng, ins, name, n=1):
        self.counts[name] = self.counts.get(name, 0) + n
        ins.then_inc(self.sem(name), 1)
        eng.wait_ge(self.sem(name), self.counts[name])

    def load(self, eng, name, dst, src):
        eng.dma_start(dst, src).then_inc(self.sem(name), 16)


    def sum_runs(self, v, name, runs):
        for l in range(len(runs) - 1):
            v.wait_ge(self.sem(name), l + 1)
            pairs = runs[l].rearrange("p (a b) h -> p a b h", b=2)
            self.nc.vector.tensor_tensor(runs[l + 1], pairs[:, :, 0, :], pairs[:, :, 1, :], ALU.add).then_inc(self.sem(name), 1)

    def sum_before(self, t, name, bank, runs):
        for l, run in enumerate(runs):
            t.wait_ge(self.sem(name), l + 1)
            later = bank.rearrange("p (a b n h) -> p a b n h", b=2, n=1 << l, h=run.shape[2])[:, :, 1, :, :]
            before = run.rearrange("p (a b) h -> p a b h", b=2)[:, :, 0:1, :]
            ins = self.nc.tensor.matmul(later, self.ones, before.to_broadcast([P, NT >> (l + 1), 1 << l, run.shape[2]]),
                                        start=False, stop=(l == len(runs) - 1))
        return ins


    def variance(self, v, n, name, stats, moments, eps):
        nc, S, half = self.nc, self.sem, self.half(n)
        for c in self.tiles(n):
            ins = nc.vector.bn_aggr(moments[:, c, :], stats[:, c, :])
        if eps is not None:
            self.link(v, ins, "dve_step")
            ins = nc.vector.tensor_tensor(moments[:, half, 1], moments[:, half, 1], eps[:, half], ALU.add)
        ins.then_inc(S(name + "_var"), 1)

    def root_inverse(self, v, n, name, rstd):
        nc, S, half = self.nc, self.sem, self.half(n)
        v.wait_ge(S(name + "_root"), n + 1)
        nc.vector.reciprocal(rstd[:, half], rstd[:, half]).then_inc(S(name + "_rstd"), 1)
        v.wait_ge(S(name + "_rstd"), n + 1)

    def root_act(self, a, n, name, moments, rstd, eps):
        a.wait_ge(self.sem(name + "_var"), n + 1)
        ins = self.nc.scalar.activation(rstd[:, self.half(n)], moments[:, self.half(n), 1], ACT.Sqrt,
                                        bias=0.0 if eps is not None else self.bias[:, 2:3])
        ins.then_inc(self.sem(name + "_root"), 1)

    def warm(self, a, function):
        self.nc.scalar.activation(self.warm_cell[:], self.bias[:, 0:1], function)

    def half(self, n):
        return slice(n % 2 * NT // 2, (n % 2 + 1) * NT // 2)

    def tiles(self, n):
        return range(NT)[self.half(n)]

    def x_stats(self, v, n):
        self.x_variance(v, n)
        self.x_root_inverse(v, n)

    def x_variance(self, v, n):
        self.variance(v, n, "x", self.st_x, self.mom_x, None)

    def x_root_inverse(self, v, n):
        self.root_inverse(v, n, "x", self.rstd)

    def x_stats_act(self, a, n):
        self.root_act(a, n, "x", self.mom_x, self.rstd, None)

    def layer_stats(self, v, n, eps):
        self.layer_variance(v, n, eps)
        self.layer_factors(v, n)

    def layer_variance(self, v, n, eps):
        self.variance(v, n, "layer", self.st, self.mom, eps)

    def layer_factors(self, v, n):
        half = self.half(n)
        self.root_inverse(v, n, "layer", self.rstd_o)
        self.nc.vector.scalar_tensor_tensor(self.shift_o[:, half], self.mom[:, half, 0], -1.0, self.rstd_o[:, half],
                                            ALU.mult, ALU.mult).then_inc(self.sem("layer_stats"), 1)

    def layer_root(self, a, n, eps):
        self.root_act(a, n, "layer", self.mom, self.rstd_o, eps)

    def layer_scaled(self, a, n, some=slice(None)):
        a.wait_ge(self.sem("layer_stats"), n + 1)
        for c in self.tiles(n)[some]:
            self.nc.scalar.activation(self.ao[:, c, :], self.ao[:, c, :], ACT.Identity, scale=self.rstd_o[:, c:c + 1],
                                      bias=self.shift_o[:, c:c + 1]).then_inc(self.sem("layer_scaled"), 1)

    def layer_added(self, g, n):
        for c in self.tiles(n):
            g.wait_ge(self.sem("layer_scaled"), NT * (n // 2) + c + 1)
            self.nc.gpsimd.tensor_tensor(self.x[:, c, :], self.x[:, c, :], self.ao[:, c, :], ALU.add).then_inc(self.sem("x_added"), 1)
        g.wait_ge(self.sem("x_added"), NT * (n // 2) + c + 1)

    def renew(self, v, n, eps=None):
        self.layer_stats(v, n, eps)
        self.row_stats(v, n)
        self.x_stats(v, n + 2)

    def row_stats(self, v, n):
        for c in self.tiles(n):
            v.wait_ge(self.sem("x_added"), NT * (n // 2) + c + 1)
            ins = self.nc.vector.bn_stats(self.st_x[:, c, :], self.x[:, c, :])
        self.link(v, ins, "dve_step")

    def renew_act(self, a, n, eps=None):
        self.layer_root(a, n, eps)
        self.layer_scaled(a, n)
        self.x_stats_act(a, n + 2)

    def normalise(self, src, dst, c):
        return self.nc.vector.tensor_scalar(dst, tile(src, c), self.mom_x[:, bass.ds(c, 1), 0], cell(self.rstd, c),
                                            ALU.subtract, ALU.mult)


def program(nc, inputs, out):
    with ExitStack() as ctx:
        p = Program(nc, inputs, ctx)
        p.x = p.sb(ctx, "x_res", [P, NT, D])
        p.ao = p.sb(ctx, "layer_out", [P, NT, D])
        p.const = p.sb(ctx, "consts", [P, 6, P])
        p.ident, p.ones, p.shift, p.corner, p.mask_ts, p.mask_st = (p.const[:, j, :] for j in range(6))
        p.st_x = p.sb(ctx, "x_row_stats", [P, NT, 6])
        p.mom_x = p.sb(ctx, "x_moments", [P, NT, 2])
        p.rstd = p.sb(ctx, "x_rstd", [P, NT])
        p.st = p.sb(ctx, "layer_row_stats", [P, NT, 6])
        p.mom = p.sb(ctx, "layer_moments", [P, NT, 2])
        p.rstd_o = p.sb(ctx, "layer_rstd", [P, NT])
        p.shift_o = p.sb(ctx, "layer_shift", [P, NT])
        p.eps_rows = p.sb(ctx, "layer_eps", [P, NT])
        p.xn = p.sb(ctx, "xn", [P, 2, D])
        p.xt = p.sb(ctx, "xt", [P, 2, P])
        p.bias = p.sb(ctx, "act_bias", [P, 3])
        p.warm_cell = p.sb(ctx, "warm_cell", [P, 1])
        p.mlp_up = p.sb(ctx, "mlp_up_weights", [P, 2 * F])
        with ExitStack() as m:
            p.xb = p.sb(m, "x_heads", [P, NT, R * DI])
            p.sz = p.sb(m, "silu_z", [P, NT, DI])
            p.bcr = p.sb(m, "bc_rotated", [P, NT, NBC])
            p.es = p.sb(m, "source_scale", [P, LEV + 2, NT, H])
            p.et = p.sb(m, "target_scale", [P, LEV, NT, H])
            p.cd = p.sb(m, "chunk_decay", [N, NT, H])
            p.gmask = p.sb(m, "level_mask", [P, LEV + 1, R, P])
            with ExitStack() as m1:
                p.rest = p.sb(m1, "proj_rest", [P, NT, REST])
                p.tri = p.sb(m1, "triangles", [P, 2 * LEV, P])
                p.vecs = p.sb(m1, "head_vecs", [P, 2, H])
                p.nbias = p.sb(m1, "norm_bias", [P, R + 1, N])
                p.rms = p.sb(m1, "rms", [P, NT, R + 1])
                project(p)
                decays(p)
            scan(p)
        p.wqk = p.sb(ctx, "w_q_k", [P, 2, 2, DQ])
        p.wv = p.sb(ctx, "w_v", [P, D])
        p.cent = p.sb(ctx, "centroids", [P, E])
        mlp(p)
        p.ew1 = p.sb(ctx, "expert_w1", [P, E, F])
        p.ew2 = p.sb(ctx, "expert_w2", [P, E * FB, D])
        p.route = p.sb(ctx, "route_consts", [P, ROUTE[-1][1]])
        p.clear = p.sb(ctx, "clear_slots", [P, SL, D + 1])
        p.slots = nc.dram_tensor("slots", (SL * P, D + 1), F32, kind="Internal").ap()
        p.routed = nc.dram_tensor("routed", (T + SL * P, D), F32, kind="Internal").ap()
        attention(p)
        experts(p, out)


def project(p):
    nc, i = p.nc, p.i
    with ExitStack() as s:
        w_in = p.sb(s, "w_in", [P, DI + R * DI + REST])
        sq = p.sb(s, "squares", [P, 2, NBC])
        pt = p.ps(s, "xt_psum", [P, 2, 512])
        px = p.ps(s, "x_psum", [P, 2, 512])
        pz = p.ps(s, "z_psum", [P, 2, 512])
        pr = p.ps(s, "rest_psum", [P, 2, 512])
        block = s.enter_context(nc.Block())

        @block.sync
        def _(sp):
            for n in range(4):
                p.load(sp, f"x_in{n}", p.x[:, 4 * n:4 * n + 4, :], i["L0_attn_x"][:, 4 * n * P:(4 * n + 4) * P, :].rearrange("a (c p) d -> p (a c) d", p=P))
            p.load(sp, "const_in", p.const[:], i["consts"])
            p.load(sp, "w_in_in", w_in[:], i["L0_attn_W_in"])
            p.load(sp, "tri_in", p.tri[:], i["triangles"])
            p.load(sp, "tri_in", p.gmask[:], i["level_masks"])
            p.load(sp, "vecs_in", p.vecs[:, 0, :], i["L0_attn_dt_bias"].unsqueeze(0).to_broadcast([P, H]))
            p.load(sp, "vecs_in", p.vecs[:, 1, :], i["L0_attn_A_log"].unsqueeze(0).to_broadcast([P, H]))
            for r, name in enumerate(["B", "B", "C"]):
                p.load(sp, "nbias_in", p.nbias[:, r, :], i[f"L0_attn_{name}_norm_bias"].to_broadcast([P, N]))

        @block.vector
        def _(v):
            p.lead(v, "a_xt_out", "a_normed", "squares_summed")

            def stats(n):
                for c in p.tiles(n):
                    v.wait_ge(p.sem(f"x_in{c // 4}"), 16)
                    ins = nc.vector.bn_stats(p.st_x[:, c, :], p.x[:, c, :])
                p.link(v, ins, "dve_step")
                p.x_stats(v, n)

            stats(0)

            def normed(c, k):
                p.after(v, "a_turned", c - 2)
                p.normalise(p.x, p.xn[:, k, :], c).then_inc(p.sem("a_normed"), 1)

            def xt_out(c, k):
                p.after(v, "a_turned", c)
                p.after(v, "projected", c - 2)
                nc.vector.tensor_copy(p.xt[:, k, :], pt[:, k, 0:P]).then_inc(p.sem("a_xt_out"), 1)

            def squares(c, k):
                p.after(v, "squared", c)
                nc.vector.tensor_reduce(tile(p.rms, c), sq[:, k, :].rearrange("p (r n) -> p r n", n=N), X, ALU.add).then_inc(p.sem("squares_summed"), 1)

            normed(0, 0)
            xt_out(0, 0)
            normed(1, 1)
            stats(1)

            def body(c, k):
                if not last(c):
                    xt_out(c + 1, 1 - k)
                if not (isinstance(c, int) and c >= NT - 2):
                    normed(c + 2, k)
                if not (isinstance(c, int) and c == 0):
                    squares(c - 1, 1 - k)

            tile_pairs(v, body, first=2)
            squares(NT - 1, 1)

        @block.tensor
        def _(t):
            p.lead(t, "a_turned", "projected")

            def turn(c, k):
                p.after(t, "a_normed", c)
                p.after(t, "a_xt_out", c - 2)
                nc.tensor.transpose(pt[:, k, 0:P], p.xn[:, k, :], p.ident).then_inc(p.sem("a_turned"), 1)

            t.wait_ge(p.sem("const_in"), 16)
            turn(0, 0)
            t.wait_ge(p.sem("w_in_in"), 16)

            def body(c, k):
                if not last(c):
                    turn(c + 1, 1 - k)
                p.after(t, "a_xt_out", c)
                p.after(t, "proj_out", c - 2)
                for bank, lo, hi in ((px, DI, DI + R * DI), (pz, 0, DI), (pr, DI + R * DI, DI + R * DI + REST)):
                    ins = nc.tensor.matmul(bank[:, k, 0:hi - lo], p.xt[:, k, :], w_in[:, lo:hi], start=True, stop=True)
                ins.then_inc(p.sem("projected"), 1)

            tile_pairs(t, body)

        @block.scalar
        def _(a):
            p.lead(a, "proj_out", "squared")
            a.wait_ge(p.sem("bias_set"), 1)
            p.x_stats_act(a, 0)
            p.x_stats_act(a, 1)

            def body(c, k):
                p.after(a, "projected", c)
                nc.scalar.activation(tile(p.xb, c).rearrange("p (r h q) -> p h r q", r=R, q=HD),
                                     px[:, k, :].rearrange("p (h r q) -> p h r q", r=R, q=HD), ACT.Silu)
                nc.scalar.activation(tile(p.sz, c), pz[:, k, 0:DI], ACT.Silu)
                p.after(a, "squares_summed", c - 2)
                nc.scalar.activation(sq[:, k, :], pr[:, k, 0:NBC], ACT.Square).then_inc(p.sem("squared"), 1)
                nc.scalar.activation(tile(p.rest, c), pr[:, k, 0:REST], ACT.Copy).then_inc(p.sem("proj_out"), 1)

            straight(body)

        @block.gpsimd
        def _(g):
            nc.gpsimd.memset(p.bias[:, 0:1], 1.0)
            nc.gpsimd.memset(p.bias[:, 2:3], LN_EPS)
            nc.gpsimd.memset(p.bias[:, 1:2], RMS_EPS).then_inc(p.sem("bias_set"), 1)


def decays(p):
    nc, i = p.nc, p.i
    rest = p.rest
    bc = rest[:, :, 0:NBC]
    dt_raw, lam_raw = rest[:, :, NBC:NBC + H], rest[:, :, NBC + H:NBC + 2 * H]
    theta = rest[:, :, NBC + 2 * H:REST]
    S = p.sem
    with ExitStack() as s:
        tri, vecs, nbias, rms = p.tri, p.vecs, p.nbias, p.rms
        m = p.sb(s, "dt_sum", [P, NT])
        names = ["u", "dt", "la", "lam", "v", "w", "mt", "cos", "sin", "turns", "angle"]
        small = {n: p.sb(s, "d_" + n, [P, NT, H]) for n in names}
        u, dt, la, lam, vv, w, mt, cos, sin, turns, angle = (small[n][:] for n in names)
        runs = [mt] + [p.sb(s, f"turns_of_{n}", [P, NT // n, ROT])[:] for n in (2, 4, 8)]
        rot = p.sb(s, "rotation", [P, 4, NT, R + 1, ROT])
        banks = [p.ps(s, f"exp_psum{j}", [P, 512]) for j in range(6)]
        p_ang = p.ps(s, "angle_psum", [P, 512])
        p_next = p.ps(s, "next_psum", [P, 512])
        flat = lambda ap: ap.rearrange("p c h -> p (c h)")
        block = s.enter_context(nc.Block())

        sums = [(p.et[:, l, :, :], tri[:, l, :]) for l in range(LEV)]
        sums += [(p.es[:, l + 1, :, :], p.shift if l == 0 else tri[:, LEV + l - 1, :]) for l in range(LEV + 1)]
        sums += [(p.cd[:], p.ones[:, 0:N])]

        halves = bc.rearrange("p c (r f n) -> p c r f n", r=R + 1, f=2)
        out = p.bcr[:].rearrange("p c (r f n) -> p c r f n", r=R + 1, f=2)
        groups = bc.rearrange("p c (r n) -> p c r n", n=N)

        def rms_scaled(engine, r):
            return engine.tensor_tensor(groups[:, :, r, :], groups[:, :, r, :], per_row(rms[:, :, r], N), ALU.mult)

        def biased(engine, r):
            return engine.tensor_tensor(groups[:, :, r, :], groups[:, :, r, :],
                                        nbias[:, r:r + 1, :].to_broadcast([P, NT, N]), ALU.mult)

        def product(engine, j, r, half, angle):
            return engine.tensor_tensor(rot[:, j, :, r, :], halves[:, :, r, half, :], angle, ALU.mult)

        @block.vector
        def _(v):
            step = lambda ins: p.link(v, ins, "dve_step")
            v.wait_ge(S("vecs_in"), 32)
            step(nc.vector.tensor_tensor(u, dt_raw, vecs[:, 0:1, :].to_broadcast([P, NT, H]), ALU.add))
            nc.vector.tensor_scalar(u, u, 20.0, None, ALU.min).then_inc(S("dt_arg"), 1)
            nc.vector.tensor_scalar(lam, lam_raw, -87.0, None, ALU.max).then_inc(S("lam_arg"), 1)
            v.wait_ge(S("softplus_out"), 1)
            step(nc.vector.tensor_scalar(dt, dt, DT_MIN, DT_MAX, ALU.max, ALU.min))
            step(nc.vector.tensor_reduce(m[:], dt, X, ALU.add))
            nc.vector.scalar_tensor_tensor(mt, theta, -1.0 / H, per_row(m[:], ROT), ALU.mult, ALU.mult).then_inc(S("turns_ready"), 1)
            p.sum_runs(v, "turns_ready", runs)
            nc.vector.scalar_tensor_tensor(la, dt, -1.0, vecs[:, 1:2, :].to_broadcast([P, NT, H]), ALU.mult, ALU.mult).then_inc(S("la_ready"), 1)
            v.wait_ge(S("rms_root"), 1)
            nc.vector.reciprocal(rms[:], rms[:]).then_inc(S("rms_ready"), 1)
            v.wait_ge(S("lam_exp"), 1)
            step(nc.vector.tensor_scalar(lam, lam, 1.0, None, ALU.add))
            step(nc.vector.reciprocal(lam, lam))
            v.wait_ge(S("angle_summed"), 1)
            step(nc.vector.tensor_scalar(flat(turns), p_ang[:], 1.0 / (2 * PI), ROUND, ALU.mult, ALU.add))
            step(nc.vector.tensor_scalar(turns, turns, ROUND, None, ALU.subtract))
            step(nc.vector.scalar_tensor_tensor(flat(angle), flat(turns), -TWO_PI_HI, p_ang[:], ALU.mult, ALU.add))
            step(nc.vector.scalar_tensor_tensor(angle, turns, -TWO_PI_LO, angle, ALU.mult, ALU.add))
            step(nc.vector.tensor_scalar(angle, angle, PI_INSIDE, -PI_INSIDE, ALU.min, ALU.max))
            step(nc.vector.scalar_tensor_tensor(turns, angle, -1.0, angle, ALU.mult, ALU.min))
            nc.vector.tensor_scalar(turns, turns, PI / 2, None, ALU.add).then_inc(S("angle_ready"), 1)
            step(nc.vector.tensor_tensor(p.es[:, 0, :, :], dt, lam, ALU.mult))
            nc.vector.tensor_tensor(vv, dt, p.es[:, 0, :, :], ALU.subtract).then_inc(S("v_ready"), 1)
            v.wait_ge(S("rms_ready"), 1)
            step(nc.vector.tensor_scalar(rms[:, :, R], rms[:, :, R], SCALE, None, ALU.mult))
            v.wait_ge(S("nbias_in"), 48)
            step(rms_scaled(nc.vector, R))
            biased(nc.vector, R).then_inc(S("c_biased"), 1)
            v.wait_ge(S("next_summed"), 1)
            step(nc.vector.tensor_tensor(flat(w), p_next[:], flat(p.es[:, 0, :, :]), ALU.add))

            def weighed(first, end):
                for n in range(first, end):
                    v.wait_ge(S("exp_out"), n + 1)
                    step(nc.vector.tensor_tensor(sums[n][0], sums[n][0], w, ALU.mult))

            v.wait_ge(S("trig_out"), 1)
            v.wait_ge(S("c_biased"), 1)
            v.wait_ge(S("b_biased"), R)
            for r in range(R + 1):
                product(nc.vector, 0, r, 0, cos)
                ins = product(nc.vector, 1, r, 1, sin)
            ins.then_inc(S("half_rotated"), 1)
            v.wait_ge(S("half_rotated"), 1)
            nc.vector.tensor_tensor(out[:, :, :, 0, :], rot[:, 0], rot[:, 1], ALU.subtract)
            weighed(LEV, 2 * LEV + 1)

        @block.gpsimd
        def _(g):
            step = lambda ins: p.link(g, ins, "pool_step")
            g.wait_ge(S("rms_ready"), 1)
            g.wait_ge(S("nbias_in"), 48)
            for r in range(R):
                step(rms_scaled(nc.gpsimd, r))
                biased(nc.gpsimd, r).then_inc(S("b_biased"), 1)
            g.wait_ge(S("b_biased"), R)
            g.wait_ge(S("trig_out"), 1)
            g.wait_ge(S("c_biased"), 1)
            for r in range(R + 1):
                step(product(nc.gpsimd, 2, r, 0, sin))
                step(product(nc.gpsimd, 3, r, 1, cos))
            nc.gpsimd.tensor_tensor(out[:, :, :, 1, :], rot[:, 2], rot[:, 3], ALU.add)

        @block.scalar
        def _(a):
            step = lambda ins: p.link(a, ins, "act_step")
            a.wait_ge(S("vecs_in"), 32)
            step(nc.scalar.activation(vecs[:, 1, :], vecs[:, 1, :], ACT.Exp))
            a.wait_ge(S("dt_arg"), 1)
            a.wait_ge(S("bias_set"), 1)
            step(nc.scalar.activation(u, u, ACT.Exp))
            a.wait_ge(S("lam_arg"), 1)
            nc.scalar.activation(lam, lam, ACT.Exp, scale=-1.0).then_inc(S("lam_exp"), 1)
            nc.scalar.activation(dt, u, ACT.Ln, bias=p.bias[:, 0:1]).then_inc(S("softplus_out"), 1)
            nc.scalar.activation(rms[:], rms[:], ACT.Sqrt, scale=1.0 / N, bias=p.bias[:, 1:2]).then_inc(S("rms_root"), 1)
            a.wait_ge(S("angle_ready"), 1)
            step(nc.scalar.activation(sin, angle, ACT.Sin))
            nc.scalar.activation(cos, turns, ACT.Sin).then_inc(S("trig_out"), 1)
            for n, (dst, _) in enumerate(sums):
                rows = N if n == 2 * LEV + 1 else P
                a.wait_ge(S("exp_summed"), n + 1)
                nc.scalar.activation(flat(dst), banks[n % 6][0:rows, :], ACT.Exp).then_inc(S("exp_out"), 1)

        @block.tensor
        def _(t):
            t.wait_ge(S("tri_in"), 32)
            t.wait_ge(S("turns_ready"), 1)
            nc.tensor.matmul(p_ang[:], tri[:, LEV - 1, :], flat(mt), start=True, stop=False)
            p.sum_before(t, "turns_ready", p_ang[:], runs).then_inc(S("angle_summed"), 1)
            t.wait_ge(S("la_ready"), 1)
            for n, (dst, lhs) in enumerate(sums):
                if n == 6:
                    t.wait_ge(S("v_ready"), 1)
                    nc.tensor.matmul(p_next[:], p.shift, flat(vv), start=True, stop=False)
                    nc.tensor.matmul(p_next[:, 0:(NT - 1) * H], p.corner, flat(vv)[:, H:], start=False, stop=True).then_inc(S("next_summed"), 1)
                if n >= 6:
                    t.wait_ge(S("exp_out"), n - 5)
                rows = N if n == 2 * LEV + 1 else P
                nc.tensor.matmul(banks[n % 6][0:rows, :], lhs, flat(la), start=True, stop=True).then_inc(S("exp_summed"), 1)


BY_DVE = 5
FIRST_BY_DVE = 7
HALF_DONE = NT // 2 + 2


def scan(p):
    nc = p.nc
    S = p.sem
    with ExitStack() as s:
        bcs = p.sb(s, "bc_tile", [P, 2, NBC])
        bct = p.sb(s, "bc_turned", [N, 2, R + 1, P])
        gm = p.sb(s, "scores", [P, 2, LEV + 1, R, P])
        xs = p.sb(s, "x_scaled", [P, 2, LEV + 2, R * DI])
        state = p.sb(s, "state", [N, 2, DI])
        decayed = p.sb(s, "state_decayed", [N, DI])
        tm = p.sb(s, "terms", [P, 2, LEV, DI])
        wo = p.sb(s, "w_out", [P, 2, D])
        ys = p.sb(s, "y_gated", [P, 2, DI])
        yt = p.sb(s, "y_turned", [P, DI])
        sq = p.sb(s, "y_squares", [P, DI])
        ss = p.eps_rows
        pt = p.ps(s, "bct_psum", [P, 512])
        pg = p.ps(s, "score_psum", [P, 512])
        p_st = p.ps(s, "state_psum", [P, 512])
        p_y = p.ps(s, "y_psum", [P, 512])
        p_terms = p.ps(s, "terms_psum", [P, LEV + 1, DI])
        block = s.enter_context(nc.Block())

        def terms_summed(eng, engine, c, k):
            p.after(eng, "b_terms_out", c)
            engine.tensor_tensor(tm[:, k, 0:3, :], tm[:, k, 0:3, :], tm[:, k, 4:7, :], ALU.add).then_inc(S("b_half"), 1)
            p.after(eng, "b_half", c)
            engine.tensor_tensor(tm[:, k, 0:2, :], tm[:, k, 0:2, :], tm[:, k, 2:4, :], ALU.add).then_inc(S("b_quarter"), 1)
            p.after(eng, "b_quarter", c)
            engine.tensor_tensor(tm[:, k, 0, :], tm[:, k, 0, :], tm[:, k, 1, :], ALU.add).then_inc(S("b_y"), 1)

        def scale(engine, c, k, level):
            heads = lambda ap: ap.rearrange("p (r h q) -> p r h q", r=R, q=HD)
            e = tile(p.es[:, level, :, :], c).unsqueeze(1).unsqueeze(3).to_broadcast([P, R, H, HD])
            return engine.tensor_tensor(heads(xs[:, k, level, :]), heads(tile(p.xb, c)), e, ALU.mult)

        @block.sync
        def _(sp):
            p.load(sp, "w_out_in", wo[:], p.i["L0_attn_W_out"].rearrange("(j p) d -> p j d", p=P))
            for j in range(2):
                p.load(sp, "mlp_w_in0", p.mlp_up[:, j * F:(j + 1) * F], p.i[f"w{j + 1}T"])

        @block.scalar
        def _(a):
            p.lead(a, "b_tile_in", "b_turned_out", "c_squared", "c_turned_out", "c_out")

            def turned(c, k):
                p.after(a, "b_state_summed", c - 2)
                nc.scalar.activation(bcs[:, k, :], tile(p.bcr, c), ACT.Copy).then_inc(S("b_tile_in"), 1)
                p.after(a, "b_turned", c)
                p.after(a, "b_terms", c - 2)
                nc.scalar.activation(bct[:, k, :, :], pt[0:N, 0:(R + 1) * P].rearrange("p (r n) -> p r n", n=P),
                                     ACT.Copy).then_inc(S("b_turned_out"), 1)

            def y_out(c):
                p.after(a, "b_gated", c)
                p.after(a, "c_squared", c - 1)
                nc.scalar.activation(sq[:], ys[:, c % 2, :], ACT.Square, accum_out=cell(ss, c)).then_inc(S("c_squared"), 1)
                p.after(a, "c_turned", c)
                nc.scalar.activation(yt[:], p_y[:, 0:DI], ACT.Copy).then_inc(S("c_turned_out"), 1)
                p.after(a, "c_multiplied", c)
                nc.scalar.activation(p.ao[:, c, :], p_y[:, DI:DI + D], ACT.Copy).then_inc(S("c_out"), 1)

            turned(0, 0)
            for c in range(NT):
                if c < NT - 1:
                    turned(c + 1, (c + 1) % 2)
                if c >= 2:
                    y_out(c - 2)
                if c == HALF_DONE:
                    p.layer_root(a, 0, ss)
                if HALF_DONE < c <= HALF_DONE + 4:
                    j = c - HALF_DONE - 1
                    p.layer_scaled(a, 0, slice(2 * j, 2 * j + 2))
            y_out(NT - 2)
            y_out(NT - 1)
            p.x_stats_act(a, 2)

        @block.tensor
        def _(t):
            p.lead(t, "b_turned", "b_scores", "b_terms", "b_state_summed", "c_turned", "c_multiplied")

            def turn_waits(c):
                p.after(t, "b_tile_in", c)
                p.after(t, "b_turned_out", c - 1)

            def turn(k):
                for r in range(R + 1):
                    ins = nc.tensor.transpose(pt[0:N, r * P:(r + 1) * P], bcs[:, k, r * N:(r + 1) * N], p.ident)
                ins.then_inc(S("b_turned"), 1)

            def scores(c, k):
                p.after(t, "b_turned_out", c)
                p.after(t, "b_masked", c - 1)
                for r in range(R):
                    ins = nc.tensor.matmul(pg[:, r * P:(r + 1) * P], bct[:, k, r, :], bct[:, k, R, :], start=True, stop=True)
                ins.then_inc(S("b_scores"), 1)

            def y_turn(c, k):
                p.after(t, "b_gated", c)
                p.after(t, "c_out", c - 1)
                for j in range(2):
                    ins = nc.tensor.transpose(p_y[:, j * P:(j + 1) * P], ys[:, k, j * P:(j + 1) * P], p.ident)
                ins.then_inc(S("c_turned"), 1)

            def y_multiply(c):
                p.after(t, "c_turned_out", c)
                for j in range(2):
                    ins = nc.tensor.matmul(p_y[:, DI:DI + D], yt[:, j * P:(j + 1) * P], wo[:, j, :], start=(j == 0), stop=(j == 1))
                ins.then_inc(S("c_multiplied"), 1)

            turn_waits(0)
            turn(0)
            scores(0, 0)
            t.wait_ge(S("w_out_in"), 16)

            def body(c, k):
                y_ready = not (isinstance(c, int) and c < 2)
                if not last(c):
                    turn_waits(c + 1)
                p.after(t, "b_scaled_dve", c)
                p.after(t, "b_scaled_pool", c)
                p.after(t, "b_state", c)
                for r in range(R):
                    ins = nc.tensor.matmul(p_st[0:N, 0:DI], bcs[:, k, r * N:(r + 1) * N],
                                           xs[:, k, LEV + 1, r * DI:(r + 1) * DI], start=(r == 0), stop=(r == R - 1))
                    if r == 0 and not last(c):
                        turn(1 - k)
                ins.then_inc(S("b_state_summed"), 1)
                if y_ready:
                    y_turn(c - 2, k)
                if not last(c):
                    scores(c + 1, 1 - k)
                p.after(t, "b_masked", c)
                p.after(t, "b_terms_out", c - 1)
                for l in range(LEV):
                    parts = [(j, r) for j in ((0, 1) if l == 0 else (l + 1,)) for r in range(R)]
                    for n, (j, r) in enumerate(parts):
                        nc.tensor.matmul(p_terms[:, l, :], gm[:, k, j, r, :], xs[:, k, j, r * DI:(r + 1) * DI],
                                         start=(n == 0), stop=(n == len(parts) - 1))
                    if l == LEV // 2 and y_ready:
                        y_multiply(c - 2)
                nc.tensor.matmul(p_terms[:, LEV, :], bct[:, k, R, :], state[:, k, :], start=True, stop=True).then_inc(S("b_terms"), 1)

            tile_pairs(t, body, first=2)
            for c in (NT - 2, NT - 1):
                y_turn(c, c % 2)
                y_multiply(c)

        @block.vector
        def _(v):
            p.lead(v, "b_masked", "b_scaled_dve", "b_decayed", "b_state", "b_terms_scaled", "b_terms_out", "b_gated", "c_stats")
            nc.vector.memset(state[:, 0, :], 0.0).then_inc(S("b_state"), 1)

            def masked(c, k):
                p.after(v, "b_scores", c)
                p.after(v, "b_terms", c - 2)
                nc.vector.tensor_tensor(gm[:, k, :, :, :].rearrange("p l r m -> p l (r m)"),
                                        pg[:, 0:R * P].unsqueeze(1).to_broadcast([P, LEV + 1, R * P]),
                                        p.gmask[:].rearrange("p l r m -> p l (r m)"), ALU.mult).then_inc(S("b_masked"), 1)

            def scaled(c, k, n=BY_DVE):
                for level in range(n):
                    ins = scale(nc.vector, c, k, LEV + 1 - level)
                ins.then_inc(S("b_scaled_dve"), 1)

            def gate(c, k):
                p.after(v, "b_y", c)
                p.after(v, "c_squared", c - 2)
                p.after(v, "c_turned", c - 2)
                nc.vector.tensor_tensor(ys[:, k, :], tm[:, k, 0, :], tile(p.sz, c), ALU.mult).then_inc(S("b_gated"), 1)

            def out_stats(c):
                p.after(v, "c_out", c)
                nc.vector.bn_stats(tile(p.st, c), tile(p.ao, c)).then_inc(S("c_stats"), 1)

            scaled(0, 0, FIRST_BY_DVE)
            masked(0, 0)

            def body(c, k):
                if not last(c):
                    masked(c + 1, 1 - k)
                    scaled(c + 1, 1 - k)
                    p.after(v, "b_state", c)
                    nc.vector.tensor_tensor(decayed[:].rearrange("p (h q) -> p h q", q=HD),
                                            state[:, k, :].rearrange("p (h q) -> p h q", q=HD),
                                            per_row(tile(p.cd, c), HD), ALU.mult).then_inc(S("b_decayed"), 1)
                    p.after(v, "b_decayed", c)
                    p.after(v, "b_state_summed", c)
                    p.after(v, "b_terms", c - 1)
                    nc.vector.tensor_tensor(state[:, 1 - k, :], decayed[:], p_st[0:N, 0:DI], ALU.add).then_inc(S("b_state"), 1)
                if not (isinstance(c, int) and c == 0):
                    gate(c - 1, 1 - k)
                p.after(v, "b_terms", c)
                p.after(v, "b_gated", c - 2)
                e = p.et[:, :, bass.ds(c, 1), :].rearrange("p l c h -> p l (c h)").unsqueeze(3).to_broadcast([P, LEV, H, HD])
                nc.vector.tensor_tensor(tm[:, k, :, :].rearrange("p l (h q) -> p l h q", q=HD),
                                        p_terms[:, 1:LEV + 1, :].rearrange("p l (h q) -> p l h q", q=HD),
                                        e, ALU.mult).then_inc(S("b_terms_scaled"), 1)
                p.after(v, "b_terms_scaled", c)
                nc.vector.tensor_tensor(tm[:, k, 0, :], p_terms[:, 0, :], tm[:, k, 0, :], ALU.add).then_inc(S("b_terms_out"), 1)
                if not (isinstance(c, int) and c < 2):
                    out_stats(c - 2)

            for c in range(2):
                body(c, c)
            with v.Fori(1, HALF_DONE // 2) as i:
                for k in range(2):
                    body(2 * i + k, k)
            mixer_eps(p, v, 0)
            p.layer_variance(v, 0, ss)
            body(HALF_DONE, 0)
            p.layer_factors(v, 0)
            for c in range(HALF_DONE + 1, NT):
                body(c, c % 2)
            terms_summed(v, nc.vector, NT - 1, 1)
            gate(NT - 1, 1)
            out_stats(NT - 2)
            p.row_stats(v, 0)
            p.x_variance(v, 2)
            out_stats(NT - 1)
            p.x_root_inverse(v, 2)

        @block.gpsimd
        def _(g):
            p.lead(g, "b_scaled_pool", "b_half", "b_quarter", "b_y")

            def sources(c, k, n=LEV + 2 - BY_DVE):
                p.after(g, "b_terms", c - 2)
                for level in range(n):
                    ins = scale(nc.gpsimd, c, k, level)
                ins.then_inc(S("b_scaled_pool"), 1)

            sources(0, 0, LEV + 2 - FIRST_BY_DVE)

            def body(c, k):
                if not last(c):
                    sources(c + 1, 1 - k)
                terms_summed(g, nc.gpsimd, c, k)

            with g.Fori(0, NT // 2 - 1) as i:
                for k in range(2):
                    body(2 * i + k, k)
            body(NT - 2, 0)
            p.layer_added(g, 0)


def mixer_eps(p, v, n):
    ss = p.eps_rows
    p.after(v, "c_squared", p.tiles(n)[-1])
    p.after(v, "c_stats", p.tiles(n)[-1])
    p.link(v, p.nc.vector.tensor_scalar(ss[:, p.half(n)], ss[:, p.half(n)], LN_EPS / DI, LN_EPS * RMS_EPS,
                                        ALU.mult, ALU.add), "dve_step")


def mlp(p):
    nc, S, i = p.nc, p.sem, p.i
    with ExitStack() as s:
        sbr = lambda name, shape: s.enter_context(nc.sbuf_tensor(name, shape, F32R))
        columns, width = MLP_COLUMNS, MLP_WIDTH
        w_late = p.sb(s, "mlp_late_weights", [P, width - 2 * F])
        w_parts = [sbr(f"mlp_weights_{part}", [P, columns["w3"]]) for part in ("high", "low")]
        scales = p.sb(s, "hidden_scales", [P, 4, FB])
        s3 = p.sb(s, "w3_scale", [P, D])
        xn4 = p.sb(s, "mlp_xn", [P, TG, D])
        xt_parts = [sbr(f"mlp_xt_{part}", [P, F]) for part in ("high", "low")]
        ts = p.sb(s, "silu_part", [P, 2, F])
        half_s1 = p.sb(s, "half_s1", [P, FB])
        s12 = p.sb(s, "s1_s2_half", [P, FB])
        product = p.sb(s, "silu_product", [P, 2, F])
        gelu_out = p.sb(s, "gelu_out", [P, 2, F])
        h = [[sbr(f"hidden{j}_{part}", [P, FB, F]) for part in ("high", "low")] for j in range(2)]
        h_last = p.sb(s, "hidden2", [P, FB, F])
        pt = p.ps(s, "mlp_xt_psum", [P, F])
        pa = p.ps(s, "w1_psum", [P, 2, F])
        pb = p.ps(s, "w2_psum", [P, 2, F])
        ph = p.ps(s, "hidden_psum", [P, 2, F])
        po = p.ps(s, "mlp_out_psum", [P, TG, D])
        block = s.enter_context(nc.Block())
        cuts = [(0, 2 * F), (columns["h1"], columns["h2"]), (columns["h2"], columns["w3"])]
        uncut = [p.mlp_up[:]] + [w_late[:, lo - 2 * F:hi - 2 * F] for lo, hi in cuts[1:]]
        w3 = w_late[:, columns["w3"] - 2 * F:].rearrange("p (k o) -> p k o", k=FB)
        passes = ((0, 0), (0, 1), (1, 0))

        def hidden(g, m):
            return FB * g + m + 1 + LEAD

        def gelued(g, l, m):
            return 2 * FB * g + FB * l + m + 1 + LEAD

        @block.sync
        def _(sp):
            def late(n, name):
                rows = i[name + "T"].rearrange("(k p) o -> p k o", p=P)
                lo = columns[name] - 2 * F
                p.load(sp, f"mlp_w_in{n}", w_late[:, lo:lo + FB * rows.shape[2]].rearrange("p (k o) -> p k o", k=FB), rows)

            late(1, "h1")
            for j, name in enumerate(["w1_s", "w2_s", "h1_s", "h2_s"]):
                p.load(sp, "scales_in", scales[:, j, :], i[name])
            p.load(sp, "scales_in", s3[:], i["L0_ffn_w3_s"].unsqueeze(0).to_broadcast([P, D]))
            late(2, "h2")
            late(2, "w3")
            for j in range(2):
                p.load(sp, "att_in", p.wqk[:, 0, j, :], i["L1_attn_Wq"])
                p.load(sp, "att_in", p.wqk[:, 1, j, :], i["L1_attn_Wk"])
            p.load(sp, "att_in", p.wv[:], i["L1_attn_Wv"])
            p.load(sp, "cent_in", p.cent[:], i["centT"])


        @block.tensor
        def _(t):
            p.lead(t, "d_turned", "d_up", "d_hidden", "d_down")

            def turn(g):
                t.wait_ge(S("d_normed"), g + 1)
                t.wait_ge(S("d_xt_out"), g + LEAD)
                for j in range(TG):
                    ins = nc.tensor.transpose(pt[:, j * P:(j + 1) * P], xn4[:, j, :], p.ident)
                ins.then_inc(S("d_turned"), 1)

            def up(g, blocks):
                t.wait_ge(S("d_xt_out"), g + 1 + LEAD)
                for m in blocks:
                    t.wait_ge(S("d_gated"), hidden(g, m - 2))
                    for bank, name in ((pa, "w1"), (pb, "w2")):
                        lo = columns[name] + m * P
                        for n, (wp, xp) in enumerate(passes):
                            ins = nc.tensor.matmul(bank[:, m % 2, :], w_parts[wp][:, lo:lo + P], xt_parts[xp][:], start=(n == 0), stop=(n == 2))
                    ins.then_inc(S("d_up"), 1)

            def layer(g, l, pieces=None):
                t.wait_ge(S("hidden_weights_low" if l == 0 else "weights_low"), l + 1)
                for m, blocks in pieces or [(m, range(FB)) for m in range(FB)]:
                    for kk in blocks:
                        if kk == 0:
                            t.wait_ge(S("d_gelu"), gelued(g, l, m - 2))
                        if m == 0:
                            t.wait_ge(S("d_gelu_low" if l else "d_gated_low"), hidden(g, kk))
                        lo = columns[f"h{l + 1}"] + kk * F + m * P
                        for n, (wp, hp) in enumerate(passes):
                            ins = nc.tensor.matmul(ph[:, m % 2, :], w_parts[wp][:, lo:lo + P], h[l][hp][:, kk, :],
                                                   start=(kk == 0 and n == 0), stop=(kk == FB - 1 and n == 2))
                    if FB - 1 in blocks:
                        ins.then_inc(S("d_hidden"), 1)

            together = [(0, range(FB - 1)), (1, range(FB - 1)), (0, [FB - 1]), (1, [FB - 1])] + [(m, range(FB)) for m in range(2, FB)]

            def down(g):
                t.wait_ge(S("d_out"), g + LEAD)
                for j in range(TG):
                    for kk in range(FB):
                        if j == 0:
                            t.wait_ge(S("d_gelu"), gelued(g, 1, kk))
                        ins = nc.tensor.matmul(po[:, j, :], h_last[:, kk, j * P:(j + 1) * P], w3[:, kk, :],
                                               start=(kk == 0), stop=(kk == FB - 1))
                ins.then_inc(S("d_down"), 1)

            turn(0)
            t.wait_ge(S("weights_low"), 1)
            up(0, range(FB))
            t.wait_ge(S("mlp_w_in2"), 32)

            def body(g, more=True):
                if more:
                    turn(g + 1)
                layer(g, 0)
                if more:
                    up(g + 1, range(0, FB // 2))
                layer(g, 1, None if more else together)
                if more:
                    up(g + 1, range(FB // 2, FB))
                down(g)

            with t.Fori(0, G - 1) as g:
                body(g)
            body(G - 1, False)


        @block.scalar
        def _(a):
            def weights_high(n):
                lo, hi = cuts[n]
                a.wait_ge(S(f"mlp_w_in{n}"), 16 if n == 1 else 32)
                nc.scalar.activation(w_parts[0][:, lo:hi], uncut[n], ACT.Copy).then_inc(S("weights_high"), 1)

            p.lead(a, "d_tanh", "d_gelu")
            weights_high(0)
            a.wait_ge(S("bias_set"), 1)
            p.warm(a, ACT.Tanh)
            weights_high(1)

            def tanh(g, blocks):
                for m in blocks:
                    a.wait_ge(S("d_up"), hidden(g, m))
                    a.wait_ge(S("d_gated"), hidden(g, m - 2))
                    nc.scalar.activation(ts[:, m % 2, :], pa[:, m % 2, :], ACT.Tanh, scale=half_s1[:, m:m + 1]).then_inc(S("d_tanh"), 1)

            def gelu(g, l):
                for m in range(FB):
                    a.wait_ge(S("d_hidden"), gelued(g, l, m))
                    if l == 0:
                        a.wait_ge(S("d_gelu_low"), hidden(g, m - 2))
                    elif m == 0:
                        a.wait_ge(S("d_down"), g + LEAD)
                    nc.scalar.activation(h_last[:, m, :] if l else gelu_out[:, m % 2, :], ph[:, m % 2, :], ACT.Gelu, scale=scales[:, 2 + l, m:m + 1]).then_inc(S("d_gelu"), 1)

            a.wait_ge(S("silu_scales"), 1)
            tanh(0, range(FB))
            weights_high(2)
            p.layer_root(a, 1, p.eps_rows)
            p.layer_scaled(a, 1)
            for g in range(G):
                if g == 2:
                    p.layer_root(a, 2, None)
                if g == 3:
                    p.x_stats_act(a, 4)
                gelu(g, 0)
                if g < G - 1:
                    tanh(g + 1, range(0, FB // 2))
                if g == 0:
                    p.x_stats_act(a, 3)
                if g == 2:
                    p.layer_scaled(a, 2)
                gelu(g, 1)
                if g < G - 1:
                    tanh(g + 1, range(FB // 2, FB))
            p.warm(a, ACT.Sqrt)

        @block.gpsimd
        def _(g):
            def gated_low(group, blocks):
                for m in blocks:
                    g.wait_ge(S("d_gated"), hidden(group, m))
                    nc.gpsimd.tensor_tensor(h[0][1][:, m, :], product[:, m % 2, :], h[0][0][:, m, :], ALU.subtract).then_inc(S("d_gated_low"), 1)
                    g.wait_ge(S("d_gated_low"), hidden(group, m))

            def gelu_low(group):
                for m in range(FB):
                    g.wait_ge(S("d_gelu_high"), hidden(group, m))
                    nc.gpsimd.tensor_tensor(h[1][1][:, m, :], gelu_out[:, m % 2, :], h[1][0][:, m, :], ALU.subtract).then_inc(S("d_gelu_low"), 1)
                    g.wait_ge(S("d_gelu_low"), hidden(group, m))

            p.lead(g, "d_gated_low", "d_gelu_low")
            lo, hi = cuts[1]
            g.wait_ge(S("weights_high"), 2)
            nc.gpsimd.tensor_tensor(w_parts[1][:, lo:hi], uncut[1], w_parts[0][:, lo:hi], ALU.subtract).then_inc(S("hidden_weights_low"), 1)
            g.wait_ge(S("hidden_weights_low"), 1)
            gated_low(0, range(FB))
            p.layer_added(g, 1)
            for group in range(G):
                gelu_low(group)
                if group < G - 1:
                    gated_low(group + 1, range(0, FB // 2))
                if group == 2:
                    p.layer_added(g, 2)
                if group < G - 1:
                    gated_low(group + 1, range(FB // 2, FB))

        @block.vector
        def _(v):
            p.lead(v, "d_gated", "d_gelu_high", "d_out", "d_xt_out")

            def normed(g):
                v.wait_ge(S("d_turned"), g + LEAD)
                for j in range(TG):
                    ins = p.normalise(p.x, xn4[:, j, :], TG * g + j)
                ins.then_inc(S("d_normed"), 1)

            def xt_out(g):
                v.wait_ge(S("d_turned"), g + 1 + LEAD)
                v.wait_ge(S("d_up"), hidden(g, -1))
                p.link(v, nc.vector.tensor_copy(xt_parts[0][:], pt[:]), "dve_step")
                nc.vector.tensor_tensor(xt_parts[1][:], pt[:], xt_parts[0][:], ALU.subtract).then_inc(S("d_xt_out"), 1)

            def gated(g, blocks):
                for m in blocks:
                    v.wait_ge(S("d_tanh"), hidden(g, m))
                    p.link(v, nc.vector.scalar_tensor_tensor(ts[:, m % 2, :], ts[:, m % 2, :], 1.0, pa[:, m % 2, :], ALU.add, ALU.mult), "dve_step")
                    v.wait_ge(S("d_gated_low"), hidden(g, m - 2))
                    p.link(v, nc.vector.scalar_tensor_tensor(product[:, m % 2, :], ts[:, m % 2, :], s12[:, m:m + 1], pb[:, m % 2, :],
                                                             ALU.mult, ALU.mult), "dve_step")
                    if g:
                        v.wait_ge(S("d_hidden"), gelued(g - 1, 0, FB - 1))
                    nc.vector.tensor_copy(h[0][0][:, m, :], product[:, m % 2, :]).then_inc(S("d_gated"), 1)

            def weights_low(n):
                lo, hi = cuts[n]
                v.wait_ge(S("weights_high"), n + 1)
                nc.vector.tensor_tensor(w_parts[1][:, lo:hi], uncut[n], w_parts[0][:, lo:hi], ALU.subtract).then_inc(S("weights_low"), 1)

            def gelu_high(g):
                for m in range(FB):
                    v.wait_ge(S("d_gelu"), gelued(g, 0, m))
                    nc.vector.tensor_copy(h[1][0][:, m, :], gelu_out[:, m % 2, :]).then_inc(S("d_gelu_high"), 1)

            def out(g):
                v.wait_ge(S("d_down"), g + 1 + LEAD)
                rows = p.ao[:, TG * g:TG * (g + 1), :]
                nc.vector.tensor_tensor(rows, po[:], s3[:].unsqueeze(1).to_broadcast([P, TG, D]), ALU.mult).then_inc(S("d_out"), 1)
                v.wait_ge(S("d_out"), g + 1 + LEAD)
                for c in range(TG * g, TG * (g + 1)):
                    ins = nc.vector.bn_stats(p.st[:, c, :], p.ao[:, c, :])
                p.link(v, ins, "dve_step")

            normed(0)
            weights_low(0)
            xt_out(0)
            normed(1)
            v.wait_ge(S("scales_in"), 80)
            p.link(v, nc.vector.tensor_scalar(half_s1[:], scales[:, 0, :], 0.5, None, ALU.mult), "dve_step")
            nc.vector.tensor_tensor(s12[:], half_s1[:], scales[:, 1, :], ALU.mult).then_inc(S("silu_scales"), 1)
            gated(0, range(FB))
            mixer_eps(p, v, 1)
            p.layer_stats(v, 1, p.eps_rows)
            weights_low(2)
            for g in range(G):
                if g < G - 1:
                    xt_out(g + 1)
                if g == 2:
                    p.layer_stats(v, 2, None)
                if g == 3:
                    p.x_stats(v, 4)
                gelu_high(g)
                if g < G - 1:
                    gated(g + 1, range(0, FB // 2))
                if g == 0:
                    p.row_stats(v, 1)
                    p.x_stats(v, 3)
                if g < G - 2:
                    normed(g + 2)
                if g < G - 1:
                    gated(g + 1, range(FB // 2, FB))
                if g == 2:
                    p.row_stats(v, 2)
                out(g)


OUT_BY_DVE = range(NT - 4, NT)


def attention(p):
    nc, S, i = p.nc, p.sem, p.i
    with ExitStack() as s:
        sbr = lambda name, shape: s.enter_context(nc.sbuf_tensor(name, shape, F32R))
        wqk, wv = p.wqk, p.wv
        qs = sbr("q_high_low", [P, T])
        kh = sbr("k_high", [P, T])
        kl = sbr("k_low", [P, T])
        unit = sbr("unit_and_masks", [P, 4, P])
        ident, mask_ts, mask_st, ones = (unit[:, j, :] for j in range(4))
        val = p.sb(s, "v_rows", [P, NT, D + 1])
        part = p.sb(s, "part_max", [P, NT, G])
        mx = p.sb(s, "row_max", [P, NT])
        rounded = sbr("max_rounded", [P, 2, NT])
        cut = p.sb(s, "max_parts", [P, NT, 4])
        shift = sbr("max_parts_turned", [4, T])
        probs = p.sb(s, "probs", [P, 4, F])
        den = p.eps_rows

        with ExitStack() as b:
            pt = p.ps(b, "att_xt_psum", [P, 2, 512])
            pqk = p.ps(b, "qk_psum", [P, 2, 512])
            pv = p.ps(b, "v_psum", [P, 2, 512])
            block = b.enter_context(nc.Block())

            @block.sync
            def _(sp):
                p.load(sp, "route_in", p.route[:], i["route"])
                p.load(sp, "experts_in", p.ew1[:], i["ew1T"])
                p.load(sp, "experts_in", p.ew2[:], i["ew2T"])
                sp.wait_ge(S("clear_set"), 1)
                p.load(sp, "slots_cleared", p.slots.rearrange("(n p) d -> p n d", p=P), p.clear[:])

            @block.gpsimd
            def _(g):
                p.layer_added(g, 3)
                nc.gpsimd.memset(cut[:, :, 3:4], 0.0)
                nc.gpsimd.memset(val[:, :, D:D + 1], 1.0)
                p.link(g, nc.gpsimd.memset(p.clear[:, :, 0:D], 0.0), "pool_step")
                g.wait_ge(S("route_in"), 16)
                nc.gpsimd.tensor_copy(p.clear[:, :, D], p.route[:, slice(*ROUTE[4])]).then_inc(S("clear_set"), 1)

            @block.tensor
            def _(t):
                p.lead(t, "e_turned", "e_projected")

                def turn(c, k):
                    p.after(t, "e_normed", c)
                    p.after(t, "e_xt_out", c - 2)
                    nc.tensor.transpose(pt[:, k, 0:P], p.xn[:, k, :], p.ident).then_inc(S("e_turned"), 1)

                turn(0, 0)
                t.wait_ge(S("att_in"), 80)

                def body(c, k):
                    if not last(c):
                        turn(c + 1, 1 - k)
                    p.after(t, "e_xt_out", c)
                    p.after(t, "e_parts", c - 2)
                    for j in range(2):
                        nc.tensor.matmul(pqk[:, k, j * P:(j + 1) * P], wqk[:, j, :, :].rearrange("p a d -> p (a d)"),
                                         p.xt[:, k, :], start=True, stop=True)
                    nc.tensor.matmul(pv[:, k, 0:D], p.xt[:, k, :], wv[:], start=True, stop=True).then_inc(S("e_projected"), 1)

                tile_pairs(t, body)

            @block.scalar
            def _(a):
                p.lead(a, "e_xt_out", "e_high")

                def xt_out(c, k):
                    p.after(a, "e_turned", c)
                    p.after(a, "e_projected", c - 2)
                    nc.scalar.activation(p.xt[:, k, :], pt[:, k, 0:P], ACT.Copy).then_inc(S("e_xt_out"), 1)

                xt_out(0, 0)

                def body(c, k):
                    if not last(c):
                        xt_out(c + 1, 1 - k)
                    p.after(a, "e_projected", c)
                    nc.scalar.activation(qs[:, bass.ts(c, P)], pqk[:, k, 0:P], ACT.Copy)
                    nc.scalar.activation(kh[:, bass.ts(c, P)], pqk[:, k, P:2 * P], ACT.Copy).then_inc(S("e_high"), 1)
                    if c == 0:
                        p.layer_root(a, 3, None)
                    if c == 1:
                        p.layer_scaled(a, 3)
                    if c == 4:
                        p.x_stats_act(a, 5)

                straight(body)

            @block.vector
            def _(v):
                p.lead(v, "e_parts", "e_normed")

                def normed(c, k):
                    p.after(v, "e_turned", c - 2)
                    p.normalise(p.x, p.xn[:, k, :], c).then_inc(S("e_normed"), 1)

                normed(0, 0)
                normed(1, 1)

                def body(c, k):
                    if c == 0:
                        p.layer_stats(v, 3, None)
                    if c == 4:
                        p.row_stats(v, 3)
                    if c == 5:
                        p.x_stats(v, 5)
                    if c < NT - 2:
                        normed(c + 2, k)
                    p.after(v, "e_projected", c)
                    nc.vector.tensor_copy(val[:, bass.ds(c, 1), 0:D].rearrange("p a d -> p (a d)"), pv[:, k, 0:D])
                    p.after(v, "e_high", c)
                    nc.vector.tensor_tensor(kl[:, bass.ts(c, P)], pqk[:, k, P:2 * P], kh[:, bass.ts(c, P)], ALU.subtract)
                    nc.vector.tensor_tensor(qs[DQ:P, bass.ts(c, P)], pqk[DQ:P, k, 0:P], qs[DQ:P, bass.ts(c, P)],
                                            ALU.subtract).then_inc(S("e_parts"), 1)

                for c in range(NT):
                    body(c, c % 2)
                nc.vector.memset(part[:], LOWEST)
                for j, source in enumerate((p.ident, p.mask_ts, p.mask_st, p.ones)):
                    nc.vector.tensor_copy(unit[:, j, :], source)

        with ExitStack() as b:
            banks = [p.ps(b, f"score_bank{j}", [P, 512]) for j in range(8)]
            block = b.enter_context(nc.Block())
            chunks = [(c, j) for c in range(NT) for j in range(c // TG + 1)]

            def width(c, j):
                return F if j < c // TG else (c % TG + 1) * P

            @block.tensor
            def _(t):
                for n, (c, j) in enumerate(chunks):
                    if n >= 8:
                        t.wait_ge(S("chunk_read"), n - 7)
                    w = width(c, j)
                    for low, k_part in enumerate((kh, kl)):
                        ins = nc.tensor.matmul(banks[n % 8][:, 0:w], qs[:, c * P:(c + 1) * P], k_part[:, j * F:j * F + w],
                                               start=(low == 0), stop=(low == 1 and j < c // TG))
                    if j == c // TG:
                        ins = nc.tensor.matmul(banks[n % 8][:, w - P:w], ident, mask_ts, start=False, stop=True)
                    ins.then_inc(S("chunk_scored"), 1)
                t.wait_ge(S("max_cut"), 1)
                for g in range(G):
                    for j in range(TG):
                        ins = nc.tensor.transpose(banks[g][0:4, j * P:(j + 1) * P], cut[:, TG * g + j, :], p.ident)
                    ins.then_inc(S("max_turned"), 1)

            @block.vector
            def _(v):
                step = lambda ins: p.link(v, ins, "dve_step")
                for n, (c, j) in enumerate(chunks):
                    v.wait_ge(S("chunk_scored"), n + 1)
                    nc.vector.tensor_reduce(part[:, c, j:j + 1], banks[n % 8][:, 0:width(c, j)], X, ALU.max).then_inc(S("chunk_read"), 1)
                v.wait_ge(S("chunk_read"), len(chunks))
                step(nc.vector.tensor_reduce(mx[:], part[:], X, ALU.max))
                step(nc.vector.tensor_scalar(mx[:], mx[:], -1.0, None, ALU.mult))
                for j in range(2):
                    step(nc.vector.tensor_copy(rounded[:, j, :], mx[:]))
                    nc.vector.tensor_copy(cut[:, :, j], rounded[:, j, :])
                    step(nc.vector.tensor_tensor(mx[:], mx[:], rounded[:, j, :], ALU.subtract))
                nc.vector.tensor_copy(cut[:, :, 2], mx[:]).then_inc(S("max_cut"), 1)

            @block.scalar
            def _(a):
                for g in range(G):
                    a.wait_ge(S("max_turned"), g + 1)
                    nc.scalar.activation(shift[:, g * F:(g + 1) * F], banks[g][0:4, :], ACT.Copy)

        with ExitStack() as b:
            banks = [p.ps(b, f"turned_bank{j}", [P, 512]) for j in range(4)]
            sums = [p.ps(b, f"v_sum{j}", [P, 512]) for j in range(TG)]
            block = b.enter_context(nc.Block())

            steps = [(g, kb, max(0, kb - TG * g)) for g in range(G) for kb in range(TG * (g + 1))]

            @block.tensor
            def _(t):
                def scores(n):
                    g, kb, t0 = steps[n]
                    if n >= 4:
                        t.wait_ge(S("exp_done"), n - 3)
                    bank, queries, keys = banks[n % 4], slice(g * F + t0 * P, (g + 1) * F), slice(kb * P, (kb + 1) * P)
                    nc.tensor.matmul(bank[:, t0 * P:F], kh[:, keys], qs[:, queries], start=True, stop=False)
                    nc.tensor.matmul(bank[:, t0 * P:F], kl[:, keys], qs[:, queries], start=False, stop=False)
                    ins = nc.tensor.matmul(bank[:, t0 * P:F], ones[0:4, :], shift[:, queries], start=False, stop=(kb < TG * g))
                    if kb >= TG * g:
                        ins = nc.tensor.matmul(bank[:, t0 * P:(t0 + 1) * P], ident, mask_st, start=False, stop=True)
                    ins.then_inc(S("turned_scored"), 1)

                scores(0)
                scores(1)
                for n, (g, kb, t0) in enumerate(steps):
                    if n + 2 < len(steps):
                        scores(n + 2)
                    t.wait_ge(S("exp_done"), n + 1)
                    for j in range(t0, TG):
                        if kb == 0 and g:
                            t.wait_ge(S("v_sums_out"), TG * (g - 1) + j + 1)
                        ins = nc.tensor.matmul(sums[j][:, 0:D + 1], probs[:, n % 4, j * P:(j + 1) * P], val[:, kb, :],
                                               start=(kb == 0), stop=(kb == TG * g + j))
                    ins.then_inc(S("v_summed"), 1)

            @block.vector
            def _(v):
                for n, (g, kb, t0) in enumerate(steps):
                    if kb >= TG * g:
                        j = kb - TG * g
                        v.wait_ge(S("v_summed"), n + 1)
                        nc.vector.tensor_copy(p.ao[:, kb, :], sums[j][:, 0:D])
                        nc.vector.tensor_copy(den[:, kb:kb + 1], sums[j][:, D:D + 1]).then_inc(S("v_sums_out"), 1)
                        v.wait_ge(S("v_sums_out"), kb + 1)
                        ins = nc.vector.bn_stats(p.st[:, kb, :], p.ao[:, kb, :])
                    if kb == TG * (g + 1) - 1:
                        p.link(v, ins, "dve_step")
                        if g % 2:
                            half = p.half(4 + g // 2)
                            p.link(v, nc.vector.scalar_tensor_tensor(den[:, half], den[:, half], LN_EPS, den[:, half],
                                                                     ALU.mult, ALU.mult), "dve_step")
                    if (g, kb) == (2, 0):
                        p.layer_stats(v, 4, p.eps_rows)
                    if (g, kb) == (2, TG * (g + 1) - 1):
                        p.row_stats(v, 4)
                        p.x_stats(v, 6)

            @block.gpsimd
            def _(g):
                p.layer_added(g, 4)

            @block.scalar
            def _(a):
                for n, (g, kb, t0) in enumerate(steps):
                    a.wait_ge(S("turned_scored"), n + 1)
                    if n >= 4:
                        a.wait_ge(S("v_summed"), n - 3)
                    nc.scalar.activation(probs[:, n % 4, t0 * P:F], banks[n % 4][:, t0 * P:F], ACT.Exp, scale=DQ ** -0.5).then_inc(S("exp_done"), 1)
                    if (g, kb) == (2, 2):
                        p.layer_root(a, 4, p.eps_rows)
                    if g == 2 and 3 <= kb < 3 + NT // 4:
                        p.layer_scaled(a, 4, slice(2 * (kb - 3), 2 * (kb - 3) + 2))
                    if (g, kb) == (3, 2):
                        p.x_stats_act(a, 6)
                p.warm(a, ACT.Sqrt)


def experts(p, out):
    nc, S, i = p.nc, p.sem, p.i
    w1, w2 = p.ew1, p.ew2
    with ExitStack() as s:
        x4 = p.sb(s, "x4", [P, NT, D])
        pay = p.sb(s, "payload", [P, NT, D + 1])
        cent = p.cent
        aff = p.sb(s, "affinity", [P, NT, E])
        gate = p.sb(s, "gate", [P, NT])
        hot = p.sb(s, "one_hot", [P, NT, E])
        pos = p.sb(s, "position", [P, NT, E])
        hot_runs = [hot[:]] + [p.sb(s, f"one_hot_of_{n}", [P, NT // n, E])[:] for n in (2, 4, 8)]
        top = p.sb(s, "top", [P, NT])
        first = p.sb(s, "first_rank", [P, NT])
        ratio = p.sb(s, "xhat_scale", [P, NT])
        share = p.sb(s, "expert_share", [P, E])
        ends = p.sb(s, "expert_ends", [P, 6, E])
        before = p.sb(s, "ends_before", [1, SL, E])
        slot_f = p.sb(s, "slot_float", [P, NT])
        owner_f = p.sb(s, "owner_float", [1, SL])
        slot = s.enter_context(nc.sbuf_tensor("slot", [P, NT], U32))
        owner = s.enter_context(nc.sbuf_tensor("owner", [1, SL], I32))
        vecs = p.sb(s, "expert_vecs", [P, E, D + 2 + FB])
        upto, rank, tiles, numbers, _ = (p.route[:, lo:hi] for lo, hi in ROUTE)

        with ExitStack() as b:
            pt = p.ps(b, "e_xt_psum", [P, 2, 512])
            pa = p.ps(b, "aff_psum", [P, 2, 512])
            pp = p.ps(b, "position_psum", [P, 512])
            pc = p.ps(b, "count_psum", [P, 512])
            block = b.enter_context(nc.Block())

            @block.sync
            def _(sp):
                p.load(sp, "expert_vecs_in", vecs[:, :, 0:D], i["L1_ffn_b2"].unsqueeze(0).to_broadcast([P, E, D]))
                p.load(sp, "expert_vecs_in", vecs[:, :, D:], i["expert_vecs"])

            @block.tensor
            def _(t):
                p.lead(t, "f_turned", "f_multiplied")
                t.wait_ge(S("cent_in"), 16)

                def turn(c, k):
                    p.after(t, "f_normed", c)
                    p.after(t, "f_xt_out", c - 2)
                    nc.tensor.transpose(pt[:, k, 0:P], p.xn[:, k, :], p.ident).then_inc(S("f_turned"), 1)

                turn(0, 0)

                def body(c, k):
                    if not last(c):
                        turn(c + 1, 1 - k)
                    p.after(t, "f_xt_out", c)
                    p.after(t, "f_aff_out", c - 2)
                    nc.tensor.matmul(pa[:, k, 0:E], p.xt[:, k, :], cent[:], start=True, stop=True).then_inc(S("f_multiplied"), 1)

                tile_pairs(t, body)
                t.wait_ge(S("one_hot"), 1)
                t.wait_ge(S("route_in"), 16)
                nc.tensor.matmul(pp[:, 0:NT * E], upto, hot[:].rearrange("p c e -> p (c e)"), start=True, stop=False)
                p.sum_before(t, "one_hot", pp[:, 0:NT * E], hot_runs).then_inc(S("positions_summed"), 1)
                t.wait_ge(S("shared"), 1)
                nc.tensor.matmul(pc[:, 0:E], p.ones, share[:], start=True, stop=True).then_inc(S("counted"), 1)

            @block.scalar
            def _(a):
                p.lead(a, "f_xt_out")

                def body(c, k):
                    p.after(a, "f_turned", c)
                    p.after(a, "f_multiplied", c - 2)
                    nc.scalar.activation(p.xt[:, k, :], pt[:, k, 0:P], ACT.Copy).then_inc(S("f_xt_out"), 1)
                    if c == 0:
                        p.layer_root(a, 5, p.eps_rows)
                    if c == 2:
                        p.layer_scaled(a, 5)
                    if c == 5:
                        p.x_stats_act(a, 7)
                        a.wait_ge(S("xhat_var"), 2)
                        nc.scalar.activation(ratio[:], ratio[:], ACT.Sqrt).then_inc(S("xhat_root"), 1)

                straight(body)
                a.wait_ge(S("aff_bounded"), 1)
                nc.scalar.activation(gate[:], gate[:], ACT.Exp, scale=-1.0).then_inc(S("gate_exp"), 1)

            @block.vector
            def _(v):
                step = lambda ins: p.link(v, ins, "dve_step")
                p.lead(v, "f_normed", "f_kept", "f_aff_out")

                def second_scale(n):
                    half = p.half(n)
                    step(nc.vector.tensor_tensor(ratio[:, half], p.mom_x[:, half, 1], p.rstd[:, half], ALU.mult))
                    step(nc.vector.tensor_tensor(ratio[:, half], ratio[:, half], p.rstd[:, half], ALU.mult))
                    nc.vector.tensor_scalar(ratio[:, half], ratio[:, half], LN_EPS, None, ALU.add).then_inc(S("xhat_var"), 1)

                def normed(c, k):
                    p.after(v, "f_turned", c - 2)
                    p.normalise(p.x, p.xn[:, k, :], c).then_inc(S("f_normed"), 1)
                    p.after(v, "f_normed", c)
                    nc.vector.tensor_copy(tile(x4, c), p.xn[:, k, :]).then_inc(S("f_kept"), 1)

                normed(0, 0)
                normed(1, 1)

                def body(c, k):
                    if c == 0:
                        p.layer_stats(v, 5, p.eps_rows)
                    if c == 4:
                        p.row_stats(v, 5)
                    if c == 5:
                        p.x_stats(v, 7)
                        second_scale(0)
                        second_scale(1)
                    if c == 8:
                        v.wait_ge(S("xhat_root"), 1)
                        nc.vector.reciprocal(ratio[:], ratio[:]).then_inc(S("xhat_scale"), 1)
                    if c < NT - 2:
                        p.after(v, "f_kept", c)
                        normed(c + 2, k)
                    p.after(v, "f_multiplied", c)
                    nc.vector.tensor_copy(tile(aff, c), pa[:, k, 0:E]).then_inc(S("f_aff_out"), 1)

                for c in range(NT):
                    body(c, c % 2)
                p.after(v, "f_kept", NT - 1)
                p.after(v, "f_aff_out", NT - 1)
                step(nc.vector.tensor_reduce(top[:], aff[:], X, ALU.max))
                nc.vector.tensor_scalar(gate[:], top[:], -87.0, None, ALU.max).then_inc(S("aff_bounded"), 1)
                step(nc.vector.tensor_tensor(hot[:], aff[:], per_row(top[:], E), ALU.is_equal))
                v.wait_ge(S("route_in"), 16)
                step(nc.vector.tensor_tensor(pos[:], hot[:], rank.unsqueeze(1).to_broadcast([P, NT, E]), ALU.mult))
                step(nc.vector.tensor_reduce(first[:], pos[:], X, ALU.max))
                nc.vector.tensor_tensor(hot[:], pos[:], per_row(first[:], E), ALU.is_equal).then_inc(S("one_hot"), 1)
                p.sum_runs(v, "one_hot", hot_runs)
                nc.vector.tensor_reduce(share[:], hot[:].rearrange("p c e -> p e c"), X, ALU.add).then_inc(S("shared"), 1)
                v.wait_ge(S("gate_exp"), 1)
                step(nc.vector.tensor_scalar(gate[:], gate[:], 1.0, None, ALU.add))
                step(nc.vector.reciprocal(gate[:], gate[:]))
                v.wait_ge(S("counted"), 1)
                step(nc.vector.tensor_scalar(ends[:, 0, :], pc[:, 0:E], 1.0 / P, 0.5 - 0.5 / P, ALU.mult, ALU.add))
                step(nc.vector.tensor_scalar(ends[:, 0, :], ends[:, 0, :], ROUND, None, ALU.add))
                step(nc.vector.tensor_scalar(ends[:, 0, :], ends[:, 0, :], ROUND, None, ALU.subtract))
                for j in range(3):
                    d = 1 << j
                    nc.vector.tensor_copy(ends[:, j + 1, 0:d], ends[:, j, 0:d])
                    step(nc.vector.tensor_tensor(ends[:, j + 1, d:], ends[:, j, d:], ends[:, j, 0:E - d], ALU.add))
                step(nc.vector.tensor_tensor(ends[:, 4, :], ends[:, 3, :], ends[:, 0, :], ALU.subtract))
                step(nc.vector.tensor_scalar(ends[:, 5, :], ends[:, 4, :], float(P), -1.0, ALU.mult, ALU.add))
                v.wait_ge(S("positions_summed"), 1)
                step(nc.vector.tensor_tensor(pos[:], pp[:, 0:NT * E].rearrange("p (c e) -> p c e", e=E),
                                             ends[:, 5:6, :].to_broadcast([P, NT, E]), ALU.add))
                step(nc.vector.tensor_tensor(pos[:], pos[:], hot[:], ALU.mult))
                step(nc.vector.tensor_reduce(slot_f[:], pos[:], X, ALU.add))
                nc.vector.tensor_copy(slot[:], slot_f[:]).then_inc(S("slots_ready"), 1)
                step(nc.vector.tensor_tensor(before[:], ends[0:1, 3:4, :].to_broadcast([1, SL, E]),
                                             per_row(tiles[0:1, :], E), ALU.is_le))
                step(nc.vector.tensor_reduce(owner_f[:], before[:], X, ALU.add))
                step(nc.vector.tensor_scalar(owner_f[:], owner_f[:], float(E - 1), None, ALU.min))
                step(nc.vector.tensor_copy(owner[:], owner_f[:]))

            @block.gpsimd
            def _(g):
                p.layer_added(g, 5)
                g.wait_ge(S("xhat_scale"), 1)
                p.after(g, "f_kept", NT - 1)
                g.wait_ge(S("route_in"), 16)
                p.link(g, nc.gpsimd.tensor_tensor(pay[:, :, 0:D], x4[:], per_row(ratio[:], D), ALU.mult), "pool_step")
                p.link(g, nc.gpsimd.tensor_copy(pay[:, :, D], numbers), "pool_step")
                g.wait_ge(S("slots_ready"), 1)
                g.wait_ge(S("slots_cleared"), 16)
                for c in range(NT):
                    g.indirect_dma_start(p.slots, bass.IndirectOffsetOnAxis(ap=slot[:, c:c + 1], axis=0),
                                         pay[:, c, :], None).then_inc(S("scattered"), 16)
                g.wait_ge(S("scattered"), 16 * NT)

        with ExitStack() as b:
            xs = p.sb(b, "slot_rows", [P, 4, D + 1])
            xst = p.sb(b, "slot_turned", [P, 2, P])
            weights = p.sb(b, "slot_weights", [P, 4, 2, F])
            own = p.sb(b, "slot_vecs", [P, 4, D + 2 + FB])
            hid = p.sb(b, "expert_hidden", [P, 2, F])
            ys = p.sb(b, "slot_out", [P, 2, D])
            tok = [b.enter_context(nc.sbuf_tensor(f"slot_token{k}", [P, 1], U32)) for k in range(2)]
            pt = p.ps(b, "slot_psum", [P, 2, 512])
            ph = p.ps(b, "slot_up_psum", [P, 2, F])
            pd = p.ps(b, "slot_down_psum", [P, 2, 512])
            block = b.enter_context(nc.Block())


            def tile_quads(eng, body, ahead=0):
                for n in range(4):
                    body(n, n)
                with eng.Fori(1, SL // 4 - 1) as j:
                    for q in range(4):
                        body(4 * j + q, q)
                for q in range(4 - ahead):
                    body(SL - 4 + q, q)

            @block.sync
            def _(sp):
                def body(n, q):
                    if not (isinstance(n, int) and n < 4):
                        for name in ("s_turned", "s_tokens"):
                            p.after(sp, name, n - 4)
                    sp.dma_start(xs[:, q, :], p.slots.rearrange("(n p) d -> n p d", p=P)[bass.ds(n, 1), :, :].rearrange("n p d -> p (n d)")).then_inc(S(f"slot_in{q}"), 16)

                tile_quads(sp, body)
                for k in range(2):
                    sp.wait_ge(S(f"returned{k}"), 8 * SL)
                for n in range(4):
                    rows = slice(n * T // 4, (n + 1) * T // 4)
                    p.load(sp, f"routed_in{n}", p.ao[:, 4 * n:4 * n + 4, :], p.routed[rows, :].rearrange("(c p) d -> p c d", p=P))
                for n in range(2):
                    sp.wait_ge(S(f"out_added{n}"), NT // 2)
                    p.load(sp, "out_written", out[:, n * T // 2:(n + 1) * T // 2, :].rearrange("a (c p) d -> p (a c) d", p=P), p.x[:, p.half(n), :])
                sp.wait_ge(S("out_written"), 32)

            @block.tensor
            def _(t):
                p.lead(t, "s_turned", "s_up", "s_down")

                def turn(n, q):
                    t.wait_ge(S(f"slot_in{q}"), 4 * n + 16 - 4 * q)
                    p.after(t, "s_xst", n - 2)
                    nc.tensor.transpose(pt[:, q % 2, 0:P], xs[:, q, 0:D], p.ident).then_inc(S("s_turned"), 1)

                def up(n, q):
                    k = q % 2
                    p.after(t, "s_xst", n)
                    p.after(t, "s_relu", n - 2)
                    for m in range(FB):
                        ins = nc.tensor.matmul(ph[:, k, m * P:(m + 1) * P], weights[:, q % 4, 0, m * P:(m + 1) * P],
                                               xst[:, k, :], start=True, stop=True)
                    ins.then_inc(S("s_up"), 1)

                def down(n, q):
                    k = q % 2
                    p.after(t, "s_relu", n)
                    p.after(t, "s_out", n - 2)
                    for m in range(FB):
                        ins = nc.tensor.matmul(pd[:, k, 0:D], hid[:, k, m * P:(m + 1) * P],
                                               weights[:, q, 1, m * D:(m + 1) * D],
                                               start=(m == 0), stop=(m == FB - 1))
                    ins.then_inc(S("s_down"), 1)

                turn(0, 0)
                turn(1, 1)
                up(0, 0)

                def body(n, q):
                    if not last(n, SL):
                        up(n + 1, q + 1)
                    if not (isinstance(n, int) and n >= SL - 2):
                        turn(n + 2, (q + 2) % 4)
                    down(n, q)

                tile_quads(t, body)

            @block.scalar
            def _(a):
                p.lead(a, "s_relu")

                def body(n, q):
                    k = q % 2
                    p.after(a, "s_up", n)
                    p.after(a, "s_down", n - 2)
                    for m in range(FB):
                        ins = nc.scalar.activation(hid[:, k, m * P:(m + 1) * P], ph[:, k, m * P:(m + 1) * P], ACT.Relu,
                                                   bias=own[:, q, D + 2 + m:D + 3 + m])
                    ins.then_inc(S("s_relu"), 1)

                straight(lambda n, _: body(n, n % 4), SL)
                for n in range(2):
                    p.layer_root(a, 6 + n, None)
                    p.layer_scaled(a, 6 + n, slice(0, NT // 2 - n * len(OUT_BY_DVE)))

            @block.vector
            def _(v):
                step = lambda ins: p.link(v, ins, "dve_step")
                p.lead(v, "s_xst", "s_own", "s_out", "s_tokens")

                def scaled(n, q):
                    k = q % 2
                    p.after(v, "s_turned", n)
                    p.after(v, "s_own", n)
                    p.after(v, "s_up", n - 2)
                    nc.vector.tensor_scalar(xst[:, k, :], pt[:, k, 0:P], own[:, q, D:D + 1], own[:, q, D + 1:D + 2],
                                            ALU.mult, ALU.add).then_inc(S("s_xst"), 1)

                def fetched(n, q):
                    e = v.value_load(owner[0:1, bass.ds(n, 1)], min_val=0, max_val=E - 1)
                    if not (isinstance(n, int) and n < 4):
                        p.after(v, "s_down", n - 4)
                    nc.vector.tensor_copy(weights[:, q, 0, :], w1[:, bass.ds(e, 1), :].rearrange("p a f -> p (a f)"))
                    nc.vector.tensor_copy(weights[:, q, 1, :], w2[:, bass.ds(FB * e, FB), :].rearrange("p m d -> p (m d)"))
                    nc.vector.tensor_copy(own[:, q, :], vecs[:, bass.ds(e, 1), :].rearrange("p a v -> p (a v)")).then_inc(S("s_own"), 1)

                def returned(n, q):
                    k = q % 2
                    if not (isinstance(n, int) and n < 2):
                        v.wait_ge(S(f"returned{k}"), 8 * n - 8 * k)
                    v.wait_ge(S(f"slot_in{q}"), 4 * n + 16 - 4 * q)
                    nc.vector.tensor_copy(tok[k][:], xs[:, q, D:D + 1]).then_inc(S("s_tokens"), 1)
                    p.after(v, "s_down", n)
                    nc.vector.tensor_tensor(ys[:, k, :], pd[:, k, 0:D], own[:, q, 0:D], ALU.add).then_inc(S("s_out"), 1)

                v.wait_ge(S("experts_in"), 32)
                v.wait_ge(S("expert_vecs_in"), 32)
                for n in range(2):
                    fetched(n, n)
                    scaled(n, n)

                def body(n, q):
                    if not (isinstance(n, int) and n >= SL - 2):
                        fetched(n + 2, (q + 2) % 4)
                        scaled(n + 2, (q + 2) % 4)
                    returned(n, q)

                tile_quads(v, body, ahead=1)
                returned(SL - 1, 3)
                for n in range(2):
                    for c in p.tiles(n):
                        v.wait_ge(S(f"routed_in{c // 4}"), 16)
                        nc.vector.scalar_tensor_tensor(p.ao[:, c, :], p.ao[:, c, :], gate[:, c:c + 1], x4[:, c, :],
                                                       ALU.mult, ALU.add).then_inc(S("experts_added"), 1)
                        if c > p.tiles(n)[0]:
                            v.wait_ge(S("experts_added"), c)
                            nc.vector.bn_stats(p.st[:, c - 1, :], p.ao[:, c - 1, :])
                    v.wait_ge(S("experts_added"), c + 1)
                    step(nc.vector.bn_stats(p.st[:, c, :], p.ao[:, c, :]))
                    p.layer_stats(v, 6 + n, None)
                v.wait_ge(S("layer_stats"), 8)
                for c in OUT_BY_DVE:
                    step(nc.vector.tensor_scalar(p.ao[:, c, :], p.ao[:, c, :], p.mom[:, c, 0:1], p.rstd_o[:, c:c + 1],
                                                 ALU.subtract, ALU.mult))
                    nc.vector.tensor_tensor(p.x[:, c, :], p.x[:, c, :], p.ao[:, c, :], ALU.add).then_inc(S("out_added1"), 1)

            @block.gpsimd
            def _(g):
                for n in range(SL):
                    p.after(g, "s_out", n)
                    g.indirect_dma_start(p.routed, bass.IndirectOffsetOnAxis(ap=tok[n % 2][:], axis=0),
                                         ys[:, n % 2, :], None).then_inc(S(f"returned{n % 2}"), 16)
                for c in range(NT - len(OUT_BY_DVE)):
                    g.wait_ge(S("layer_scaled"), 3 * NT + c + 1)
                    nc.gpsimd.tensor_tensor(p.x[:, c, :], p.x[:, c, :], p.ao[:, c, :], ALU.add).then_inc(S(f"out_added{2 * c // NT}"), 1)



_DIRECT = ["L0_attn_x", "L0_attn_W_in", "L0_attn_A_log", "L0_attn_dt_bias", "L0_attn_B_norm_bias",
           "L0_attn_C_norm_bias", "L0_attn_W_out", "L0_ffn_w3_s", "L1_attn_Wq", "L1_attn_Wk", "L1_attn_Wv", "L1_ffn_b2"]


def constants():
    import numpy as np

    j, m = np.arange(P)[:, None], np.arange(P)[None, :]
    consts = [j == m, j >= 0 * m, j == m + 1, (j == 0) & (m == P - 1)]
    consts = [np.broadcast_to(a, (P, P)).astype(np.float32) for a in consts]
    consts += [np.where(m > j, -1e30, 0.0).astype(np.float32), np.where(j > m, -1e30, 0.0).astype(np.float32)]
    blocks = range(1, LEV + 1)
    triangles = [((j >> k) == (m >> k)) & (j <= m) for k in blocks] + [((j >> k) == (m >> k)) & (j > m) for k in blocks]
    levels = [j == m] + [((j >> (k + 1)) == (m >> (k + 1))) & ((j >> k) % 2 == 0) & ((m >> k) % 2 == 1) for k in range(LEV)]
    stack = lambda masks: np.ascontiguousarray(np.stack(masks, axis=1).astype(np.float32))
    return {
        "consts": stack(consts),
        "triangles": stack(triangles),
        "level_masks": np.ascontiguousarray(np.repeat(stack(levels)[:, :, None, :], R, axis=2)),
        "route": np.concatenate([j <= m] + [np.broadcast_to(np.array(row), (P, len(row))) for row in (range(E, 0, -1), range(SL))]
                                + [np.arange(T).reshape(NT, P).T, T + np.arange(SL * P).reshape(SL, P).T], axis=1).astype(np.float32),
    }


def kernel(**inputs):
    import numpy as np
    import concourse.bacc as _bacc
    from concourse import mybir as _mybir
    from concourse.bass_utils import run_bass_kernel_spmd as _run

    a = {n: np.asarray(v) for n, v in inputs.items()}
    arrays = {n: a[n] for n in _DIRECT}
    arrays["w1T"], arrays["w2T"] = a["L0_ffn_w1_w"].T, a["L0_ffn_w2_w"].T
    arrays["h1T"], arrays["h2T"], arrays["w3T"] = a["L0_ffn_h1_w"].T, a["L0_ffn_h2_w"].T, a["L0_ffn_w3_w"].T
    for n in ("w1_s", "w2_s", "h1_s", "h2_s"):
        arrays[n] = a["L0_ffn_" + n].reshape(FB, P).T
    arrays["centT"] = a["L1_ffn_centroids"].T
    arrays["expert_vecs"] = np.concatenate([a["L1_ffn_ln_g"].T[:, :, None], a["L1_ffn_ln_b"].T[:, :, None],
                                            a["L1_ffn_b1"].reshape(E, FB, P).transpose(2, 0, 1)], axis=2)
    arrays["ew1T"] = a["L1_ffn_w1"].transpose(2, 0, 1)
    arrays["ew2T"] = a["L1_ffn_w2"].reshape(E, D, FB, P).transpose(3, 0, 2, 1).reshape(P, E * FB, D)
    arrays.update(constants())
    arrays = {n: np.ascontiguousarray(v) for n, v in arrays.items()}

    nc = _bacc.Bacc("TRN2", target_bir_lowering=False, num_devices=1)
    drams = {n: nc.dram_tensor("in_" + n, v.shape, _mybir.dt.from_np(v.dtype), kind="ExternalInput").ap() for n, v in arrays.items()}
    out = nc.dram_tensor("out", a["L0_attn_x"].shape, _mybir.dt.float32, kind="ExternalOutput").ap()
    program(nc, drams, out)
    r = _run(nc, [{"in_" + n: v for n, v in arrays.items()}], core_ids=[0])
    return r.results[0]["out"]
```
